# Optimizing a Trainium2 kernel written in Bass

```python
import numpy as np
import jax
import jax.numpy as jnp

def _softmax(x, axis=-1):
    return jax.nn.softmax(x, axis=axis)

def _gelu(x):
    return jax.nn.gelu(x, approximate=True)

def _silu(x):
    return jax.nn.silu(x)

def _sigmoid(x):
    return jax.nn.sigmoid(x)

def _layernorm(x, axis=-1, eps=1e-05):
    m = jnp.mean(x, axis=axis, keepdims=True)
    v = jnp.var(x, axis=axis, keepdims=True)
    return (x - m) / jnp.sqrt(v + eps)

def _scatter_add(tgt, idx, src, axis=0):
    return tgt.at[idx].add(src)

def _segment_sum(src, seg, n):
    return jax.ops.segment_sum(src, seg, n)
kernel_name = 'mk_conv_attn_hybrid_d4_conv_nhwc128_r4_9013a0'

def setup_inputs(seed: int=0):
    np.random.seed(seed)
    _w = jnp.asarray

    def _rec_inputs():
        import jax
        import jax.numpy as jnp
        _gk = jax.random.key(seed)
        x = -7.109e-05 + 0.9999 * jax.random.normal(jax.random.fold_in(_gk, 1), (64, 32, 32, 32), jnp.float32)
        return x
    x = _rec_inputs()

    def _L0_conv_setup():
        import jax, jax.numpy as jnp
        import numpy as np
        L, H, D, DL, B = (32, 32, 32, 32, 128)
        key = jax.random.key(seed)
        k1, k2, k3 = jax.random.split(key, 3)
        gain = np.sqrt(2.0 / (1.0 + 0.01 ** 2))
        std1 = np.float32(gain / np.sqrt(DL))
        std2 = np.float32(gain / np.sqrt(D))
        x = jax.random.normal(k1, (B, L, H, D), dtype=jnp.float32)
        W1 = jax.random.normal(k2, (L, H, D, DL), dtype=jnp.float32) * std1
        b1 = jnp.zeros((L, H, DL), dtype=jnp.float32)
        W2 = jax.random.normal(k3, (L, H, DL, D), dtype=jnp.float32) * std2
        b2 = jnp.zeros((L, H, D), dtype=jnp.float32)
        return {'x': x, 'W1': W1, 'b1': b1, 'W2': W2, 'b2': b2}
    _L0_conv_all = _L0_conv_setup()
    _L0_conv_in = {k: v for k, v in _L0_conv_all.items() if k in ('W1', 'b1', 'W2', 'b2')}
    del _L0_conv_all

    def _L1_conv_setup():
        import jax, jax.numpy as jnp
        import numpy as np
        from jax import lax
        H = 32

        def _ema_scan(x):
            xt = jnp.moveaxis(x, 1, 0)

            def step(s, xi):
                s = s * 0.9 + xi * 0.1
                return (s, s)
            _, ys = lax.scan(step, jnp.zeros_like(xt[0]), xt)
            return jnp.moveaxis(ys, 0, 1)
        key = jax.random.key(seed)
        k1, k2, k3, k4, k5 = jax.random.split(key, 5)
        B, T, N = (4, 24, 128)
        x = jax.random.normal(k1, (B, T, N, H), dtype=jnp.float32)
        s = 1.0 / np.sqrt(H)
        W_exp = jax.random.uniform(k2, (2 * H, H), jnp.float32, -s, s)
        b_exp = jax.random.uniform(k3, (2 * H,), jnp.float32, -s, s)
        W_con = jax.random.uniform(k4, (H, H), jnp.float32, -s, s)
        b_con = jax.random.uniform(k5, (H,), jnp.float32, -s, s)
        return {'spatial_temporal_representation': x, 'W_exp': W_exp, 'b_exp': b_exp, 'W_con': W_con, 'b_con': b_con}
    _L1_conv_all = _L1_conv_setup()
    _L1_conv_in = {k: v for k, v in _L1_conv_all.items() if k in ('W_exp', 'b_exp', 'W_con', 'b_con')}
    del _L1_conv_all

    def _L2_attn_setup():
        import jax, jax.numpy as jnp
        import numpy as np
        N_HEADS = 4
        LN_EPS = 0.001
        key = jax.random.key(seed)
        ks = jax.random.split(key, 9)
        B, S, D = (4, 512, 32)
        w = 0.08
        return {'x': jax.random.normal(ks[0], (B, S, D), jnp.float32), 'Wq': jax.random.normal(ks[1], (D, D), jnp.float32) * w, 'bq': jnp.zeros((D,), jnp.float32), 'Wk': jax.random.normal(ks[2], (D, D), jnp.float32) * w, 'bk': jnp.zeros((D,), jnp.float32), 'Wv': jax.random.normal(ks[3], (D, D), jnp.float32) * w, 'bv': jnp.zeros((D,), jnp.float32), 'Wu': jax.random.normal(ks[4], (D, 2 * D), jnp.float32) * w, 'bu': jnp.zeros((2 * D,), jnp.float32), 'pos_w': jax.random.normal(ks[5], (2 * S - 1,), jnp.float32) * 0.02, 'ln_gamma': 1.0 + jax.random.normal(ks[6], (2 * D,), jnp.float32) * 0.3, 'ln_beta': jax.random.normal(ks[7], (2 * D,), jnp.float32) * 0.0001, 'Wf': jax.random.normal(ks[8], (2 * D, D), jnp.float32) * w, 'bf': jnp.zeros((D,), jnp.float32)}
    _L2_attn_all = _L2_attn_setup()
    _L2_attn_in = {k: v for k, v in _L2_attn_all.items() if k in ('Wq', 'bq', 'Wk', 'bk', 'Wv', 'bv', 'Wu', 'bu', 'pos_w', 'ln_gamma', 'ln_beta', 'Wf', 'bf')}
    del _L2_attn_all

    def _L2_ffn_setup():
        import jax, jax.numpy as jnp
        import numpy as np
        B, S, D, E, H, O, K = (128, 512, 32, 16, 128, 32, 8)
        key = jax.random.key(seed)
        k0, k1, k2, k3 = jax.random.split(key, 4)
        x = jax.random.normal(k0, (B, S, D), dtype=jnp.float32)
        gate_w = jax.random.normal(k1, (E, D), dtype=jnp.float32) * (1.0 / np.sqrt(D))
        gate_b = jnp.zeros((E,), dtype=jnp.float32)
        weight1 = jax.random.uniform(k2, (E, D + 1, H), dtype=jnp.float32, minval=-1.0, maxval=1.0) * (1.0 / np.sqrt(D + 1))
        weight2 = jax.random.uniform(k3, (E, H + 1, O), dtype=jnp.float32, minval=-1.0, maxval=1.0) * (1.0 / np.sqrt(H + 1))
        return {'x': x, 'gate_w': gate_w, 'gate_b': gate_b, 'weight1': weight1, 'weight2': weight2}
    _L2_ffn_all = _L2_ffn_setup()
    _L2_ffn_in = {k: v for k, v in _L2_ffn_all.items() if k in ('gate_w', 'gate_b', 'weight1', 'weight2')}
    del _L2_ffn_all

    def _L3_attn_setup():
        import jax, jax.numpy as jnp
        import numpy as np
        E = 32
        H = 4
        D = E // H
        key = jax.random.key(seed)
        ks = jax.random.split(key, 5)
        b, n = (4, 1024)
        x = jax.random.normal(ks[0], (b, n, E), dtype=jnp.float32)
        W_qkv = jax.random.normal(ks[1], (E, 3 * E), dtype=jnp.float32) * (1.0 / np.sqrt(E))
        b_qkv = jax.random.normal(ks[2], (3 * E,), dtype=jnp.float32) * 0.01
        W_proj = jax.random.normal(ks[3], (E, E), dtype=jnp.float32) * (1.0 / np.sqrt(E))
        b_proj = jax.random.normal(ks[4], (E,), dtype=jnp.float32) * 0.01
        return {'x': x, 'W_qkv': W_qkv, 'b_qkv': b_qkv, 'W_proj': W_proj, 'b_proj': b_proj}
    _L3_attn_all = _L3_attn_setup()
    _L3_attn_in = {k: v for k, v in _L3_attn_all.items() if k in ('W_qkv', 'b_qkv', 'W_proj', 'b_proj')}
    del _L3_attn_all

    def _L3_ffn_setup():
        import jax, jax.numpy as jnp
        import numpy as np
        B, N, D, C, E, K = (8, 2048, 32, 32, 8, 2)
        key = jax.random.key(seed)
        k0, k1, k2 = jax.random.split(key, 3)
        x = jax.random.normal(k0, (B, N, D), dtype=jnp.float32)
        router_w = jax.random.normal(k1, (D, E), dtype=jnp.float32) * 0.05
        router_b = jnp.zeros((E,), dtype=jnp.float32)
        expert_w = jax.random.normal(k2, (E, D, C), dtype=jnp.float32) * (1.0 / np.sqrt(D))
        expert_b = jnp.zeros((E, C), dtype=jnp.float32)
        return {'x': x, 'router_w': router_w, 'router_b': router_b, 'expert_w': expert_w, 'expert_b': expert_b}
    _L3_ffn_all = _L3_ffn_setup()
    _L3_ffn_in = {k: v for k, v in _L3_ffn_all.items() if k in ('router_w', 'router_b', 'expert_w', 'expert_b')}
    del _L3_ffn_all
    return {'x': x, 'L0_conv_W1': _L0_conv_in['W1'], 'L0_conv_b1': _L0_conv_in['b1'], 'L0_conv_W2': _L0_conv_in['W2'], 'L0_conv_b2': _L0_conv_in['b2'], 'L1_conv_W_exp': _L1_conv_in['W_exp'], 'L1_conv_b_exp': _L1_conv_in['b_exp'], 'L1_conv_W_con': _L1_conv_in['W_con'], 'L1_conv_b_con': _L1_conv_in['b_con'], 'L2_attn_Wq': _L2_attn_in['Wq'], 'L2_attn_bq': _L2_attn_in['bq'], 'L2_attn_Wk': _L2_attn_in['Wk'], 'L2_attn_bk': _L2_attn_in['bk'], 'L2_attn_Wv': _L2_attn_in['Wv'], 'L2_attn_bv': _L2_attn_in['bv'], 'L2_attn_Wu': _L2_attn_in['Wu'], 'L2_attn_bu': _L2_attn_in['bu'], 'L2_attn_pos_w': _L2_attn_in['pos_w'], 'L2_attn_ln_gamma': _L2_attn_in['ln_gamma'], 'L2_attn_ln_beta': _L2_attn_in['ln_beta'], 'L2_attn_Wf': _L2_attn_in['Wf'], 'L2_attn_bf': _L2_attn_in['bf'], 'L2_ffn_gate_w': _L2_ffn_in['gate_w'], 'L2_ffn_gate_b': _L2_ffn_in['gate_b'], 'L2_ffn_weight1': _L2_ffn_in['weight1'], 'L2_ffn_weight2': _L2_ffn_in['weight2'], 'L3_attn_W_qkv': _L3_attn_in['W_qkv'], 'L3_attn_b_qkv': _L3_attn_in['b_qkv'], 'L3_attn_W_proj': _L3_attn_in['W_proj'], 'L3_attn_b_proj': _L3_attn_in['b_proj'], 'L3_ffn_router_w': _L3_ffn_in['router_w'], 'L3_ffn_router_b': _L3_ffn_in['router_b'], 'L3_ffn_expert_w': _L3_ffn_in['expert_w'], 'L3_ffn_expert_b': _L3_ffn_in['expert_b']}

def reference(x, L0_conv_W1, L0_conv_b1, L0_conv_W2, L0_conv_b2, L1_conv_W_exp, L1_conv_b_exp, L1_conv_W_con, L1_conv_b_con, L2_attn_Wq, L2_attn_bq, L2_attn_Wk, L2_attn_bk, L2_attn_Wv, L2_attn_bv, L2_attn_Wu, L2_attn_bu, L2_attn_pos_w, L2_attn_ln_gamma, L2_attn_ln_beta, L2_attn_Wf, L2_attn_bf, L2_ffn_gate_w, L2_ffn_gate_b, L2_ffn_weight1, L2_ffn_weight2, L3_attn_W_qkv, L3_attn_b_qkv, L3_attn_W_proj, L3_attn_b_proj, L3_ffn_router_w, L3_ffn_router_b, L3_ffn_expert_w, L3_ffn_expert_b):
    import jax
    import jax.numpy as jnp

    def _L0_conv_ref(x, W1, b1, W2, b2):
        import jax, jax.numpy as jnp
        import numpy as np
        L, H, D, DL, B = (32, 32, 32, 32, 128)
        h = jnp.einsum('blhd,lhde->blhe', x, W1) + b1
        h = jax.nn.gelu(h, approximate=False)
        out = jnp.einsum('blhe,lhed->blhd', h, W2) + b2
        return out

    def _L1_conv_ref(spatial_temporal_representation, W_exp, b_exp, W_con, b_con):
        import jax, jax.numpy as jnp
        import numpy as np
        from jax import lax
        H = 32

        def _ema_scan(x):
            xt = jnp.moveaxis(x, 1, 0)

            def step(s, xi):
                s = s * 0.9 + xi * 0.1
                return (s, s)
            _, ys = lax.scan(step, jnp.zeros_like(xt[0]), xt)
            return jnp.moveaxis(ys, 0, 1)
        x = spatial_temporal_representation
        expanded = jnp.einsum('btnh,oh->btno', x, W_exp) + b_exp
        state_primary, state_gating = jnp.split(expanded, 2, axis=-1)
        gated_activation = jax.nn.sigmoid(_ema_scan(state_gating))
        out = jnp.einsum('btnh,oh->btno', state_primary * gated_activation, W_con) + b_con
        return out

    def _L2_attn_ref(x, Wq, bq, Wk, bk, Wv, bv, Wu, bu, pos_w, ln_gamma, ln_beta, Wf, bf):
        import jax, jax.numpy as jnp
        import numpy as np
        N_HEADS = 4
        LN_EPS = 0.001
        B, S, D = x.shape
        H = N_HEADS
        hd = D // H
        q = jax.nn.silu(x @ Wq + bq)
        k = jax.nn.silu(x @ Wk + bk)
        v = jax.nn.silu(x @ Wv + bv)
        u = x @ Wu + bu
        idx = S - 1 + jnp.arange(S)[None, :] - jnp.arange(S)[:, None]
        rel = pos_w[idx]
        pos_attn = jnp.einsum('nm,bmd->bnd', rel, v)
        qh = q.reshape(B, S, H, hd).transpose(0, 2, 1, 3)
        kh = k.reshape(B, S, H, hd).transpose(0, 2, 1, 3)
        vh = v.reshape(B, S, H, hd).transpose(0, 2, 1, 3)
        scores = jnp.einsum('bhnd,bhmd->bhnm', qh, kh) / jnp.sqrt(jnp.float32(hd))
        causal = jnp.tril(jnp.ones((S, S), dtype=bool))
        scores = jnp.where(causal[None, None], scores * scores, 0.0)
        self_attn = jnp.einsum('bhnm,bhmd->bhnd', jax.nn.silu(scores), vh)
        self_attn = self_attn.transpose(0, 2, 1, 3).reshape(B, S, D)
        a = jnp.concatenate([self_attn, pos_attn], axis=-1)
        mu = jnp.mean(a, axis=-1, keepdims=True)
        var = jnp.mean(jnp.square(a - mu), axis=-1, keepdims=True)
        a = (a - mu) * jax.lax.rsqrt(var + LN_EPS) * ln_gamma + ln_beta
        out = jax.nn.relu(u * a @ Wf + bf) + x
        return out

    def _L2_ffn_ref(x, gate_w, gate_b, weight1, weight2):
        import jax, jax.numpy as jnp
        import numpy as np
        B, S, D, E, H, O, K = (128, 512, 32, 16, 128, 32, 8)
        Bn, Sn, Dn = x.shape
        logits = jnp.einsum('bsd,ed->bse', x, gate_w) + gate_b
        probs = jax.nn.softmax(logits, axis=1)
        vals, idx = jax.lax.top_k(probs.transpose(0, 2, 1), K)
        topv = vals.transpose(0, 2, 1)
        topi = idx.transpose(0, 2, 1)
        flat_idx = topi.reshape(Bn, K * E)
        gathered = jnp.take_along_axis(x, flat_idx[:, :, None], axis=1)
        gathered = gathered.reshape(Bn, K, E, Dn)
        pooled = jnp.einsum('bked,bke->bed', gathered, topv)
        ones = jnp.ones((E, Bn, 1), dtype=x.dtype)
        h = jnp.concatenate([pooled.transpose(1, 0, 2), ones], axis=-1)
        h = jax.nn.gelu(jnp.einsum('ebd,edh->ebh', h, weight1), approximate=False)
        h = jnp.concatenate([h, ones], axis=-1)
        out = jnp.einsum('ebh,eho->ebo', h, weight2)
        out = out.transpose(1, 0, 2)
        weighted = jnp.einsum('beo,bke->bkeo', out, topv).reshape(Bn, K * E, O)
        outputs = jnp.zeros((Bn, Sn, O), dtype=x.dtype)
        outputs = outputs.at[jnp.arange(Bn)[:, None], flat_idx].add(weighted)
        return outputs

    def _L3_attn_ref(x, W_qkv, b_qkv, W_proj, b_proj):
        import jax, jax.numpy as jnp
        import numpy as np
        E = 32
        H = 4
        D = E // H
        b, n, e = x.shape
        qkv = (x @ W_qkv + b_qkv).reshape(b, n, H, D, 3)
        qkv = jnp.transpose(qkv, (4, 0, 2, 1, 3))
        q, k, v = (qkv[0], qkv[1], qkv[2])
        scale = 1.0 / np.float32(np.sqrt(e))
        scores = jnp.einsum('bhnd,bhmd->bhnm', q, k) * scale
        att = jax.nn.softmax(scores, axis=-1)
        out = jnp.einsum('bhnm,bhmd->bhnd', att, v)
        out = jnp.transpose(out, (0, 2, 1, 3)).reshape(b, n, e)
        return out @ W_proj + b_proj

    def _L3_ffn_ref(x, router_w, router_b, expert_w, expert_b):
        import jax, jax.numpy as jnp
        import numpy as np
        B, N, D, C, E, K = (8, 2048, 32, 32, 8, 2)
        router_probs = jax.nn.softmax(x @ router_w + router_b, axis=-1)
        top_p, top_i = jax.lax.top_k(router_probs, K)
        top_p = top_p / jnp.sum(top_p, axis=-1, keepdims=True)
        expert_out = jnp.einsum('bnd,edc->bnec', x, expert_w) + expert_b
        gathered = jnp.take_along_axis(expert_out, top_i[..., None], axis=2)
        return jnp.einsum('bnk,bnkc->bnc', top_p, gathered)

    def _gn(v, G=32, eps=1e-05):
        B_, H_, W_, C_ = v.shape
        g = v.reshape(B_, H_, W_, G, C_ // G)
        m = jnp.mean(g, axis=(1, 2, 4), keepdims=True)
        s = jnp.var(g, axis=(1, 2, 4), keepdims=True)
        return ((g - m) / jnp.sqrt(s + eps)).reshape(v.shape)

    def _ln_c(v, eps=1e-06):
        m = jnp.mean(v, axis=-1, keepdims=True)
        s = jnp.var(v, axis=-1, keepdims=True)
        return (v - m) / jnp.sqrt(s + eps)

    def _ln_t(v, eps=1e-05):
        m = jnp.mean(v, axis=-1, keepdims=True)
        s = jnp.var(v, axis=-1, keepdims=True)
        return (v - m) / jnp.sqrt(s + eps)

    def _to_tokens(v):
        B_, H_, W_, C_ = v.shape
        return v.reshape(B_, H_ * W_, C_)

    def _from_tokens(t, like):
        return t.reshape(like.shape)
    x = x + _L0_conv_ref(_gn(x), L0_conv_W1, L0_conv_b1, L0_conv_W2, L0_conv_b2)
    x = x + _L1_conv_ref(_gn(x), L1_conv_W_exp, L1_conv_b_exp, L1_conv_W_con, L1_conv_b_con)
    t = _to_tokens(x)
    t = t + _L2_attn_ref(_ln_t(t), L2_attn_Wq, L2_attn_bq, L2_attn_Wk, L2_attn_bk, L2_attn_Wv, L2_attn_bv, L2_attn_Wu, L2_attn_bu, L2_attn_pos_w, L2_attn_ln_gamma, L2_attn_ln_beta, L2_attn_Wf, L2_attn_bf)
    t = t + _L2_ffn_ref(_ln_t(t), L2_ffn_gate_w, L2_ffn_gate_b, L2_ffn_weight1, L2_ffn_weight2)
    t = t + _L3_attn_ref(_ln_t(t), L3_attn_W_qkv, L3_attn_b_qkv, L3_attn_W_proj, L3_attn_b_proj)
    t = t + _L3_ffn_ref(_ln_t(t), L3_ffn_router_w, L3_ffn_router_b, L3_ffn_expert_w, L3_ffn_expert_b)
    x = _from_tokens(t, x)
    return x

_drawn_inputs = setup_inputs


def setup_inputs(seed=0):
    import zlib

    import numpy as np

    out = dict(_drawn_inputs(seed))
    spreads = {'L0_conv_b1': (0.0, 0.1),
     'L0_conv_b2': (0.0, 0.1),
     'L2_attn_bq': (0.0, 0.677),
     'L2_attn_bk': (0.0, 0.549),
     'L2_attn_bv': (0.0, 0.1),
     'L2_attn_bu': (0.0, 0.277),
     'L2_attn_bf': (0.0, 0.1),
     'L2_ffn_gate_b': (0.0, 2.0),
     'L3_ffn_router_b': (0.0, 0.1),
     'L3_ffn_expert_b': (0.0, 0.332)}
    factors = {'L2_attn_Wk': 2.827,
     'L2_attn_ln_beta': 64.0,
     'L2_ffn_gate_w': 8.0,
     'L2_ffn_weight1': 8.0,
     'L2_ffn_weight2': 8.0,
     'L3_attn_b_qkv': 3.426,
     'L3_attn_b_proj': 3.815,
     'L2_attn_pos_w': 4.659}
    for name, (base, spread) in spreads.items():
        noise = np.random.default_rng([zlib.crc32(name.encode()), seed]).standard_normal(out[name].shape)
        drawn = base * np.exp(spread * noise) if base else spread * noise
        out[name] = jnp.asarray(drawn.astype(out[name].dtype))
    for name, factor in factors.items():
        out[name] = (out[name] * factor).astype(out[name].dtype)
    return out
```

```python
from contextlib import ExitStack

import concourse.bass as bass
from concourse import mybir
from concourse.alu_op_type import AluOpType as ALU

F32 = mybir.dt.float32
BF16 = mybir.dt.bfloat16
ACT = mybir.ActivationFunctionType
X = mybir.AxisListType.X

P = 128
B = 64
S = 1024
C = 32
R = P // C
NI = S // R
ROWS = 32
NC = NI // ROWS
CH = NC * B
J = S // P


def pairs(eng, lo, hi, body):
    turns = (hi - lo) // 2
    with eng.Fori(0, turns) as k:
        for u in range(2):
            body(2 * k + (lo + u), (lo + u) % 2)
    if (hi - lo) % 2:
        body(hi - 1, (hi - 1) % 2)


def positionwise_layers(nc, t):
    with ExitStack() as ctx:
        def sb(name, shape, dt=F32):
            return ctx.enter_context(nc.sbuf_tensor(name, shape, dt))

        def ps(name, shape, dt=F32):
            return ctx.enter_context(nc.psum_tensor(name, shape, dt))

        def sem(name):
            return ctx.enter_context(nc.semaphore(name))

        xt = sb("xt", [P, NI, B])
        b1 = sb("b1", [P, NI])
        b2 = sb("b2", [P, NI])
        stats = sb("stats", [P, B, 6])
        moment = sb("moment", [P, B])
        mean = sb("mean", [P, B])
        dev = sb("dev", [P, 2, B])
        var = sb("var", [P, B])
        rstd = sb("rstd", [P, B])
        minus_half = sb("minus_half", [P, B])
        ident = sb("ident", [P, P])
        share = sb("share", [P, P])
        w1 = sb("w1", [P, 2, NC, C])
        w2 = sb("w2", [P, 2, NC, C])
        xn = sb("xn", [P, 2, CH])
        xc = sb("xc", [P, 2, CH])
        pre = sb("pre", [P, 2, CH])
        hid = sb("hid", [P, 2, CH])
        res = sb("res", [P, 2, CH])
        w_main = sb("w_main", [P, P])
        w_gate = sb("w_gate", [P, P])
        w_con = sb("w_con", [P, P])
        b_main = sb("b_main", [P, 1])
        b_gate = sb("b_gate", [P, 1])
        b_gate10 = sb("b_gate10", [P, 1])
        b_con = sb("b_con", [P, 1])
        drive = sb("drive", [P, 2, CH])
        ema = sb("ema", [P, 2, CH])
        gate = sb("gate", [P, 2, CH])
        gated = sb("gated", [P, 2, CH])
        staged = sb("staged", [P, 2, P])
        rows = sb("rows", [P, 2, P])

        p_hid = [ps(f"p_hid{u}", [P, CH]) for u in range(2)]
        p_out = [ps(f"p_out{u}", [P, CH]) for u in range(2)]
        p_gate = [ps(f"p_gate{u}", [P, CH]) for u in range(2)]
        p_rows = [ps(f"p_rows{u}", [P, CH]) for u in range(2)]
        p_stat = p_gate[0]
        p_main, p_con = p_hid, p_out

        loaded = sem("loaded")
        small_loaded = sem("small_loaded")
        zeroed = sem("zeroed")
        consts = sem("consts")
        w_in = [sem(f"w_in{u}") for u in range(2)]
        chain = sem("chain")
        moment_ready = sem("moment_ready")
        group_made = sem("group_made")
        var_ready = sem("var_ready")
        rstd_ready = sem("rstd_ready")
        centred0 = sem("centred0")
        centred1 = sem("centred1")
        xn_ready = sem("xn_ready")
        hid_made = sem("hid_made")
        begun = sem("begun")
        pre_ready = sem("pre_ready")
        gelu_ready = sem("gelu_ready")
        out_made = sem("out_made")
        fin_done = sem("fin_done")
        yn_ready = sem("yn_ready")
        split_made = sem("split_made")
        b10_ready = sem("b10_ready")
        drive_ready = sem("drive_ready")
        ema_ready = sem("ema_ready")
        gate_ready = sem("gate_ready")
        gated_ready = sem("gated_ready")
        con_made = sem("con_made")
        t_ready = sem("t_ready")
        staged_ready = sem("staged_ready")
        turned = sem("turned")
        rows_ready = sem("rows_ready")
        stored = [sem(f"stored{u}") for u in range(2)]
        block = ctx.enter_context(nc.Block())


        @block.sync
        def _(sp):
            sp.dma_start(xt[:, :, :], t["x"]).then_inc(loaded, 16)
            sp.dma_start(b1[:, :], t["L0_conv_b1"]).then_inc(loaded, 16)
            sp.dma_start(b2[:, :], t["L0_conv_b2"]).then_inc(loaded, 16)
            for n in range(2):
                sp.dma_start(w1[:, n], t["L0_conv_W1"][:, n * NC:(n + 1) * NC, :]).then_inc(w_in[n], 16)
                sp.dma_start(w2[:, n], t["L0_conv_W2"][:, n * NC:(n + 1) * NC, :]).then_inc(w_in[n], 16)

            def weights(n, u):
                sp.wait_ge(out_made, n - 1)
                sp.dma_start(w1[:, u], t["L0_conv_W1"][:, bass.ds(n * NC, NC), :]).then_inc(w_in[u], 16)
                sp.dma_start(w2[:, u], t["L0_conv_W2"][:, bass.ds(n * NC, NC), :]).then_inc(w_in[u], 16)

            pairs(sp, 2, ROWS, weights)

            def store(n, u):
                sp.wait_ge(rows_ready, n + 1)
                sp.dma_start(t["rows1"][bass.ds(n * P, P), :], rows[:, u, :]).then_inc(stored[u], 16)

            pairs(sp, 0, 2 * B, store)
            sp.wait_ge(stored[0], 16 * B)
            sp.wait_ge(stored[1], 16 * B)

        @block.gpsimd
        def _(pool):
            pool.memset(ident[:, :], 0.0).then_inc(zeroed, 1)
            pool.memset(share[:, :], 0.0).then_inc(zeroed, 1)
            pool.memset(w_main[:, :], 0.0).then_inc(zeroed, 1)
            pool.memset(w_gate[:, :], 0.0).then_inc(zeroed, 1)
            pool.memset(w_con[:, :], 0.0).then_inc(zeroed, 1)
            pool.memset(minus_half[:, :], -0.5).then_inc(zeroed, 1)
            pool.wait_ge(zeroed, 6)
            pool.affine_select(out=ident[:, :], in_=ident[:, :], compare_op=ALU.not_equal, fill=1.0,
                               base=0, pattern=[[-1, P]], channel_multiplier=1).then_inc(consts, 1)
            for k in range(-(R - 1), R):
                pool.wait_ge(consts, k + R)
                pool.affine_select(out=share[:, :], in_=share[:, :], compare_op=ALU.not_equal,
                                   fill=0.5 / R, base=k * C, pattern=[[-1, P]],
                                   channel_multiplier=1).then_inc(consts, 1)
            for n in range(2):
                pool.wait_ge(var_ready, n + 1)
                pool.tensor_tensor(rstd[:, :], var[:, :], minus_half[:, :], ALU.pow).then_inc(rstd_ready, 1)
            pool.wait_ge(t_ready, ROWS)

            def stage(b, half):
                pool.tensor_copy(staged[:, half, :],
                                 xt[:, half * P:(half + 1) * P, bass.ds(b, 1)]).then_inc(staged_ready, 1)

            stage(0, 0)
            stage(0, 1)
            with pool.Fori(1, B) as b:
                for half in range(2):
                    pool.wait_ge(turned, 2 * b + half - 1)
                    stage(b, half)

        N_LOAD, N_SMALL = 16 * 3, 16 * 6 * R
        N_CONSTS = 2 * R

        @block.vector
        def _(dve):
            done = [0]

            def step(ins):
                done[0] += 1
                ins.then_inc(chain, 1)
                dve.wait_ge(chain, done[0])

            def statistics(n):
                with dve.Fori(0, B) as b:
                    dve.bn_stats(stats[:, bass.ds(b, 1), :],
                                 xt[:, :, bass.ds(b, 1)]).then_inc(chain, 1)
                done[0] += B
                dve.wait_ge(chain, done[0])
                even_mean, even_ss = stats[:, :, 1], stats[:, :, 2]
                odd_mean, odd_ss = stats[:, :, 4], stats[:, :, 5]
                dve.tensor_tensor(moment[:, :], even_mean, odd_mean, ALU.add).then_inc(moment_ready, 1)
                dve.wait_ge(group_made, 2 * n + 1)
                step(dve.tensor_copy(mean[:, :], p_stat[:, 0:B]))
                step(dve.tensor_tensor(dev[:, 0], even_mean, mean[:, :], ALU.subtract))
                step(dve.tensor_tensor(dev[:, 1], odd_mean, mean[:, :], ALU.subtract))
                step(dve.tensor_tensor(dev[:, :, :], dev[:, :, :], dev[:, :, :], ALU.mult))
                step(dve.tensor_tensor(dev[:, 0], dev[:, 0], dev[:, 1], ALU.add))
                step(dve.tensor_tensor(dev[:, 1], even_ss, odd_ss, ALU.add))
                dve.scalar_tensor_tensor(out=moment[:, :], in0=dev[:, 1], scalar=2.0 / NI, in1=dev[:, 0],
                                         op0=ALU.mult, op1=ALU.add).then_inc(moment_ready, 1)
                dve.wait_ge(group_made, 2 * n + 2)
                dve.tensor_scalar(var[:, :], p_stat[:, 0:B], 1e-5, None, ALU.add).then_inc(var_ready, 1)
                dve.wait_ge(rstd_ready, n + 1)

            mean_b = mean[:, :].rearrange("p (o b) -> p o b", o=1).broadcast_to([P, NC, B])
            rstd_b = rstd[:, :].rearrange("p (o b) -> p o b", o=1).broadcast_to([P, NC, B])

            def v3(ap):
                return ap.rearrange("p (i b) -> p i b", b=B)

            def row(k):
                return xt[:, bass.ds(k * NC, NC), :]

            def normalise(k, u, used, count, out_sem, before):
                if used is not None:
                    dve.wait_ge(used, count)
                dve.tensor_tensor(v3(xc[:, u, :]), row(k), mean_b, ALU.subtract).then_inc(before, 1)
                dve.wait_ge(before, k + 1)
                dve.tensor_tensor(v3(xn[:, u, :]), v3(xc[:, u, :]), rstd_b, ALU.mult).then_inc(out_sem, 1)

            dve.wait_ge(loaded, N_LOAD)
            dve.wait_ge(consts, N_CONSTS)
            statistics(0)

            def bias1(k, u):
                dve.wait_ge(hid_made, k + 1)
                dve.tensor_tensor(v3(pre[:, u, :]), v3(p_hid[u][:, :]),
                                  b1[:, bass.ds(k * NC, NC)].rearrange("p (i o) -> p i o", o=1)
                                  .broadcast_to([P, NC, B]), ALU.add).then_inc(pre_ready, 1)

            def finish(k, u):
                dve.wait_ge(out_made, k + 1)
                dve.tensor_tensor(v3(res[:, u, :]), v3(p_out[u][:, :]),
                                  b2[:, bass.ds(k * NC, NC)].rearrange("p (i o) -> p i o", o=1)
                                  .broadcast_to([P, NC, B]), ALU.add).then_inc(fin_done, 1)
                dve.wait_ge(fin_done, 2 * k + 1)
                dve.tensor_tensor(row(k), v3(res[:, u, :]), row(k), ALU.add).then_inc(fin_done, 1)

            normalise(0, 0, None, 0, xn_ready, centred0)
            normalise(1, 1, None, 0, xn_ready, centred0)
            bias1(0, 0)

            def body0(k, u):
                normalise(k, u, hid_made, k - 1, xn_ready, centred0)
                bias1(k - 1, 1 - u)
                finish(k - 2, u)

            pairs(dve, 2, ROWS, body0)
            bias1(ROWS - 1, 1)
            finish(ROWS - 2, 0)
            finish(ROWS - 1, 1)
            dve.wait_ge(fin_done, 2 * ROWS)

            dve.wait_ge(small_loaded, N_SMALL)
            statistics(1)
            dve.tensor_scalar(b_gate10[:, :], b_gate[:, :], 0.1, None, ALU.mult).then_inc(b10_ready, 1)
            step(dve.memset(ema[:, 1, :], 0.0))

            def average(k, u):
                dve.wait_ge(drive_ready, k + 1)
                dve.scalar_tensor_tensor(out=ema[:, u, :], in0=ema[:, 1 - u, :], scalar=0.9,
                                         in1=drive[:, u, :], op0=ALU.mult, op1=ALU.add).then_inc(ema_ready, 1)

            def gating(k, u):
                dve.wait_ge(gate_ready, k + 1)
                dve.wait_ge(split_made, k + 1)
                dve.scalar_tensor_tensor(out=gated[:, u, :], in0=p_main[u][:, :], scalar=b_main[:, 0:1],
                                         in1=gate[:, u, :], op0=ALU.add, op1=ALU.mult).then_inc(gated_ready, 1)

            def finish1(k, u):
                dve.wait_ge(con_made, k + 1)
                dve.scalar_tensor_tensor(out=row(k), in0=v3(p_con[u][:, :]), scalar=b_con[:, 0:1],
                                         in1=row(k), op0=ALU.add, op1=ALU.add).then_inc(t_ready, 1)

            normalise(0, 0, None, 0, yn_ready, centred1)
            normalise(1, 1, None, 0, yn_ready, centred1)
            average(0, 0)
            dve.wait_ge(ema_ready, 1)
            gating(0, 0)

            def body1(k, u):
                normalise(k, u, split_made, k - 1, yn_ready, centred1)
                dve.wait_ge(ema_ready, k - 1)
                average(k - 1, 1 - u)
                gating(k - 1, 1 - u)
                finish1(k - 2, u)

            pairs(dve, 2, ROWS, body1)
            dve.wait_ge(ema_ready, ROWS - 1)
            average(ROWS - 1, 1)
            gating(ROWS - 1, 1)
            finish1(ROWS - 2, 0)
            finish1(ROWS - 1, 1)

            def copy_rows(n, u):
                dve.wait_ge(turned, n + 1)
                dve.wait_ge(stored[u], 8 * (n - u))
                dve.tensor_copy(rows[:, u, :], p_rows[u][:, 0:P]).then_inc(rows_ready, 1)

            for n in range(2):
                dve.wait_ge(turned, n + 1)
                dve.tensor_copy(rows[:, n, :], p_rows[n][:, 0:P]).then_inc(rows_ready, 1)
            pairs(dve, 2, 2 * B, copy_rows)

        @block.scalar
        def _(act):
            act.wait_ge(zeroed, 6)
            for r in range(R):
                q = slice(r * C, (r + 1) * C)
                act.dma_start(w_main[q, q], t["L1_conv_W_exp"][:, 0:C]).then_inc(small_loaded, 16)
                act.dma_start(w_gate[q, q], t["L1_conv_W_exp"][:, C:2 * C]).then_inc(small_loaded, 16)
                act.dma_start(w_con[q, q], t["L1_conv_W_con"]).then_inc(small_loaded, 16)
                act.dma_start(b_main[q, :], t["L1_conv_b_exp"][0:C, :]).then_inc(small_loaded, 16)
                act.dma_start(b_gate[q, :], t["L1_conv_b_exp"][C:2 * C, :]).then_inc(small_loaded, 16)
                act.dma_start(b_con[q, :], t["L1_conv_b_con"]).then_inc(small_loaded, 16)

            def gelu(k, u):
                act.wait_ge(pre_ready, k + 1)
                act.activation(hid[:, u, :], pre[:, u, :], ACT.Gelu).then_inc(gelu_ready, 1)

            def body(k, u):
                act.wait_ge(out_made, k - 1)
                gelu(k, u)

            act.preload_act_table(ACT.Gelu)
            gelu(0, 0)
            gelu(1, 1)
            pairs(act, 2, ROWS, body)
            act.preload_act_table(ACT.Sigmoid)

            def drives(k, u):
                act.wait_ge(split_made, k + 1)
                act.activation(drive[:, u, :], p_gate[u][:, :], ACT.Identity, bias=b_gate10[:, 0:1],
                               scale=0.1).then_inc(drive_ready, 1)

            def sigmoid(k, u):
                act.wait_ge(ema_ready, k + 1)
                act.activation(gate[:, u, :], ema[:, u, :], ACT.Sigmoid).then_inc(gate_ready, 1)

            def body1(k, u):
                act.wait_ge(ema_ready, k - 1)
                drives(k, u)
                act.wait_ge(gated_ready, k - 2)
                sigmoid(k - 1, 1 - u)

            act.wait_ge(b10_ready, 1)
            drives(0, 0)
            drives(1, 1)
            sigmoid(0, 0)
            act.wait_ge(ema_ready, 1)
            drives(2, 0)
            sigmoid(1, 1)
            pairs(act, 3, ROWS, body1)
            act.wait_ge(gated_ready, ROWS - 2)
            sigmoid(ROWS - 1, 1)

        @block.tensor
        def _(pe):
            def averages(n):
                for k in range(2):
                    pe.wait_ge(moment_ready, 2 * n + k + 1)
                    pe.matmul(p_stat[:, 0:B], share[:, :], moment[:, :], start=True, stop=True).then_inc(group_made, 1)

            pe.wait_ge(consts, N_CONSTS)
            averages(0)

            def products(w, dst, src):
                for i in range(NC):
                    for r in range(R):
                        q = slice(r * C, (r + 1) * C)
                        last = pe.matmul(dst[q, i * B:(i + 1) * B], w[q, i, :], src[q, i * B:(i + 1) * B],
                                         start=True, stop=True, skip_group_check=True)
                return last

            def first(k, u, at):
                pe.wait_ge(w_in[u], at)
                pe.wait_ge(xn_ready, k + 1)
                pe.sem_inc(begun, 1)
                products(w1[:, u], p_hid[u], xn[:, u, :]).then_inc(hid_made, 1)

            def second(k, u):
                pe.wait_ge(gelu_ready, k + 1)
                pe.sem_inc(begun, 1)
                products(w2[:, u], p_out[u], hid[:, u, :]).then_inc(out_made, 1)

            def body(k, u):
                pe.wait_ge(pre_ready, k - 1)
                first(k, u, 16 * (k - u) + 32)
                pe.wait_ge(fin_done, 2 * k - 4)
                second(k - 1, 1 - u)

            first(0, 0, 32)
            first(1, 1, 32)
            second(0, 0)
            pe.wait_ge(pre_ready, 1)
            first(2, 0, 64)
            second(1, 1)
            pairs(pe, 3, ROWS, body)
            pe.wait_ge(fin_done, 2 * (ROWS - 2))
            second(ROWS - 1, 1)
            averages(1)

            def split(k, u):
                pe.wait_ge(yn_ready, k + 1)
                pe.matmul(p_main[u][:, :], w_main[:, :], xn[:, u, :], start=True, stop=True)
                pe.matmul(p_gate[u][:, :], w_gate[:, :], xn[:, u, :], start=True, stop=True).then_inc(split_made, 1)

            def con(k, u):
                pe.wait_ge(gated_ready, k + 1)
                pe.matmul(p_con[u][:, :], w_con[:, :], gated[:, u, :], start=True, stop=True).then_inc(con_made, 1)

            def body1(k, u):
                pe.wait_ge(gated_ready, k - 1)
                pe.wait_ge(drive_ready, k - 1)
                split(k, u)
                pe.wait_ge(t_ready, k - 2)
                con(k - 1, 1 - u)

            pe.wait_ge(var_ready, 2)
            split(0, 0)
            split(1, 1)
            con(0, 0)
            pe.wait_ge(gated_ready, 1)
            pe.wait_ge(drive_ready, 1)
            split(2, 0)
            con(1, 1)
            pairs(pe, 3, ROWS, body1)
            pe.wait_ge(t_ready, ROWS - 2)
            con(ROWS - 1, 1)
            def turn(n, u):
                pe.wait_ge(staged_ready, n + 1)
                pe.transpose(p_rows[u][:, 0:P], staged[:, u, :], ident[:, :]).then_inc(turned, 1)

            def turn_next(n, u):
                pe.wait_ge(rows_ready, n - 1)
                turn(n, u)

            turn(0, 0)
            turn(1, 1)
            pairs(pe, 2, 2 * B, turn_next)


H = 4
D = C // H
SLOTS = 8
HALF = S // 2
Q_PART = [0, 0, 1, 1, 0, 2]
K_PART = [0, 1, 0, 1, 2, 0]


def wait(eng, semaphore, value):
    if not isinstance(value, int) or value > 0:
        eng.wait_ge(semaphore, value)


def over_images(body, eng):
    body(0, 0, True, False)
    with eng.Fori(0, (B - 2) // 2) as k:
        for u in range(2):
            body(2 * k + 1 + u, (1 + u) % 2, False, False)
    body(B - 1, (B - 1) % 2, False, True)


def mid(ap, n):
    return ap.rearrange("p (j o) -> p j o", o=1).broadcast_to([ap.shape[0], ap.shape[1], n])


def normalise_tokens(dve, pool_pow, x, out, width, eps, s, chained, at):
    steps = [0]

    def step(ins):
        steps[0] += 1
        ins.then_inc(chained, 1)
        dve.wait_ge(chained, at + steps[0])

    step(dve.tensor_reduce(s["sum"][:, :], x, X, ALU.add))
    step(dve.tensor_scalar(s["sum"][:, :], s["sum"][:, :], 1.0 / width, None, ALU.mult))
    step(dve.tensor_tensor(s["centred"], x, mid(s["sum"][:, :], width), ALU.subtract))
    step(dve.tensor_tensor(s["square"], s["centred"], s["centred"], ALU.mult))
    step(dve.tensor_reduce(s["sum"][:, :], s["square"], X, ALU.add))
    pool_pow(dve.tensor_scalar(s["var"][:, :], s["sum"][:, :], 1.0 / width, eps, ALU.mult, ALU.add))
    step(dve.tensor_tensor(out, s["centred"], mid(s["rstd"][:, :], width), ALU.mult))
    return steps[0]


def silu_attention_layer(nc, t):
    with ExitStack() as ctx:
        def sb(name, shape, dt=F32):
            return ctx.enter_context(nc.sbuf_tensor("b_" + name, shape, dt))

        def ps(name, shape, dt=F32):
            return ctx.enter_context(nc.psum_tensor("b_" + name, shape, dt))

        def sem(name):
            return ctx.enter_context(nc.semaphore("b_" + name))

        QKV, U = 3 * C, 2 * C
        ident = sb("ident", [P, P])
        ident16 = sb("ident16", [P, P], BF16)
        w_in = sb("w_in", [C + 1, QKV + U])
        w_out = sb("w_out", [U + 1, C])
        gamma = sb("gamma", [P, U])
        beta = sb("beta", [P, U])
        hankel = sb("hankel", [P, S])
        rel = sb("rel", [P, S])
        last_col = sb("last_col", [P, 1])
        last_w = sb("last_w", [P, P])
        minus_half = sb("minus_half", [P, J])
        x_in = sb("x_in", [P, J, C])
        ln = {"sum": sb("ln_sum", [P, J]), "var": sb("ln_var", [P, J]), "rstd": sb("ln_rstd", [P, J]),
              "centred": sb("ln_centred", [P, J, C])[:, :, :], "square": sb("ln_square", [P, J, C])[:, :, :]}
        ln2 = {"sum": sb("ln2_sum", [P, J]), "var": sb("ln2_var", [P, J]), "rstd": sb("ln2_rstd", [P, J]),
               "centred": sb("ln2_centred", [P, J, U])[:, :, :], "square": sb("ln2_square", [P, J, U])[:, :, :]}
        xl = sb("xl", [P, J, C])
        base = sb("base", [P, 2, J, C])
        xlT = sb("xlT", [C + 1, S])
        qkv = sb("qkv", [P, J, QKV])
        rest = sb("rest", [P, J, 2 * C])
        parts = sb("parts", [P, J, 2, H, SLOTS, D], BF16)
        qT = sb("qT", [P, 2, 2, S], BF16)
        kT = sb("kT", [P, 2, 2, S], BF16)
        v = sb("v", [P, J, C])
        v_pad = sb("v_pad", [P, 2, J, H, 32])
        v_after = sb("v_after", [P, J, C])
        u_gate = sb("u_gate", [P, 2, J, U])
        pos = sb("pos", [P, 2, J, C])
        sq = sb("sq", [P, 3, 2, HALF])
        wt = sb("wt", [P, 3, 2, HALF])
        o_sb = sb("o_sb", [P, 2, HALF])
        cat = sb("cat", [P, J, U])
        ua = sb("ua", [P, J, U])
        uaT = sb("uaT", [U + 1, S])
        result = sb("result", [P, J, C])

        p_s = [ps(f"p_s{k}", [P, 2, HALF]) for k in range(2)]
        p_o = [ps(f"p_o{k}", [P, HALF]) for k in range(2)]
        p_m = ps("p_m", [P, 2, HALF])
        p_m16 = p_m[:, :, :].rearrange("p a b -> p (a b)").bitcast(BF16).rearrange("p (a b) -> p a b", a=2)

        UNITS = [(qc, kb, g) for qc in range(2) for kb in range(4 * (qc + 1)) for g in range(2)]
        N = len(UNITS)
        assert N % 6 == 0

        def span(n):
            qc, kb, _ = UNITS[n]
            q0 = max(qc * HALF, kb * P)
            return q0, (qc + 1) * HALF - q0

        MASKED = [n for n, (qc, kb, _) in enumerate(UNITS) if kb >= 4 * qc]

        const_in = sem("const_in")
        ext_in = sem("ext_in")
        last_in = sem("last_in")
        hankel_in = sem("hankel_in")
        cleared = sem("cleared")
        ident_made = sem("ident_made")
        rel_made = sem("rel_made")
        x_loaded = sem("x_loaded")
        chain1, chain2, chain3 = sem("chain1"), sem("chain2"), sem("chain3")
        var_made, rstd_made = sem("var_made"), sem("rstd_made")
        var2_made, rstd2_made = sem("var2_made"), sem("rstd2_made")
        xl_made = sem("xl_made")
        base_made = sem("base_made")
        xl_turned = sem("xl_turned")
        xlT_made = sem("xlT_made")
        qkv_projected = sem("qkv_projected")
        qkv_made = sem("qkv_made")
        parts_made = sem("parts_made")
        v_made = sem("v_made")
        v_pad_made = sem("v_pad_made")
        suffix = sem("suffix")
        qk_turned = sem("qk_turned")
        qk_copied = sem("qk_copied")
        upos_made = sem("upos_made")
        upos_copied = sem("upos_copied")
        scored = sem("scored")
        squared = sem("squared")
        masked = sem("masked")
        weighed = sem("weighed")
        summed = sem("summed")
        o_copied = sem("o_copied")
        o_turned = sem("o_turned")
        cat_made = sem("cat_made")
        ua_made = sem("ua_made")
        ua_turned = sem("ua_turned")
        uaT_made = sem("uaT_made")
        projected = sem("projected")
        result_made = sem("result_made")
        stored = sem("stored")
        pe_begun, pool_begun = sem("pe_begun"), sem("pool_begun")
        block = ctx.enter_context(nc.Block())

        src = t["t1"].rearrange("(b s) c -> b s c", b=B)
        dst = t["t2"].rearrange("(b s) c -> b s c", b=B)

        def image(ap, i):
            return ap[bass.ds(i, 1), :, :].rearrange("b (j p) c -> p (b j) c", p=P)

        N_CONST = 16 * 12
        K1 = 6 + 1

        @block.sync
        def _(sp):
            ext = t["pos_ext"]
            n_w = t["pos_w"].shape[1]
            sp.dma_start(ext[:, 0:n_w], t["pos_w"]).then_inc(ext_in, 16)
            sp.dma_start(last_col[:, :], t["pos_w"][:, n_w - 1:n_w].broadcast_to([P, 1])).then_inc(last_in, 16)
            for k, name in enumerate(("q", "k", "v")):
                sp.dma_start(w_in[0:C, k * C:(k + 1) * C], t["L2_attn_W" + name]).then_inc(const_in, 16)
                sp.dma_start(w_in[C:C + 1, k * C:(k + 1) * C], t["L2_attn_b" + name]).then_inc(const_in, 16)
            sp.dma_start(w_in[0:C, QKV:QKV + U], t["L2_attn_Wu"]).then_inc(const_in, 16)
            sp.dma_start(w_in[C:C + 1, QKV:QKV + U], t["L2_attn_bu"]).then_inc(const_in, 16)
            sp.dma_start(w_out[0:U, :], t["L2_attn_Wf"]).then_inc(const_in, 16)
            sp.dma_start(w_out[U:U + 1, :], t["L2_attn_bf"]).then_inc(const_in, 16)
            sp.dma_start(gamma[:, :], t["L2_attn_ln_gamma"].broadcast_to([P, U])).then_inc(const_in, 16)
            sp.dma_start(beta[:, :], t["L2_attn_ln_beta"].broadcast_to([P, U])).then_inc(const_in, 16)
            sp.wait_ge(rel_made, 1)
            sp.dma_start(ext[:, n_w:n_w + P], last_w[0:1, :]).then_inc(ext_in, 16)
            sp.wait_ge(ext_in, 32)
            sp.dma_start(hankel[:, :], bass.AP(tensor=ext.tensor, offset=ext.offset, ap=[[1, P], [1, S]])).then_inc(hankel_in, 16)

            def load(i):
                sp.dma_start(x_in[:, :, :], image(src, i)).then_inc(x_loaded, 16)

            def store(i):
                sp.wait_ge(result_made, i + 1)
                sp.dma_start(image(dst, i), result[:, :, :]).then_inc(stored, 16)

            load(0)

            def body(i, u, first, last):
                if not last:
                    sp.wait_ge(base_made, i + 1)
                    load(i + 1)
                if not first:
                    store(i - 1)

            over_images(body, sp)
            store(B - 1)
            sp.wait_ge(stored, 16 * B)

        @block.gpsimd
        def _(pool):
            pool.memset(ident[:, :], 0.0).then_inc(cleared, 1)
            pool.memset(ident16[:, :], 0.0).then_inc(cleared, 1)
            pool.memset(parts[:, :, :, :, :, :], 0.0).then_inc(cleared, 1)
            pool.memset(v_pad[:, :, :, :, :], 0.0).then_inc(cleared, 1)
            pool.memset(v_after[:, J - 1, :], 0.0).then_inc(cleared, 1)
            pool.memset(minus_half[:, :], -0.5).then_inc(cleared, 1)
            pool.wait_ge(cleared, 8)
            for m in (ident, ident16):
                pool.affine_select(out=m[:, :], in_=m[:, :], compare_op=ALU.not_equal, fill=1.0, base=0,
                                   pattern=[[-1, P]], channel_multiplier=1).then_inc(ident_made, 1)

            def mask(i, n):
                if n in MASKED:
                    pool.wait_ge(squared, N * i + n + 1)
                    pool.sem_inc(pool_begun, 1)
                    diag = sq[:, n % 3, :, 0:P]
                    pool.affine_select(out=diag, in_=diag, compare_op=ALU.is_ge, fill=0.0, base=0,
                                       pattern=[[0, 2], [1, P]], channel_multiplier=-1).then_inc(masked, 1)

            def power(i):
                pool.wait_ge(var_made, i + 1)
                pool.tensor_tensor(ln["rstd"][:, :], ln["var"][:, :], minus_half[:, :], ALU.pow).then_inc(rstd_made, 1)

            def power2(i):
                pool.wait_ge(var2_made, i + 1)
                pool.tensor_tensor(ln2["rstd"][:, :], ln2["var"][:, :], minus_half[:, :], ALU.pow).then_inc(rstd2_made, 1)

            def suffixes(i):
                pool.wait_ge(v_made, i + 1)
                wait(pool, upos_made, i)
                for j in range(J - 2, -1, -1):
                    if j < J - 2:
                        pool.wait_ge(suffix, (J - 1) * i + J - 2 - j)
                    pool.tensor_tensor(v_after[:, j, :], v_after[:, j + 1, :], v[:, j + 1, :], ALU.add).then_inc(suffix, 1)

            power(0)
            suffixes(0)

            def body(i, u, first, last):
                for n in range(N):
                    mask(i, n)
                    if n == 4 and not first:
                        power2(i - 1)
                    if n == 11 and not last:
                        power(i + 1)
                    if n == 15 and not last:
                        suffixes(i + 1)

            over_images(body, pool)
            power2(B - 1)

        @block.scalar
        def _(act):
            act.preload_act_table(ACT.Silu)

            def square(i, n):
                act.wait_ge(scored, N * i + n + 1)
                m = span(n)[1]
                act.activation(sq[:, n % 3, :, 0:m], p_s[n % 2][:, :, 0:m], ACT.Square).then_inc(squared, 1)

            def weigh(i, n):
                if n in MASKED:
                    act.wait_ge(masked, len(MASKED) * i + MASKED.index(n) + 1)
                else:
                    act.wait_ge(squared, N * i + n + 1)
                wait(act, summed, N * i + n - 2)
                m = span(n)[1]
                act.activation(wt[:, n % 3, :, 0:m], sq[:, n % 3, :, 0:m], ACT.Silu,
                               scale=1.0 / D).then_inc(weighed, 1)

            def silu_qkv(i):
                act.wait_ge(qkv_projected, i + 1)
                wait(act, parts_made, i)
                wait(act, v_made, i)
                act.activation(qkv[:, :, :].rearrange("p (a j) c -> p a (j c)", a=2),
                               p_m[:, :, 0:J // 2 * QKV], ACT.Silu).then_inc(qkv_made, 1)

            silu_qkv(0)
            square(0, 0)

            def body(i, u, first, last):
                for n in range(N):
                    if n + 1 < N:
                        square(i, n + 1)
                    elif not last:
                        square(i + 1, 0)
                    weigh(i, n)
                    if n == 14 and not last:
                        silu_qkv(i + 1)

            over_images(body, act)

        @block.tensor
        def _(pe):
            def turn_xl(i):
                pe.wait_ge(xl_made, i + 1)
                for j in range(J):
                    ins = pe.transpose(p_m[0:C, j // 4, (j % 4) * P:(j % 4 + 1) * P], xl[:, j, :], ident[:, :])
                ins.then_inc(xl_turned, 1)

            def project_qkv(i):
                pe.wait_ge(xlT_made, i + 1)
                for j in range(J):
                    o = (j % 4) * QKV
                    ins = pe.matmul(p_m[:, j // 4, o:o + QKV], xlT[:, j * P:(j + 1) * P], w_in[:, 0:QKV],
                                    start=True, stop=True, skip_group_check=True)
                ins.then_inc(qkv_projected, 1)

            def turn_qk(i, which):
                pe.wait_ge(parts_made, i + 1)
                if which:
                    pe.wait_ge(qk_copied, 2 * i + 1)
                for g in range(2):
                    for j in range(J):
                        ins = pe.transpose(p_m16[:, g, j * P:(j + 1) * P],
                                           parts[:, j, which, 2 * g:2 * g + 2, :, :].rearrange("p h s d -> p (h s d)"),
                                           ident16[:, :])
                ins.then_inc(qk_turned, 1)

            def project_u_and_positions(i):
                pe.wait_ge(qk_copied, 2 * i + 2)
                for j in range(J):
                    pe.matmul(p_m[:, 0, j * U:(j + 1) * U], xlT[:, j * P:(j + 1) * P], w_in[:, QKV:QKV + U],
                              start=True, stop=True, skip_group_check=True)
                pe.wait_ge(suffix, (J - 1) * (i + 1))
                for j in range(J):
                    for m in range(j + 1):
                        x0 = (j - m) * P
                        pe.matmul(p_m[:, 1, j * C:(j + 1) * C], rel[:, x0:x0 + P], v[:, m, :],
                                  start=(m == 0), stop=False, skip_group_check=True)
                    ins = pe.matmul(p_m[:, 1, j * C:(j + 1) * C], last_w[:, :], v_after[:, j, :],
                                    start=False, stop=True, skip_group_check=True)
                ins.then_inc(upos_made, 1)

            def score(i, u, n):
                qc, kb, g = UNITS[n]
                q0, m = span(n)
                if n == 0:
                    pe.wait_ge(qk_copied, 2 * i + 2)
                    pe.wait_ge(v_pad_made, i + 1)
                wait(pe, squared, N * i + n - 1)
                for r in range(2):
                    rows = slice(64 * r, 64 * r + 64)
                    ins = pe.matmul(p_s[n % 2][:, r, 0:m], kT[rows, u, g, kb * P:(kb + 1) * P],
                                    qT[rows, u, g, q0:q0 + m], start=True, stop=True)
                ins.then_inc(scored, 1)

            def add_up(i, u, n):
                qc, kb, g = UNITS[n]
                q0, m = span(n)
                if kb == 0:
                    wait(pe, o_copied, 2 * i + qc - 1)
                pe.wait_ge(weighed, N * i + n + 1)
                for r in range(2):
                    h = 2 * g + r
                    ins = pe.matmul(p_o[qc][32 * h:32 * h + 32, q0 - qc * HALF:q0 - qc * HALF + m],
                                    v_pad[:, u, kb, h, :], wt[:, n % 3, r, 0:m], start=(kb == 0),
                                    stop=(kb == 4 * (qc + 1) - 1), tile_position=(0, 32 * h))
                ins.then_inc(summed, 1)

            def turn_o(i):
                pe.wait_ge(o_copied, 2 * i + 2)
                pe.wait_ge(upos_copied, 2 * i + 2)
                for j in range(J):
                    ins = pe.transpose(p_m[:, j // 4, (j % 4) * P:(j % 4 + 1) * P],
                                       o_sb[:, j // 4, (j % 4) * P:(j % 4 + 1) * P], ident[:, :])
                ins.then_inc(o_turned, 1)

            def turn_ua(i):
                pe.wait_ge(ua_made, i + 1)
                pe.sem_inc(pe_begun, 1)
                for j in range(J):
                    ins = pe.transpose(p_m[0:U, j // 4, (j % 4) * P:(j % 4 + 1) * P], ua[:, j, :], ident[:, :])
                ins.then_inc(ua_turned, 1)

            def project_out(i):
                pe.wait_ge(uaT_made, i + 1)
                for j in range(J):
                    ins = pe.matmul(p_m[:, 0, j * C:(j + 1) * C], uaT[:, j * P:(j + 1) * P], w_out[:, :],
                                    start=True, stop=True, skip_group_check=True)
                ins.then_inc(projected, 1)

            pe.wait_ge(ident_made, 2)
            pe.wait_ge(const_in, N_CONST)
            pe.wait_ge(rel_made, 2)
            turn_xl(0)
            project_qkv(0)
            turn_qk(0, 0)
            turn_qk(0, 1)
            project_u_and_positions(0)
            score(0, 0, 0)
            score(0, 0, 1)

            def body(i, u, first, last):
                for n in range(N):
                    if n + 2 < N:
                        score(i, u, n + 2)
                    elif not last:
                        score(i + 1, 1 - u, n + 2 - N)
                    add_up(i, u, n)
                    if not first:
                        if n == 0:
                            turn_o(i - 1)
                        if n == 6:
                            turn_ua(i - 1)
                        if n == 8:
                            project_out(i - 1)
                    if not last:
                        if n == 12:
                            if not first:
                                pe.wait_ge(result_made, i)
                            turn_xl(i + 1)
                        if n == 13:
                            project_qkv(i + 1)
                        if n == 17:
                            turn_qk(i + 1, 0)
                        if n == 18:
                            turn_qk(i + 1, 1)
                        if n == 20:
                            project_u_and_positions(i + 1)

            over_images(body, pe)
            turn_o(B - 1)
            turn_ua(B - 1)
            project_out(B - 1)

        @block.vector
        def _(dve):
            dve.memset(xlT[C:C + 1, :], 1.0).then_inc(cleared, 1)
            dve.memset(uaT[U:U + 1, :], 1.0).then_inc(cleared, 1)
            dve.wait_ge(last_in, 16)
            dve.tensor_copy(last_w[:, :], last_col[:, 0:1].broadcast_to([P, P])).then_inc(rel_made, 1)
            dve.wait_ge(hankel_in, 16)
            dve.tensor_copy(rel[:, :], hankel[:, ::-1]).then_inc(rel_made, 1)
            dve.wait_ge(cleared, 8)
            dve.wait_ge(const_in, N_CONST)

            def prepare(i, u):
                dve.wait_ge(x_loaded, 16 * (i + 1))
                wait(dve, base_made, i)

                def power(ins):
                    ins.then_inc(var_made, 1)
                    dve.wait_ge(rstd_made, i + 1)

                wait(dve, xl_turned, i)
                normalise_tokens(dve, power, x_in[:, :, :], xl[:, :, :], C, 1e-5, ln, chain1, K1 * i)
                dve.sem_inc(xl_made, 1)
                dve.tensor_tensor(base[:, u, :, :], x_in[:, :, :], xl[:, :, :], ALU.add).then_inc(chain1, 1)
                dve.wait_ge(chain1, K1 * i + K1)
                dve.sem_inc(base_made, 1)
                dve.wait_ge(xl_turned, i + 1)
                wait(dve, upos_made, i)
                dve.tensor_copy(xlT[0:C, :], p_m[0:C, :, :].rearrange("p a b -> p (a b)")).then_inc(xlT_made, 1)
                dve.wait_ge(qkv_made, i + 1)
                wait(dve, qk_turned, 2 * i)
                qk = qkv[:, :, 0:2 * C].rearrange("p j (a d) -> p j a d", d=D)
                left = rest[:, :, :].rearrange("p j (a d) -> p j a d", d=D)

                def slot(s, sides=slice(0, 2)):
                    return parts[:, :, sides, :, s, :].rearrange("p j a h d -> p j (a h) d")

                n = [0]

                def step(ins):
                    n[0] += 1
                    ins.then_inc(chain2, 1)
                    dve.wait_ge(chain2, 11 * i + n[0])

                Q, K = slice(0, 1), slice(1, 2)
                step(dve.tensor_copy(slot(0), qk))
                step(dve.tensor_tensor(left, qk, slot(0), ALU.subtract))
                step(dve.tensor_copy(slot(3), left))
                step(dve.tensor_tensor(left, left, slot(3), ALU.subtract))
                step(dve.tensor_copy(slot(5, Q), left[:, :, 0:H, :]))
                step(dve.tensor_copy(slot(4, K), left[:, :, H:2 * H, :]))
                step(dve.tensor_copy(slot(1, Q), slot(0, Q)))
                step(dve.tensor_copy(slot(4, Q), slot(0, Q)))
                step(dve.tensor_copy(slot(2, Q), slot(3, Q)))
                step(dve.tensor_copy(slot(2, K), slot(0, K)))
                step(dve.tensor_copy(slot(5, K), slot(0, K)))
                dve.tensor_copy(slot(1, K), slot(3, K)).then_inc(parts_made, 1)
                wait(dve, suffix, (J - 1) * i)
                dve.tensor_copy(v[:, :, :], qkv[:, :, 2 * C:3 * C]).then_inc(v_made, 1)
                wait(dve, summed, N * (i - 1))
                dve.tensor_copy(v_pad[:, u, :, :, 0:D],
                                qkv[:, :, 2 * C:3 * C].rearrange("p j (h d) -> p j h d", d=D)).then_inc(v_pad_made, 1)
                for which, dst16 in ((0, qT), (1, kT)):
                    dve.wait_ge(qk_turned, 2 * i + which + 1)
                    dve.tensor_copy(dst16[:, u, :, :], p_m16).then_inc(qk_copied, 1)
                dve.wait_ge(upos_made, i + 1)
                dve.tensor_copy(u_gate[:, u, :, :].rearrange("p j c -> p (j c)"), p_m[:, 0, :]).then_inc(upos_copied, 1)
                dve.tensor_copy(pos[:, u, :, :].rearrange("p j c -> p (j c)"), p_m[:, 1, 0:J * C]).then_inc(upos_copied, 1)

            def copy_o(i, qc):
                dve.wait_ge(summed, N * i + (8 if qc == 0 else N))
                wait(dve, o_turned, i)
                dve.tensor_copy(o_sb[:, qc, :], p_o[qc][:, :]).then_inc(o_copied, 1)

            def finish(i, u):
                dve.wait_ge(o_turned, i + 1)
                wait(dve, ua_made, i)
                turned = p_m[:, :, :].rearrange("p a (j h c) -> p (a j) h c", h=H, c=32)
                dve.tensor_copy(cat[:, :, 0:C].rearrange("p j (h d) -> p j h d", d=D),
                                turned[:, :, :, 0:D]).then_inc(cat_made, 1)
                dve.tensor_copy(cat[:, :, C:U], pos[:, u, :, :]).then_inc(cat_made, 1)
                dve.wait_ge(cat_made, 2 * i + 2)

                def power(ins):
                    ins.then_inc(var2_made, 1)
                    dve.wait_ge(rstd2_made, i + 1)

                k = normalise_tokens(dve, power, cat[:, :, :], cat[:, :, :], U, 1e-3, ln2, chain3, (6 + 2) * i)
                gam = gamma[:, :].rearrange("p (o c) -> p o c", o=1).broadcast_to([P, J, U])
                bet = beta[:, :].rearrange("p (o c) -> p o c", o=1).broadcast_to([P, J, U])
                dve.tensor_tensor(cat[:, :, :], cat[:, :, :], gam, ALU.mult).then_inc(chain3, 1)
                dve.wait_ge(chain3, 8 * i + k + 1)
                dve.tensor_tensor(cat[:, :, :], cat[:, :, :], bet, ALU.add).then_inc(chain3, 1)
                dve.wait_ge(chain3, 8 * i + k + 2)
                wait(dve, ua_turned, i)
                dve.tensor_tensor(ua[:, :, :], cat[:, :, :], u_gate[:, u, :, :], ALU.mult).then_inc(ua_made, 1)
                dve.wait_ge(ua_turned, i + 1)
                wait(dve, projected, i)
                dve.tensor_copy(uaT[0:U, :], p_m[0:U, :, :].rearrange("p a b -> p (a b)")).then_inc(uaT_made, 1)
                dve.wait_ge(projected, i + 1)
                wait(dve, stored, 16 * i)
                dve.scalar_tensor_tensor(out=result[:, :, :].rearrange("p j c -> p (j c)"), in0=p_m[:, 0, 0:J * C],
                                         scalar=0.0, in1=base[:, u, :, :].rearrange("p j c -> p (j c)"),
                                         op0=ALU.max, op1=ALU.add).then_inc(result_made, 1)

            prepare(0, 0)

            def body(i, u, first, last):
                if not first:
                    finish(i - 1, 1 - u)
                copy_o(i, 0)
                if not last:
                    prepare(i + 1, 1 - u)
                copy_o(i, 1)

            over_images(body, dve)
            finish(B - 1, (B - 1) % 2)


NE = 16
TOP = 8
GROUP = P // NE
HID = 128


def expert_choice_layer(nc, t):
    with ExitStack() as ctx:
        def sb(name, shape, dt=F32):
            return ctx.enter_context(nc.sbuf_tensor("c_" + name, shape, dt))

        def ps(name, shape, dt=F32):
            return ctx.enter_context(nc.psum_tensor("c_" + name, shape, dt))

        def sem(name):
            return ctx.enter_context(nc.semaphore("c_" + name))

        ROUNDS = B // GROUP
        GJ = GROUP * J
        ident = sb("ident", [P, P])
        gate_w = sb("gate_w", [C + 1, P + P - NE])
        w1 = sb("w1", [C + 1, NE, HID])
        w2 = sb("w2", [HID, NE, C])
        w2_bias = sb("w2_bias", [1, NE, C])
        one = sb("one", [1, GROUP])
        own = sb("own", [P, GROUP])
        minus_half = sb("minus_half", [P, GJ])
        x_in = sb("x_in", [P, GJ, C])
        ln = {"sum": sb("ln_sum", [P, GJ]), "var": sb("ln_var", [P, GJ]), "rstd": sb("ln_rstd", [P, GJ]),
              "centred": sb("ln_centred", [P, GJ, C])[:, :, :], "square": sb("ln_square", [P, GJ, C])[:, :, :]}
        xl = sb("xl", [P, GJ, C])
        xlT = sb("xlT", [C + 1, 2, S])
        peak = sb("peak", [P, 1])
        expo = sb("expo", [P, S])
        total = sb("total", [P, 1])
        share = sb("share", [P, 1])
        probs = sb("probs", [P, S])
        best = sb("best", [P, TOP])
        without = sb("without", [P, S])
        picked = sb("picked", [P, S])
        pickedT = sb("pickedT", [P, J, P])
        pooled = sb("pooled", [C + 1, GROUP, NE])
        hid = sb("hid", [P, NE, GROUP])
        outT = sb("outT", [C, GROUP, NE])
        spread = sb("spread", [P, GROUP, C])
        result = sb("result", [P, GJ, C])

        p_t = ps("p_t", [P, 4, 512])
        p_l = ps("p_l", [P, 2, 512])
        p_x = ps("p_x", [P, 512])
        p_y = ps("p_y", [P, 512])

        const_in, cleared, padded, ident_made = sem("const_in"), sem("cleared"), sem("padded"), sem("ident_made")
        x_loaded, chain, var_made, rstd_made, xl_made = (
            sem("x_loaded"), sem("chain"), sem("var_made"), sem("rstd_made"), sem("xl_made"))
        turned, copied, gated = sem("turned"), sem("copied"), sem("gated")
        peak_made, expo_made, picked_made = sem("peak_made"), sem("expo_made"), sem("picked_made")
        picked_turned, pickedT_made = sem("picked_turned"), sem("pickedT_made")
        pooling_done, pooled_made = sem("pooling_done"), sem("pooled_made")
        hid_summed, hid_made = sem("hid_summed"), sem("hid_made")
        out_summed, outT_made, out_turned, spread_made = (
            sem("out_summed"), sem("outT_made"), sem("out_turned"), sem("spread_made"))
        scattered, result_made, stored, pe_begun, dve_begun = (
            sem("scattered"), sem("result_made"), sem("stored"), sem("pe_begun"), sem("dve_begun"))
        block = ctx.enter_context(nc.Block())

        def image(ap, i):
            return ap.rearrange("(b s) c -> b s c", b=B)[bass.ds(i, 1), :, :].rearrange("b (j p) c -> p (b j) c", p=P)

        @block.sync
        def _(sp):
            sp.wait_ge(padded, 1)
            sp.dma_start(gate_w[0:C, P - NE:P], t["L2_ffn_gate_w"]).then_inc(const_in, 16)
            sp.dma_start(gate_w[C:C + 1, P - NE:P], t["L2_ffn_gate_b"]).then_inc(const_in, 16)
            sp.dma_start(w1[:, :, :], t["L2_ffn_weight1"].rearrange("e d h -> d e h")).then_inc(const_in, 16)
            w2_in = t["L2_ffn_weight2"].rearrange("e h o -> h e o")
            sp.dma_start(w2[:, :, :], w2_in[0:HID]).then_inc(const_in, 16)
            sp.dma_start(w2_bias[:, :, :], w2_in[HID:HID + 1]).then_inc(const_in, 16)
            def load(k):
                for b in range(GROUP):
                    sp.dma_start(x_in[:, b * J:(b + 1) * J, :], image(t["t2"], k * GROUP + b)).then_inc(x_loaded, 16)

            def store(k):
                for b in range(GROUP):
                    sp.dma_start(image(t["t3"], k * GROUP + b), result[:, b * J:(b + 1) * J, :]).then_inc(stored, 16)

            load(0)
            with sp.Fori(0, ROUNDS - 1) as k:
                sp.wait_ge(result_made, k + 1)
                load(k + 1)
                store(k)
            sp.wait_ge(result_made, ROUNDS)
            store(ROUNDS - 1)
            sp.wait_ge(stored, 16 * B)

        @block.gpsimd
        def _(pool):
            pool.memset(ident[:, :], 0.0).then_inc(cleared, 1)
            pool.memset(minus_half[:, :], -0.5).then_inc(cleared, 1)
            pool.memset(own[:, :], 1.0).then_inc(cleared, 1)
            pool.wait_ge(cleared, 3)
            pool.affine_select(out=ident[:, :], in_=ident[:, :], compare_op=ALU.not_equal, fill=1.0, base=0,
                               pattern=[[-1, P]], channel_multiplier=1).then_inc(ident_made, 1)
            pool.affine_select(out=own[:, :], in_=own[:, :], compare_op=ALU.is_ge, fill=0.0, base=0,
                               pattern=[[-NE, GROUP]], channel_multiplier=1).then_inc(ident_made, 1)
            pool.wait_ge(ident_made, 2)
            pool.affine_select(out=own[:, :], in_=own[:, :], compare_op=ALU.is_ge, fill=0.0, base=NE - 1,
                               pattern=[[NE, GROUP]], channel_multiplier=-1).then_inc(ident_made, 1)
            with pool.Fori(0, ROUNDS) as k:
                pool.wait_ge(var_made, k + 1)
                pool.tensor_tensor(ln["rstd"][:, :], ln["var"][:, :], minus_half[:, :], ALU.pow).then_inc(rstd_made, 1)

        @block.scalar
        def _(act):
            with act.Fori(0, ROUNDS) as k:
                act.wait_ge(peak_made, k + 1)
                act.activation(expo[:, :], p_l[:, :, :].rearrange("p a b -> p (a b)"), ACT.Exp, bias=peak[:, 0:1],
                               accum_out=total[:, 0:1]).then_inc(expo_made, 1)
                act.wait_ge(hid_summed, k + 1)
                act.activation(hid[:, :, :].rearrange("p e b -> p (e b)"), p_x[:, 0:P], ACT.Gelu).then_inc(hid_made, 1)

        @block.tensor
        def _(pe):
            def arrived(semaphore, value):
                pe.wait_ge(semaphore, value)
                pe.sem_inc(pe_begun, 1)

            pe.wait_ge(ident_made, 3)
            pe.wait_ge(const_in, 16 * 5)
            with pe.Fori(0, ROUNDS) as k:
                arrived(xl_made, k + 1)
                for b in range(GROUP + 1):
                    if b < GROUP:
                        if b >= 2:
                            arrived(copied, GROUP * k + b - 1)
                        for j in range(J):
                            at = 2 * (b % 2) + j // 4
                            ins = pe.transpose(p_t[0:C, at, (j % 4) * P:(j % 4 + 1) * P], xl[:, b * J + j, :], ident[:, :])
                        ins.then_inc(turned, 1)
                    if b > 0:
                        c = b - 1
                        arrived(copied, GROUP * k + c + 1)
                        w = gate_w[:, P - NE - NE * c:2 * P - NE - NE * c]
                        for half in range(2):
                            ins = pe.matmul(p_l[:, half, :], w, xlT[:, c % 2, half * 512:(half + 1) * 512],
                                            start=(c == 0), stop=(c == GROUP - 1), skip_group_check=True)
                        ins.then_inc(gated, 1)
                arrived(picked_made, k + 1)
                for j in range(J):
                    ins = pe.transpose(p_t[:, j // 4, (j % 4) * P:(j % 4 + 1) * P], picked[:, j * P:(j + 1) * P], ident[:, :])
                ins.then_inc(picked_turned, 1)
                arrived(pickedT_made, k + 1)
                for b in range(GROUP):
                    for j in range(J):
                        ins = pe.matmul(p_x[0:C, b * NE:(b + 1) * NE], xl[:, b * J + j, :],
                                        pickedT[:, j, b * NE:(b + 1) * NE], start=(j == 0), stop=(j == J - 1),
                                        skip_group_check=True)
                ins.then_inc(pooling_done, 1)
                arrived(pooled_made, k + 1)
                for e in range(NE):
                    ins = pe.matmul(p_x[:, e * GROUP:(e + 1) * GROUP], w1[:, e, :], pooled[:, :, e],
                                    start=True, stop=True, skip_group_check=True)
                ins.then_inc(hid_summed, 1)
                arrived(hid_made, k + 1)
                for e in range(NE):
                    at = p_y[0:C, e * GROUP:(e + 1) * GROUP]
                    pe.matmul(at, w2[:, e, :], hid[:, e, :], start=True, stop=False, skip_group_check=True)
                    ins = pe.matmul(at, w2_bias[:, e, :], one[:, :], start=False, stop=True, skip_group_check=True)
                ins.then_inc(out_summed, 1)
                arrived(outT_made, k + 1)
                pe.transpose(p_x[:, 0:C], outT[:, :, :].rearrange("o b e -> o (b e)"), ident[0:C, 0:C]).then_inc(out_turned, 1)
                arrived(spread_made, k + 1)
                for j in range(J):
                    ins = pe.matmul(p_t[:, j // 2, (j % 2) * 256:(j % 2 + 1) * 256], picked[:, j * P:(j + 1) * P],
                                    spread[:, :, :].rearrange("p b c -> p (b c)"), start=True, stop=True,
                                    skip_group_check=True)
                ins.then_inc(scattered, 1)

        @block.vector
        def _(dve):
            dve.memset(gate_w[:, :], 0.0).then_inc(chain, 1)
            dve.memset(xlT[C:C + 1, :, :], 1.0).then_inc(chain, 1)
            dve.memset(pooled[C:C + 1, :, :], 1.0).then_inc(chain, 1)
            dve.memset(one[:, :], 1.0).then_inc(chain, 1)
            dve.wait_ge(chain, 4)
            dve.sem_inc(padded, 1)
            dve.wait_ge(ident_made, 3)
            M = 6 + 4 + GROUP
            with dve.Fori(0, ROUNDS) as k:
                dve.wait_ge(x_loaded, 16 * GROUP * (k + 1))

                def power(ins):
                    ins.then_inc(var_made, 1)
                    dve.wait_ge(rstd_made, k + 1)

                n = [normalise_tokens(dve, power, x_in[:, :, :], xl[:, :, :], C, 1e-5, ln, chain, M * k + 4)]
                dve.sem_inc(xl_made, 1)

                def step(ins):
                    n[0] += 1
                    ins.then_inc(chain, 1)
                    dve.wait_ge(chain, M * k + 4 + n[0])

                for b in range(GROUP):
                    dve.wait_ge(turned, GROUP * k + b + 1)
                    if b >= 2:
                        dve.wait_ge(gated, GROUP * k + b - 1)
                    dve.tensor_copy(xlT[0:C, b % 2, :], p_t[0:C, 2 * (b % 2):2 * (b % 2) + 2, :]
                                    .rearrange("p a b -> p (a b)")).then_inc(copied, 1)
                dve.wait_ge(gated, GROUP * (k + 1))
                logits = p_l[:, :, :].rearrange("p a b -> p (a b)")
                dve.tensor_reduce(peak[:, :], logits, X, ALU.max, negate=True).then_inc(peak_made, 1)
                dve.wait_ge(expo_made, k + 1)
                step(dve.reciprocal(share[:, :], total[:, :]))
                step(dve.tensor_scalar(probs[:, :], expo[:, :], share[:, 0:1], None, ALU.mult))
                dve.sem_inc(dve_begun, 1)
                step(dve.max(best[:, :], probs[:, :]))
                dve.sem_inc(dve_begun, 1)
                step(dve.match_replace(out=without[:, :], in_to_replace=best[:, :], in_values=probs[:, :], imm_value=-1.0))
                dve.scalar_tensor_tensor(out=picked[:, :], in0=without[:, :], scalar=0.0, in1=probs[:, :],
                                         op0=ALU.is_lt, op1=ALU.mult).then_inc(picked_made, 1)
                dve.wait_ge(picked_turned, k + 1)
                dve.tensor_copy(pickedT[:, :, :].rearrange("p j q -> p (j q)"),
                                p_t[:, 0:2, :].rearrange("p a b -> p (a b)")).then_inc(pickedT_made, 1)
                dve.wait_ge(pooling_done, k + 1)
                dve.tensor_copy(pooled[0:C, :, :].rearrange("p b e -> p (b e)"), p_x[0:C, 0:P]).then_inc(pooled_made, 1)
                dve.wait_ge(out_summed, k + 1)
                dve.tensor_copy(outT[:, :, :], p_y[0:C, 0:P].rearrange("o (e b) -> o b e", b=GROUP)).then_inc(outT_made, 1)
                dve.wait_ge(out_turned, k + 1)
                dve.tensor_tensor(spread[:, :, :], p_x[:, 0:C].rearrange("p (o c) -> p o c", o=1).broadcast_to([P, GROUP, C]),
                                  mid(own[:, :], C), ALU.mult).then_inc(spread_made, 1)
                dve.wait_ge(scattered, k + 1)
                wait(dve, stored, 16 * GROUP * k)
                for b in range(GROUP):
                    at = p_t[:, :, :].rearrange("p a (j b c) -> p (a j) b c", j=2, b=GROUP)[:, :, b, :]
                    dve.tensor_tensor(result[:, b * J:(b + 1) * J, :], at, x_in[:, b * J:(b + 1) * J, :],
                                            ALU.add).then_inc(chain, 1)
                n[0] += GROUP
                assert n[0] == M
                dve.wait_ge(chain, M * (k + 1) + 4)
                dve.sem_inc(result_made, 1)


ER = 8


def softmax_attention_and_router_layer(nc, t):
    with ExitStack() as ctx:
        def sb(name, shape, dt=F32):
            return ctx.enter_context(nc.sbuf_tensor("d_" + name, shape, dt))

        def ps(name, shape, dt=F32):
            return ctx.enter_context(nc.psum_tensor("d_" + name, shape, dt))

        def sem(name):
            return ctx.enter_context(nc.semaphore("d_" + name))

        QKV = 3 * C
        SCALE = float(C) ** -0.5
        RING = 4
        SHIFT = 6
        ident = sb("ident", [P, P])
        ident16 = sb("ident16", [P, P], BF16)
        w_in = sb("w_in", [C + 1, QKV])
        w_out = sb("w_out", [C + 1, C])
        w_router = sb("w_router", [C + 1, ER])
        w_expert = sb("w_expert", [C + 1, ER * C])
        earlier = sb("earlier", [P, ER, ER])
        minus_half = sb("minus_half", [P, J])
        x_in = sb("x_in", [P, J, C])
        ln = {"sum": sb("ln_sum", [P, J]), "var": sb("ln_var", [P, J]), "rstd": sb("ln_rstd", [P, J]),
              "centred": sb("ln_centred", [P, J, C])[:, :, :], "square": sb("ln_square", [P, J, C])[:, :, :]}
        ln2 = {"sum": sb("ln2_sum", [P, J]), "var": sb("ln2_var", [P, J]), "rstd": sb("ln2_rstd", [P, J]),
               "centred": sb("ln2_centred", [P, J, C])[:, :, :], "square": sb("ln2_square", [P, J, C])[:, :, :]}
        xl = sb("xl", [P, J, C])
        x_keep = sb("x_keep", [P, 2, J, C])
        xlT = sb("xlT", [C + 1, S])
        qkv = sb("qkv", [P, J, QKV])
        rest = sb("rest", [P, J, 2 * C])
        parts = sb("parts", [P, J, 2, H, SLOTS, D], BF16)
        qT = sb("qT", [P, 2, 2, S], BF16)
        kT = sb("kT", [P, 2, 2, S], BF16)
        v_pad = sb("v_pad", [P, 2, J, H, 32])
        peaks = sb("peaks", [P, J * H, 2])
        shift = sb("shift", [P, J * H])
        wt = sb("wt", [P, RING, 2, HALF])
        o_sb = sb("o_sb", [P, 2, HALF])
        share = sb("share", [P, J * H])
        att = sb("att", [P, J, C])
        attT = sb("attT", [C + 1, S])
        x4 = sb("x4", [P, J, C])
        xl4 = sb("xl4", [P, J, C])
        xl4T = sb("xl4T", [C + 1, S])
        col = sb("col", [P, J])
        expo = sb("expo", [P, J, ER])
        prob = sb("prob", [P, J, ER])
        above = sb("above", [P, J, ER, ER])
        equal = sb("equal", [P, J, ER, ER])
        rank = sb("rank", [P, J, ER])
        mix = sb("mix", [P, J, ER])
        scaled = sb("scaled", [P, 4, ER, C])
        mixed = sb("mixed", [P, 4, C])
        result = sb("result", [P, J, C])

        p_s = [ps(f"p_s{k}", [P, 2, HALF]) for k in range(2)]
        p_o = [ps(f"p_o{k}", [P, HALF]) for k in range(2)]
        p_m = ps("p_m", [P, 2, HALF])
        p_m16 = p_m[:, :, :].rearrange("p a b -> p (a b)").bitcast(BF16).rearrange("p (a b) -> p a b", a=2)

        UNITS = [(qc, kb, g) for qc in range(2) for kb in range(J) for g in range(2)]
        N = len(UNITS)
        assert N % RING == 0
        PEAKS = [(j, h, half) for j in range(J) for h in range(H) for half in range(2)]
        NP = len(PEAKS)
        PEAK_UNITS = range(17, 29)

        const_in, cleared, ident_made = sem("const_in"), sem("cleared"), sem("ident_made")
        x_loaded = sem("x_loaded")
        chain1, chain2, chain3, chain4 = sem("chain1"), sem("chain2"), sem("chain3"), sem("chain4")
        var_made, rstd_made = sem("var_made"), sem("rstd_made")
        var2_made, rstd2_made = sem("var2_made"), sem("rstd2_made")
        xl_made = sem("xl_made")
        x_kept = sem("x_kept")
        xl_turned = sem("xl_turned")
        xlT_made = sem("xlT_made")
        qkv_projected = sem("qkv_projected")
        qkv_made = sem("qkv_made")
        parts_made = sem("parts_made")
        v_pad_made = sem("v_pad_made")
        qk_turned = sem("qk_turned")
        qk_copied = sem("qk_copied")
        peak_scored = sem("peak_scored")
        peak_read = sem("peak_read")
        shift_made = sem("shift_made")
        scored = sem("scored")
        weighed = sem("weighed")
        summed = sem("summed")
        o_copied = sem("o_copied")
        o_turned = sem("o_turned")
        att_made = sem("att_made")
        att_turned = sem("att_turned")
        attT_made = sem("attT_made")
        projected = sem("projected")
        xl4_made = sem("xl4_made")
        xl4_turned = sem("xl4_turned")
        xl4T_made = sem("xl4T_made")
        routed = sem("routed")
        logits_read = sem("logits_read")
        expo_made = sem("expo_made")
        experts_made = sem("experts_made")
        experts_read = sem("experts_read")
        result_made = sem("result_made")
        stored = sem("stored")
        pe_begun = sem("pe_begun")
        block = ctx.enter_context(nc.Block())

        src = t["t3"].rearrange("(b s) c -> b s c", b=B)
        dst = t["t4"].rearrange("(b s) c -> b s c", b=B)

        def image(ap, i):
            return ap[bass.ds(i, 1), :, :].rearrange("b (j p) c -> p (b j) c", p=P)

        @block.sync
        def _(sp):
            sp.dma_start(w_in[0:C, :], t["L3_attn_W_qkv"]).then_inc(const_in, 16)
            sp.dma_start(w_in[C:C + 1, :], t["L3_attn_b_qkv"]).then_inc(const_in, 16)
            sp.dma_start(w_out[0:C, :], t["L3_attn_W_proj"]).then_inc(const_in, 16)
            sp.dma_start(w_out[C:C + 1, :], t["L3_attn_b_proj"]).then_inc(const_in, 16)
            sp.dma_start(w_router[0:C, :], t["L3_ffn_router_w"]).then_inc(const_in, 16)
            sp.dma_start(w_router[C:C + 1, :], t["L3_ffn_router_b"]).then_inc(const_in, 16)
            sp.dma_start(w_expert[0:C, :].rearrange("d (e c) -> d e c", e=ER),
                         t["L3_ffn_expert_w"].rearrange("e d c -> d e c")).then_inc(const_in, 16)
            sp.dma_start(w_expert[C:C + 1, :], t["L3_ffn_expert_b"]).then_inc(const_in, 16)

            def load(i):
                sp.dma_start(x_in[:, :, :], image(src, i)).then_inc(x_loaded, 16)

            def store(i):
                sp.wait_ge(result_made, 2 * i + 2)
                sp.dma_start(image(dst, i), result[:, :, :]).then_inc(stored, 16)

            load(0)

            def body(i, u, first, last):
                if not last:
                    sp.wait_ge(x_kept, i + 1)
                    load(i + 1)
                if not first:
                    store(i - 1)

            over_images(body, sp)
            store(B - 1)
            sp.wait_ge(stored, 16 * B)

        @block.gpsimd
        def _(pool):
            pool.memset(ident[:, :], 0.0).then_inc(cleared, 1)
            pool.memset(ident16[:, :], 0.0).then_inc(cleared, 1)
            pool.memset(earlier[:, :, :], 1.0).then_inc(cleared, 1)
            pool.memset(parts[:, :, :, :, :, :], 0.0).then_inc(cleared, 1)
            pool.memset(v_pad[:, :, :, :, :], 0.0).then_inc(cleared, 1)
            pool.memset(minus_half[:, :], -0.5).then_inc(cleared, 1)
            pool.wait_ge(cleared, 6)
            for m in (ident, ident16):
                pool.affine_select(out=m[:, :], in_=m[:, :], compare_op=ALU.not_equal, fill=1.0, base=0,
                                   pattern=[[-1, P]], channel_multiplier=1).then_inc(ident_made, 1)
            pool.affine_select(out=earlier[:, :, :], in_=earlier[:, :, :], compare_op=ALU.is_gt, fill=0.0, base=0,
                               pattern=[[1, ER], [-1, ER]], channel_multiplier=0).then_inc(ident_made, 1)
            pool.memset(parts[:, :, 1, :, SHIFT, 0:3], 1.0).then_inc(ident_made, 1)
            pool.memset(v_pad[:, :, :, :, D:D + 1], 1.0).then_inc(ident_made, 1)

            def power(i):
                pool.wait_ge(var_made, i + 1)
                pool.tensor_tensor(ln["rstd"][:, :], ln["var"][:, :], minus_half[:, :], ALU.pow).then_inc(rstd_made, 1)

            def power2(i):
                pool.wait_ge(var2_made, i + 1)
                pool.tensor_tensor(ln2["rstd"][:, :], ln2["var"][:, :], minus_half[:, :], ALU.pow).then_inc(rstd2_made, 1)

            power(0)

            def body(i, u, first, last):
                if not first:
                    power2(i - 1)
                if not last:
                    power(i + 1)

            over_images(body, pool)
            power2(B - 1)

        @block.scalar
        def _(act):
            act.preload_act_table(ACT.Exp)

            def weigh(i, n):
                act.wait_ge(scored, N * i + n + 1)
                wait(act, summed, N * i + n + 1 - RING)
                act.activation(wt[:, n % RING, :, :], p_s[n % 2][:, :, :], ACT.Exp, scale=SCALE).then_inc(weighed, 1)

            def copy_xlT(i):
                act.wait_ge(xl_turned, i + 1)
                wait(act, qkv_projected, i)
                act.activation(xlT[0:C, :], p_m[0:C, :, :].rearrange("p a b -> p (a b)"), ACT.Copy).then_inc(xlT_made, 1)

            def copy_qkv(i):
                act.wait_ge(qkv_projected, i + 1)
                wait(act, parts_made, i)
                wait(act, v_pad_made, i)
                act.activation(qkv[:, :, :].rearrange("p (a j) c -> p a (j c)", a=2),
                               p_m[:, :, 0:J // 2 * QKV], ACT.Copy).then_inc(qkv_made, 1)

            def copy_qk(i, u, k):
                act.wait_ge(qk_turned, 3 * i + k + 1)
                out = (kT, qT, qT)[k]
                wait(act, scored, N * (i - 1))
                act.activation(out[:, u, :, :], p_m16, ACT.Copy).then_inc(qk_copied, 1)

            def exp_router(i):
                act.wait_ge(logits_read, i + 1)
                act.activation(expo[:, :, :], expo[:, :, :], ACT.Exp).then_inc(expo_made, 1)

            def turned_copy(i, made, out, out_semaphore):
                act.wait_ge(made, i + 1)
                act.activation(out[0:C, :], p_m[0:C, :, :].rearrange("p a b -> p (a b)"), ACT.Copy).then_inc(out_semaphore, 1)

            copy_xlT(0)
            copy_qkv(0)
            for k in range(3):
                copy_qk(0, 0, k)

            def body(i, u, first, last):
                for n in range(N):
                    weigh(i, n)
                    if not first:
                        if n == 2:
                            turned_copy(i - 1, att_turned, attT, attT_made)
                        if n == 7:
                            turned_copy(i - 1, xl4_turned, xl4T, xl4T_made)
                        if n == 9:
                            exp_router(i - 1)
                    if not last:
                        if n == 13:
                            copy_xlT(i + 1)
                        if n == 14:
                            copy_qkv(i + 1)
                        if n == 16:
                            copy_qk(i + 1, 1 - u, 0)
                        if n == 17:
                            copy_qk(i + 1, 1 - u, 1)
                        if n == N - 3:
                            copy_qk(i + 1, 1 - u, 2)

            over_images(body, act)
            turned_copy(B - 1, att_turned, attT, attT_made)
            turned_copy(B - 1, xl4_turned, xl4T, xl4T_made)
            exp_router(B - 1)

        @block.tensor
        def _(pe):
            def arrived(semaphore, value):
                wait(pe, semaphore, value)
                pe.sem_inc(pe_begun, 1)

            def turn(i, made, x, done):
                arrived(made, i + 1)
                for j in range(J):
                    ins = pe.transpose(p_m[0:C, j // 4, (j % 4) * P:(j % 4 + 1) * P], x[:, j, :], ident[:, :])
                ins.then_inc(done, 1)

            def project(i, made, xT, w, width, done, half=False):
                arrived(made, i + 1)
                for j in range(J):
                    at = p_m[:, 0, j * width:(j + 1) * width] if half else \
                        p_m[:, j // 4, (j % 4) * width:(j % 4 + 1) * width]
                    ins = pe.matmul(at, xT[:, j * P:(j + 1) * P], w[:, :], start=True, stop=True,
                                    skip_group_check=True)
                ins.then_inc(done, 1)

            def turn_xl(i):
                wait(pe, experts_read, 2 * (i - 1))
                turn(i, xl_made, xl, xl_turned)

            def turn_qk(i, k):
                if k == 2:
                    pe.wait_ge(peak_read, NP * (i + 1))
                    pe.wait_ge(shift_made, i + 1)
                else:
                    arrived(parts_made, i + 1)
                    if k == 1:
                        arrived(qk_copied, 3 * i + 1)
                for g in range(2):
                    for j in range(J):
                        ins = pe.transpose(p_m16[:, g, j * P:(j + 1) * P],
                                           parts[:, j, int(k == 0), 2 * g:2 * g + 2, :, :].rearrange("p h s d -> p (h s d)"),
                                           ident16[:, :])
                ins.then_inc(qk_turned, 1)

            def peak(i, u, m):
                j, h, half = PEAKS[m]
                g, r = h // 2, h % 2
                if m == 0:
                    arrived(qk_copied, 3 * i + 2)
                if m >= 2:
                    pe.wait_ge(peak_read, NP * i + m - 1)
                else:
                    wait(pe, peak_read, NP * i)
                rows = slice(64 * r, 64 * r + SHIFT * D)
                pe.matmul(p_m[:, m % 2, :], qT[rows, u, g, j * P:(j + 1) * P],
                          kT[rows, u, g, half * HALF:(half + 1) * HALF], start=True, stop=True).then_inc(peak_scored, 1)

            def score(i, u, n):
                qc, kb, g = UNITS[n]
                if n == 0:
                    pe.wait_ge(qk_copied, 3 * i + 3)
                    pe.wait_ge(v_pad_made, i + 1)
                wait(pe, weighed, N * i + n - 1)
                for r in range(2):
                    rows = slice(64 * r, 64 * r + 64)
                    ins = pe.matmul(p_s[n % 2][:, r, :], kT[rows, u, g, kb * P:(kb + 1) * P],
                                    qT[rows, u, g, qc * HALF:(qc + 1) * HALF], start=True, stop=True)
                ins.then_inc(scored, 1)

            def add_up(i, u, n):
                qc, kb, g = UNITS[n]
                if kb == 0:
                    wait(pe, o_copied, 2 * i + qc - 1)
                pe.wait_ge(weighed, N * i + n + 1)
                for r in range(2):
                    h = 2 * g + r
                    ins = pe.matmul(p_o[qc][32 * h:32 * h + 32, :], v_pad[:, u, kb, h, :], wt[:, n % RING, r, :],
                                    start=(kb == 0), stop=(kb == J - 1), tile_position=(0, 32 * h))
                ins.then_inc(summed, 1)

            def turn_o(i):
                pe.wait_ge(o_copied, 2 * i + 2)
                for j in range(J):
                    ins = pe.transpose(p_m[:, j // 4, (j % 4) * P:(j % 4 + 1) * P],
                                       o_sb[:, j // 4, (j % 4) * P:(j % 4 + 1) * P], ident[:, :])
                ins.then_inc(o_turned, 1)

            def experts(i, half):
                if half:
                    arrived(experts_read, 2 * i + 1)
                else:
                    arrived(logits_read, i + 1)
                for j in range(J // 2):
                    tok = (half * J // 2 + j) * P
                    ins = pe.matmul(p_m[:, j // 2, (j % 2) * 256:(j % 2 + 1) * 256], xl4T[:, tok:tok + P],
                                    w_expert[:, :], start=True, stop=True, skip_group_check=True)
                ins.then_inc(experts_made, 1)

            def finish_turn_att(i):
                turn(i, att_made, att, att_turned)

            def finish_project(i):
                project(i, attT_made, attT, w_out, C, projected, half=True)

            def finish_turn_x(i):
                turn(i, xl4_made, xl4, xl4_turned)

            def finish_route(i):
                project(i, xl4T_made, xl4T, w_router, ER, routed, half=True)

            pe.wait_ge(ident_made, 5)
            pe.wait_ge(const_in, 16 * 8)
            turn_xl(0)
            project(0, xlT_made, xlT, w_in, QKV, qkv_projected)
            turn_qk(0, 0)
            turn_qk(0, 1)
            for m in range(NP):
                peak(0, 0, m)
            turn_qk(0, 2)
            score(0, 0, 0)
            score(0, 0, 1)

            def body(i, u, first, last):
                for n in range(N):
                    if n + 2 < N:
                        score(i, u, n + 2)
                    elif not last:
                        score(i + 1, 1 - u, n + 2 - N)
                    add_up(i, u, n)
                    if not first:
                        if n == 0:
                            turn_o(i - 1)
                        if n == 1:
                            finish_turn_att(i - 1)
                        if n == 3:
                            finish_project(i - 1)
                        if n == 6:
                            finish_turn_x(i - 1)
                        if n == 7:
                            finish_route(i - 1)
                        if n == 9:
                            experts(i - 1, 0)
                        if n == 10:
                            experts(i - 1, 1)
                    if not last:
                        if n == 12:
                            turn_xl(i + 1)
                        if n == 13:
                            project(i + 1, xlT_made, xlT, w_in, QKV, qkv_projected)
                        if n == 15:
                            turn_qk(i + 1, 0)
                        if n == 16:
                            turn_qk(i + 1, 1)
                        if n in PEAK_UNITS:
                            k = n - PEAK_UNITS[0]
                            for m in range(NP * k // len(PEAK_UNITS), NP * (k + 1) // len(PEAK_UNITS)):
                                peak(i + 1, 1 - u, m)
                        if n == 29:
                            turn_qk(i + 1, 2)

            over_images(body, pe)
            i = B - 1
            turn_o(i)
            finish_turn_att(i)
            finish_project(i)
            finish_turn_x(i)
            finish_route(i)
            experts(i, 0)
            experts(i, 1)

        @block.vector
        def _(dve):
            dve.memset(xlT[C:C + 1, :], 1.0).then_inc(chain4, 1)
            dve.memset(attT[C:C + 1, :], 1.0).then_inc(chain4, 1)
            dve.memset(xl4T[C:C + 1, :], 1.0).then_inc(chain4, 1)
            dve.wait_ge(chain4, 3)
            dve.wait_ge(ident_made, 5)

            def prepare(i, u):
                dve.wait_ge(x_loaded, 16 * (i + 1))
                wait(dve, xl_turned, i)

                def power(ins):
                    ins.then_inc(var_made, 1)
                    dve.wait_ge(rstd_made, i + 1)

                normalise_tokens(dve, power, x_in[:, :, :], xl[:, :, :], C, 1e-5, ln, chain1, 6 * i)
                dve.sem_inc(xl_made, 1)
                dve.tensor_copy(x_keep[:, u, :, :], x_in[:, :, :]).then_inc(x_kept, 1)
                dve.wait_ge(qkv_made, i + 1)
                wait(dve, qk_turned, 3 * i)
                qk = qkv[:, :, 0:2 * C].rearrange("p j (a d) -> p j a d", d=D)
                left = rest[:, :, :].rearrange("p j (a d) -> p j a d", d=D)

                def slot(s, sides=slice(0, 2)):
                    return parts[:, :, sides, :, s, :].rearrange("p j a h d -> p j (a h) d")

                n = [0]

                def step(ins):
                    n[0] += 1
                    ins.then_inc(chain2, 1)
                    dve.wait_ge(chain2, 15 * i + n[0])

                Q, K = slice(0, 1), slice(1, 2)
                step(dve.tensor_copy(slot(0), qk))
                step(dve.tensor_tensor(left, qk, slot(0), ALU.subtract))
                step(dve.tensor_copy(slot(3), left))
                step(dve.tensor_tensor(left, left, slot(3), ALU.subtract))
                step(dve.tensor_copy(slot(5, Q), left[:, :, 0:H, :]))
                step(dve.tensor_copy(slot(4, K), left[:, :, H:2 * H, :]))
                step(dve.tensor_copy(slot(1, Q), slot(0, Q)))
                step(dve.tensor_copy(slot(4, Q), slot(0, Q)))
                step(dve.tensor_copy(slot(2, Q), slot(3, Q)))
                step(dve.tensor_copy(slot(2, K), slot(0, K)))
                step(dve.tensor_copy(slot(5, K), slot(0, K)))
                dve.tensor_copy(slot(1, K), slot(3, K)).then_inc(parts_made, 1)
                wait(dve, summed, N * (i - 1))
                dve.tensor_copy(v_pad[:, u, :, :, 0:D],
                                qkv[:, :, 2 * C:3 * C].rearrange("p j (h d) -> p j h d", d=D)).then_inc(v_pad_made, 1)
                assert n[0] == 11

            def row_maxima(i):
                n = [11]

                def step(ins):
                    n[0] += 1
                    ins.then_inc(chain2, 1)
                    dve.wait_ge(chain2, 15 * i + n[0])

                for m in range(NP):
                    j, h, half = PEAKS[m]
                    dve.wait_ge(peak_scored, NP * i + m + 1)
                    dve.tensor_reduce(peaks[:, j * H + h, half:half + 1], p_m[:, m % 2, :], X, ALU.max).then_inc(peak_read, 1)
                dve.wait_ge(peak_read, NP * (i + 1))
                step(dve.tensor_reduce(shift[:, :], peaks[:, :, :], X, ALU.max, negate=True))

                def part(k):
                    return parts[:, :, 0, :, SHIFT, k]

                sh = shift[:, :].rearrange("p (j h) -> p j h", h=H)
                step(dve.tensor_copy(part(0), sh))
                step(dve.tensor_tensor(sh, sh, part(0), ALU.subtract))
                step(dve.tensor_copy(part(1), sh))
                dve.tensor_tensor(part(2), sh, part(1), ALU.subtract).then_inc(shift_made, 1)
                assert n[0] == 15

            def copy_o(i, qc):
                dve.wait_ge(summed, N * i + (N // 2) * (qc + 1))
                wait(dve, o_turned, i)
                dve.tensor_copy(o_sb[:, qc, :], p_o[qc][:, :]).then_inc(o_copied, 1)

            def finish(i, u):
                n = [0]
                K = 2 + 6 + 10

                def step(ins):
                    n[0] += 1
                    ins.then_inc(chain3, 1)
                    dve.wait_ge(chain3, K * i + n[0])

                dve.wait_ge(o_turned, i + 1)
                turned = p_m[:, :, :].rearrange("p a (j h c) -> p (a j h) c", h=H, c=32)
                step(dve.reciprocal(share[:, :], turned[:, :, D]))
                dve.tensor_tensor(att[:, :, :].rearrange("p j (h d) -> p (j h) d", d=D), turned[:, :, 0:D],
                                  mid(share[:, :], D), ALU.mult).then_inc(att_made, 1)
                dve.wait_ge(projected, i + 1)
                step(dve.tensor_tensor(x4[:, :, :].rearrange("p j c -> p (j c)"), p_m[:, 0, 0:J * C],
                                       x_keep[:, u, :, :].rearrange("p j c -> p (j c)"), ALU.add))

                def power(ins):
                    ins.then_inc(var2_made, 1)
                    dve.wait_ge(rstd2_made, i + 1)

                n[0] += normalise_tokens(dve, power, x4[:, :, :], xl4[:, :, :], C, 1e-5, ln2, chain3, K * i + n[0])
                dve.sem_inc(xl4_made, 1)
                dve.wait_ge(routed, i + 1)
                logits = p_m[:, 0, 0:J * ER].rearrange("p (j e) -> p j e", e=ER)
                step(dve.tensor_reduce(col[:, :], logits, X, ALU.max))
                dve.tensor_tensor(expo[:, :, :], logits, mid(col[:, :], ER), ALU.subtract).then_inc(logits_read, 1)
                dve.wait_ge(expo_made, i + 1)
                step(dve.tensor_reduce(col[:, :], expo[:, :, :], X, ALU.add))
                step(dve.reciprocal(col[:, :], col[:, :]))
                step(dve.tensor_tensor(prob[:, :, :], expo[:, :, :], mid(col[:, :], ER), ALU.mult))
                mine = prob[:, :, :].rearrange("p j (e o) -> p j e o", o=1).broadcast_to([P, J, ER, ER])
                other = prob[:, :, :].rearrange("p j (o e) -> p j o e", o=1).broadcast_to([P, J, ER, ER])
                before = earlier[:, :, :].rearrange("p (o e) f -> p o e f", o=1).broadcast_to([P, J, ER, ER])
                step(dve.tensor_tensor(equal[:, :, :, :], other, mine, ALU.is_equal))
                step(dve.tensor_tensor(equal[:, :, :, :], equal[:, :, :, :], before, ALU.mult))
                step(dve.tensor_tensor(above[:, :, :, :], other, mine, ALU.is_gt))
                step(dve.tensor_tensor(above[:, :, :, :], above[:, :, :, :], equal[:, :, :, :], ALU.add))
                step(dve.tensor_reduce(rank[:, :, :], above[:, :, :, :], X, ALU.add))
                step(dve.scalar_tensor_tensor(out=mix[:, :, :], in0=rank[:, :, :], scalar=2.0, in1=prob[:, :, :],
                                              op0=ALU.is_lt, op1=ALU.mult))
                dve.tensor_reduce(col[:, :], mix[:, :, :], X, ALU.add).then_inc(chain4, 1)
                dve.wait_ge(chain4, 6 * i + 4)
                dve.reciprocal(col[:, :], col[:, :]).then_inc(chain4, 1)
                dve.wait_ge(chain4, 6 * i + 5)
                dve.tensor_tensor(mix[:, :, :], mix[:, :, :], mid(col[:, :], ER), ALU.mult).then_inc(chain4, 1)
                dve.wait_ge(chain4, 6 * i + 6)
                wait(dve, stored, 16 * i)
                for half in range(2):
                    js = slice(half * J // 2, (half + 1) * J // 2)
                    dve.wait_ge(experts_made, 2 * i + half + 1)
                    dve.tensor_tensor(scaled[:, :, :, :].rearrange("p j e c -> p (j e) c"),
                                      p_m[:, :, :].rearrange("p a (x c) -> p (a x) c", c=C),
                                      mid(mix[:, js, :].rearrange("p j e -> p (j e)"), C), ALU.mult).then_inc(experts_read, 1)
                    dve.wait_ge(experts_read, 2 * i + half + 1)
                    dve.tensor_reduce(mixed[:, :, :], scaled[:, :, :, :].rearrange("p j e c -> p j c e"), X,
                                      ALU.add).then_inc(chain4, 1)
                    dve.wait_ge(chain4, 6 * i + 7 + 2 * half)
                    dve.tensor_tensor(result[:, js, :], mixed[:, :, :], x4[:, js, :], ALU.add).then_inc(result_made, 1)
                    if half == 0:
                        dve.wait_ge(result_made, 2 * i + 1)
                        dve.sem_inc(chain4, 1)
                assert n[0] == K, n[0]

            prepare(0, 0)
            row_maxima(0)

            def body(i, u, first, last):
                if not first:
                    finish(i - 1, 1 - u)
                if not last:
                    prepare(i + 1, 1 - u)
                copy_o(i, 0)
                if not last:
                    row_maxima(i + 1)
                copy_o(i, 1)

            over_images(body, dve)
            finish(B - 1, (B - 1) % 2)


def kernel(**inputs):
    import numpy as np
    import concourse.bacc as bacc
    from concourse.bass_utils import run_bass_kernel_spmd as run

    def lay(a):
        return np.ascontiguousarray(a)

    i = {k: np.asarray(v) for k, v in inputs.items()}
    W = i["L0_conv_W1"].reshape(NI, R, C, C)
    arrays = {
        "x": lay(i["x"].reshape(B, NI, R * C).transpose(2, 1, 0)),
        "L0_conv_W1": lay(i["L0_conv_W1"].reshape(NI, R * C, C).transpose(1, 0, 2)),
        "L0_conv_W2": lay(i["L0_conv_W2"].reshape(NI, R * C, C).transpose(1, 0, 2)),
        "L0_conv_b1": lay(i["L0_conv_b1"].reshape(NI, R * C).T),
        "L0_conv_b2": lay(i["L0_conv_b2"].reshape(NI, R * C).T),
        "L1_conv_W_exp": lay(i["L1_conv_W_exp"].T),
        "L1_conv_W_con": lay(i["L1_conv_W_con"].T),
        "L1_conv_b_exp": lay(i["L1_conv_b_exp"].reshape(2 * C, 1)),
        "L1_conv_b_con": lay(i["L1_conv_b_con"].reshape(C, 1)),
    }
    arrays.update({
        "L2_attn_Wq": i["L2_attn_Wq"], "L2_attn_Wk": i["L2_attn_Wk"], "L2_attn_Wv": i["L2_attn_Wv"],
        "L2_attn_Wu": i["L2_attn_Wu"], "L2_attn_Wf": i["L2_attn_Wf"],
        "pos_w": i["L2_attn_pos_w"].reshape(1, -1),
    })
    for name in ("L2_attn_bq", "L2_attn_bk", "L2_attn_bv", "L2_attn_bu", "L2_attn_bf", "L2_attn_ln_gamma",
                 "L2_attn_ln_beta"):
        arrays[name] = i[name].reshape(1, -1)
    arrays.update({
        "L2_ffn_gate_w": lay(i["L2_ffn_gate_w"].T), "L2_ffn_gate_b": i["L2_ffn_gate_b"].reshape(1, -1),
        "L2_ffn_weight1": i["L2_ffn_weight1"], "L2_ffn_weight2": i["L2_ffn_weight2"],
    })
    arrays.update({
        "L3_attn_W_qkv": lay(i["L3_attn_W_qkv"].reshape(C, H, D, 3).transpose(0, 3, 1, 2).reshape(C, 3 * C)),
        "L3_attn_b_qkv": lay(i["L3_attn_b_qkv"].reshape(H, D, 3).transpose(2, 0, 1).reshape(1, 3 * C)),
        "L3_attn_W_proj": i["L3_attn_W_proj"], "L3_attn_b_proj": i["L3_attn_b_proj"].reshape(1, -1),
        "L3_ffn_router_w": i["L3_ffn_router_w"], "L3_ffn_router_b": i["L3_ffn_router_b"].reshape(1, -1),
        "L3_ffn_expert_w": i["L3_ffn_expert_w"], "L3_ffn_expert_b": i["L3_ffn_expert_b"].reshape(1, -1),
    })
    nc = bacc.Bacc("TRN2", target_bir_lowering=False, num_devices=1)
    t = {k: nc.dram_tensor("in_" + k, a.shape, F32, kind="ExternalInput").ap() for k, a in arrays.items()}
    t["rows1"] = nc.dram_tensor("t1", (B * NI, R * C), F32, kind="Internal").ap()
    t["t1"] = t["rows1"].rearrange("n (r c) -> (n r) c", c=C)
    t["pos_ext"] = nc.dram_tensor("pos_ext", (1, t["pos_w"].shape[1] + P), F32, kind="Internal").ap()
    t["t2"] = nc.dram_tensor("t2", (B * S, C), F32, kind="Internal").ap()
    t["t3"] = nc.dram_tensor("t3", (B * S, C), F32, kind="Internal").ap()
    t["t4"] = nc.dram_tensor("out", (B * S, C), F32, kind="ExternalOutput").ap()
    positionwise_layers(nc, t)
    silu_attention_layer(nc, t)
    expert_choice_layer(nc, t)
    softmax_attention_and_router_layer(nc, t)
    r = run(nc, [{"in_" + k: a for k, a in arrays.items()}], core_ids=[0])
    return r.results[0]["out"].reshape(B, ROWS, ROWS, C)
```

```python
from contextlib import ExitStack

import concourse.bass as bass
from concourse import mybir
from concourse.alu_op_type import AluOpType as ALU

F32 = mybir.dt.float32
BF16 = mybir.dt.bfloat16
ACT = mybir.ActivationFunctionType
X = mybir.AxisListType.X

P = 128
B = 64
S = 1024
C = 32
R = P // C
NI = S // R
ROWS = 32
NC = NI // ROWS
CH = NC * B
J = S // P


def pairs(eng, lo, hi, body):
    turns = (hi - lo) // 2
    with eng.Fori(0, turns) as k:
        for u in range(2):
            body(2 * k + (lo + u), (lo + u) % 2)
    if (hi - lo) % 2:
        body(hi - 1, (hi - 1) % 2)


def positionwise_layers(nc, t):
    with ExitStack() as ctx:
        def sb(name, shape, dt=F32):
            return ctx.enter_context(nc.sbuf_tensor(name, shape, dt))

        def ps(name, shape, dt=F32):
            return ctx.enter_context(nc.psum_tensor(name, shape, dt))

        def sem(name):
            return ctx.enter_context(nc.semaphore(name))

        xt = sb("xt", [P, NI, B])
        b1 = sb("b1", [P, NI])
        b2 = sb("b2", [P, NI])
        stats = sb("stats", [P, B, 6])
        moment = sb("moment", [P, B])
        mean = sb("mean", [P, B])
        dev = sb("dev", [P, 2, B])
        var = sb("var", [P, B])
        rstd = sb("rstd", [P, B])
        minus_half = sb("minus_half", [P, B])
        ident = sb("ident", [P, P])
        share = sb("share", [P, P])
        w1 = sb("w1", [P, 2, NC, C])
        w2 = sb("w2", [P, 2, NC, C])
        xn = sb("xn", [P, 2, CH])
        xc = sb("xc", [P, 2, CH])
        pre = sb("pre", [P, 2, CH])
        hid = sb("hid", [P, 2, CH])
        res = sb("res", [P, 2, CH])
        w_main = sb("w_main", [P, P])
        w_gate = sb("w_gate", [P, P])
        w_con = sb("w_con", [P, P])
        b_main = sb("b_main", [P, 1])
        b_gate = sb("b_gate", [P, 1])
        b_gate10 = sb("b_gate10", [P, 1])
        b_con = sb("b_con", [P, 1])
        drive = sb("drive", [P, 2, CH])
        ema = sb("ema", [P, 2, CH])
        gate = sb("gate", [P, 2, CH])
        gated = sb("gated", [P, 2, CH])
        staged = sb("staged", [P, 2, P])
        rows = sb("rows", [P, 2, 2, P])

        p_hid = [ps(f"p_hid{u}", [P, CH]) for u in range(2)]
        p_out = [ps(f"p_out{u}", [P, CH]) for u in range(2)]
        p_gate = [ps(f"p_gate{u}", [P, CH]) for u in range(2)]
        p_rows = [ps(f"p_rows{u}", [P, CH]) for u in range(2)]
        p_stat = p_gate[0]
        p_main, p_con = p_hid, p_out

        loaded = sem("loaded")
        small_loaded = sem("small_loaded")
        zeroed = sem("zeroed")
        consts = sem("consts")
        w_in = [sem(f"w_in{u}") for u in range(2)]
        chain = sem("chain")
        moment_ready = sem("moment_ready")
        group_made = sem("group_made")
        var_ready = sem("var_ready")
        rstd_ready = sem("rstd_ready")
        centred0 = sem("centred0")
        centred1 = sem("centred1")
        xn_ready = sem("xn_ready")
        hid_made = sem("hid_made")
        begun = sem("begun")
        pre_ready = sem("pre_ready")
        gelu_ready = sem("gelu_ready")
        out_made = sem("out_made")
        fin_done = sem("fin_done")
        yn_ready = sem("yn_ready")
        split_made = sem("split_made")
        b10_ready = sem("b10_ready")
        drive_ready = sem("drive_ready")
        ema_ready = sem("ema_ready")
        gate_ready = sem("gate_ready")
        gated_ready = sem("gated_ready")
        con_made = sem("con_made")
        t_ready = sem("t_ready")
        staged_ready = sem("staged_ready")
        turned = sem("turned")
        rows_ready = sem("rows_ready")
        stored = [sem(f"stored{u}") for u in range(2)]
        block = ctx.enter_context(nc.Block())


        @block.sync
        def _(sp):
            sp.dma_start(xt[:, :, :], t["x"]).then_inc(loaded, 16)
            sp.dma_start(b1[:, :], t["L0_conv_b1"]).then_inc(loaded, 16)
            sp.dma_start(b2[:, :], t["L0_conv_b2"]).then_inc(loaded, 16)
            for n in range(2):
                sp.dma_start(w1[:, n], t["L0_conv_W1"][:, n * NC:(n + 1) * NC, :]).then_inc(w_in[n], 16)
                sp.dma_start(w2[:, n], t["L0_conv_W2"][:, n * NC:(n + 1) * NC, :]).then_inc(w_in[n], 16)

            def weights(n, u):
                sp.wait_ge(out_made, n - 1)
                sp.dma_start(w1[:, u], t["L0_conv_W1"][:, bass.ds(n * NC, NC), :]).then_inc(w_in[u], 16)
                sp.dma_start(w2[:, u], t["L0_conv_W2"][:, bass.ds(n * NC, NC), :]).then_inc(w_in[u], 16)

            pairs(sp, 2, ROWS, weights)

            def store(b, u):
                sp.wait_ge(rows_ready, 2 * b + 2)
                sp.dma_start(t["rows1"][bass.ds(b * NI, NI), :].rearrange("(h p) c -> p h c", h=2),
                             rows[:, u, :, :]).then_inc(stored[u], 16)

            pairs(sp, 0, B, store)
            sp.wait_ge(stored[0], 8 * B)
            sp.wait_ge(stored[1], 8 * B)

        @block.gpsimd
        def _(pool):
            pool.memset(ident[:, :], 0.0).then_inc(zeroed, 1)
            pool.memset(share[:, :], 0.0).then_inc(zeroed, 1)
            pool.memset(w_main[:, :], 0.0).then_inc(zeroed, 1)
            pool.memset(w_gate[:, :], 0.0).then_inc(zeroed, 1)
            pool.memset(w_con[:, :], 0.0).then_inc(zeroed, 1)
            pool.memset(minus_half[:, :], -0.5).then_inc(zeroed, 1)
            pool.wait_ge(zeroed, 6)
            pool.affine_select(out=ident[:, :], in_=ident[:, :], compare_op=ALU.not_equal, fill=1.0,
                               base=0, pattern=[[-1, P]], channel_multiplier=1).then_inc(consts, 1)
            for k in range(-(R - 1), R):
                pool.wait_ge(consts, k + R)
                pool.affine_select(out=share[:, :], in_=share[:, :], compare_op=ALU.not_equal,
                                   fill=0.5 / R, base=k * C, pattern=[[-1, P]],
                                   channel_multiplier=1).then_inc(consts, 1)
            for n in range(2):
                pool.wait_ge(var_ready, n + 1)
                pool.tensor_tensor(rstd[:, :], var[:, :], minus_half[:, :], ALU.pow).then_inc(rstd_ready, 1)
            pool.wait_ge(t_ready, ROWS)

            def stage(b, half):
                pool.tensor_copy(staged[:, half, :],
                                 xt[:, half * P:(half + 1) * P, bass.ds(b, 1)]).then_inc(staged_ready, 1)

            stage(0, 0)
            stage(0, 1)
            with pool.Fori(1, B) as b:
                for half in range(2):
                    pool.wait_ge(turned, 2 * b + half - 1)
                    stage(b, half)

        N_LOAD, N_SMALL = 16 * 3, 16 * 6 * R
        N_CONSTS = 2 * R

        @block.vector
        def _(dve):
            done = [0]

            def step(ins):
                done[0] += 1
                ins.then_inc(chain, 1)
                dve.wait_ge(chain, done[0])

            def statistics(n):
                with dve.Fori(0, B) as b:
                    dve.bn_stats(stats[:, bass.ds(b, 1), :],
                                 xt[:, :, bass.ds(b, 1)]).then_inc(chain, 1)
                done[0] += B
                dve.wait_ge(chain, done[0])
                even_mean, even_ss = stats[:, :, 1], stats[:, :, 2]
                odd_mean, odd_ss = stats[:, :, 4], stats[:, :, 5]
                dve.tensor_tensor(moment[:, :], even_mean, odd_mean, ALU.add).then_inc(moment_ready, 1)
                dve.wait_ge(group_made, 2 * n + 1)
                step(dve.tensor_copy(mean[:, :], p_stat[:, 0:B]))
                step(dve.tensor_tensor(dev[:, 0], even_mean, mean[:, :], ALU.subtract))
                step(dve.tensor_tensor(dev[:, 1], odd_mean, mean[:, :], ALU.subtract))
                step(dve.tensor_tensor(dev[:, :, :], dev[:, :, :], dev[:, :, :], ALU.mult))
                step(dve.tensor_tensor(dev[:, 0], dev[:, 0], dev[:, 1], ALU.add))
                step(dve.tensor_tensor(dev[:, 1], even_ss, odd_ss, ALU.add))
                dve.scalar_tensor_tensor(out=moment[:, :], in0=dev[:, 1], scalar=2.0 / NI, in1=dev[:, 0],
                                         op0=ALU.mult, op1=ALU.add).then_inc(moment_ready, 1)
                dve.wait_ge(group_made, 2 * n + 2)
                dve.tensor_scalar(var[:, :], p_stat[:, 0:B], 1e-5, None, ALU.add).then_inc(var_ready, 1)
                dve.wait_ge(rstd_ready, n + 1)

            mean_b = mean[:, :].rearrange("p (o b) -> p o b", o=1).broadcast_to([P, NC, B])
            rstd_b = rstd[:, :].rearrange("p (o b) -> p o b", o=1).broadcast_to([P, NC, B])

            def v3(ap):
                return ap.rearrange("p (i b) -> p i b", b=B)

            def row(k):
                return xt[:, bass.ds(k * NC, NC), :]

            def normalise(k, u, used, count, out_sem, before):
                if used is not None:
                    dve.wait_ge(used, count)
                dve.tensor_tensor(v3(xc[:, u, :]), row(k), mean_b, ALU.subtract).then_inc(before, 1)
                dve.wait_ge(before, k + 1)
                dve.tensor_tensor(v3(xn[:, u, :]), v3(xc[:, u, :]), rstd_b, ALU.mult).then_inc(out_sem, 1)

            dve.wait_ge(loaded, N_LOAD)
            dve.wait_ge(consts, N_CONSTS)
            statistics(0)

            def bias1(k, u):
                dve.wait_ge(hid_made, k + 1)
                dve.tensor_tensor(v3(pre[:, u, :]), v3(p_hid[u][:, :]),
                                  b1[:, bass.ds(k * NC, NC)].rearrange("p (i o) -> p i o", o=1)
                                  .broadcast_to([P, NC, B]), ALU.add).then_inc(pre_ready, 1)

            def finish(k, u):
                dve.wait_ge(out_made, k + 1)
                dve.tensor_tensor(v3(res[:, u, :]), v3(p_out[u][:, :]),
                                  b2[:, bass.ds(k * NC, NC)].rearrange("p (i o) -> p i o", o=1)
                                  .broadcast_to([P, NC, B]), ALU.add).then_inc(fin_done, 1)
                dve.wait_ge(fin_done, 2 * k + 1)
                dve.tensor_tensor(row(k), v3(res[:, u, :]), row(k), ALU.add).then_inc(fin_done, 1)

            normalise(0, 0, None, 0, xn_ready, centred0)
            normalise(1, 1, None, 0, xn_ready, centred0)
            bias1(0, 0)

            def body0(k, u):
                normalise(k, u, hid_made, k - 1, xn_ready, centred0)
                bias1(k - 1, 1 - u)
                finish(k - 2, u)

            pairs(dve, 2, ROWS, body0)
            bias1(ROWS - 1, 1)
            finish(ROWS - 2, 0)
            finish(ROWS - 1, 1)
            dve.wait_ge(fin_done, 2 * ROWS)

            dve.wait_ge(small_loaded, N_SMALL)
            statistics(1)
            dve.tensor_scalar(b_gate10[:, :], b_gate[:, :], 0.1, None, ALU.mult).then_inc(b10_ready, 1)
            step(dve.memset(ema[:, 1, :], 0.0))

            def average(k, u):
                dve.wait_ge(drive_ready, k + 1)
                dve.scalar_tensor_tensor(out=ema[:, u, :], in0=ema[:, 1 - u, :], scalar=0.9,
                                         in1=drive[:, u, :], op0=ALU.mult, op1=ALU.add).then_inc(ema_ready, 1)

            def gating(k, u):
                dve.wait_ge(gate_ready, k + 1)
                dve.wait_ge(split_made, k + 1)
                dve.scalar_tensor_tensor(out=gated[:, u, :], in0=p_main[u][:, :], scalar=b_main[:, 0:1],
                                         in1=gate[:, u, :], op0=ALU.add, op1=ALU.mult).then_inc(gated_ready, 1)

            def finish1(k, u):
                dve.wait_ge(con_made, k + 1)
                dve.scalar_tensor_tensor(out=row(k), in0=v3(p_con[u][:, :]), scalar=b_con[:, 0:1],
                                         in1=row(k), op0=ALU.add, op1=ALU.add).then_inc(t_ready, 1)

            normalise(0, 0, None, 0, yn_ready, centred1)
            normalise(1, 1, None, 0, yn_ready, centred1)
            average(0, 0)
            dve.wait_ge(ema_ready, 1)
            gating(0, 0)

            def body1(k, u):
                normalise(k, u, split_made, k - 1, yn_ready, centred1)
                dve.wait_ge(ema_ready, k - 1)
                average(k - 1, 1 - u)
                gating(k - 1, 1 - u)
                finish1(k - 2, u)

            pairs(dve, 2, ROWS, body1)
            dve.wait_ge(ema_ready, ROWS - 1)
            average(ROWS - 1, 1)
            gating(ROWS - 1, 1)
            finish1(ROWS - 2, 0)
            finish1(ROWS - 1, 1)

            def copy_rows(b, u):
                for half in range(2):
                    dve.wait_ge(turned, 2 * b + half + 1)
                    dve.tensor_copy(rows[:, u, half, :], p_rows[half][:, 0:P]).then_inc(rows_ready, 1)

            def copy_next(b, u):
                dve.wait_ge(stored[u], 8 * (b - u))
                copy_rows(b, u)

            for b in range(2):
                copy_rows(b, b)
            pairs(dve, 2, B, copy_next)

        @block.scalar
        def _(act):
            act.wait_ge(zeroed, 6)
            for r in range(R):
                q = slice(r * C, (r + 1) * C)
                act.dma_start(w_main[q, q], t["L1_conv_W_exp"][:, 0:C]).then_inc(small_loaded, 16)
                act.dma_start(w_gate[q, q], t["L1_conv_W_exp"][:, C:2 * C]).then_inc(small_loaded, 16)
                act.dma_start(w_con[q, q], t["L1_conv_W_con"]).then_inc(small_loaded, 16)
                act.dma_start(b_main[q, :], t["L1_conv_b_exp"][0:C, :]).then_inc(small_loaded, 16)
                act.dma_start(b_gate[q, :], t["L1_conv_b_exp"][C:2 * C, :]).then_inc(small_loaded, 16)
                act.dma_start(b_con[q, :], t["L1_conv_b_con"]).then_inc(small_loaded, 16)

            def gelu(k, u):
                act.wait_ge(pre_ready, k + 1)
                act.activation(hid[:, u, :], pre[:, u, :], ACT.Gelu).then_inc(gelu_ready, 1)

            def body(k, u):
                act.wait_ge(out_made, k - 1)
                gelu(k, u)

            act.preload_act_table(ACT.Gelu)
            gelu(0, 0)
            gelu(1, 1)
            pairs(act, 2, ROWS, body)
            act.preload_act_table(ACT.Sigmoid)

            def drives(k, u):
                act.wait_ge(split_made, k + 1)
                act.activation(drive[:, u, :], p_gate[u][:, :], ACT.Identity, bias=b_gate10[:, 0:1],
                               scale=0.1).then_inc(drive_ready, 1)

            def sigmoid(k, u):
                act.wait_ge(ema_ready, k + 1)
                act.activation(gate[:, u, :], ema[:, u, :], ACT.Sigmoid).then_inc(gate_ready, 1)

            def body1(k, u):
                act.wait_ge(ema_ready, k - 1)
                drives(k, u)
                act.wait_ge(gated_ready, k - 2)
                sigmoid(k - 1, 1 - u)

            act.wait_ge(b10_ready, 1)
            drives(0, 0)
            drives(1, 1)
            sigmoid(0, 0)
            act.wait_ge(ema_ready, 1)
            drives(2, 0)
            sigmoid(1, 1)
            pairs(act, 3, ROWS, body1)
            act.wait_ge(gated_ready, ROWS - 2)
            sigmoid(ROWS - 1, 1)

        @block.tensor
        def _(pe):
            def averages(n):
                for k in range(2):
                    pe.wait_ge(moment_ready, 2 * n + k + 1)
                    pe.matmul(p_stat[:, 0:B], share[:, :], moment[:, :], start=True, stop=True).then_inc(group_made, 1)

            pe.wait_ge(consts, N_CONSTS)
            averages(0)

            def products(w, dst, src):
                for i in range(NC):
                    for r in range(R):
                        q = slice(r * C, (r + 1) * C)
                        last = pe.matmul(dst[q, i * B:(i + 1) * B], w[q, i, :], src[q, i * B:(i + 1) * B],
                                         start=True, stop=True, skip_group_check=True)
                return last

            def first(k, u, at):
                pe.wait_ge(w_in[u], at)
                pe.wait_ge(xn_ready, k + 1)
                pe.sem_inc(begun, 1)
                products(w1[:, u], p_hid[u], xn[:, u, :]).then_inc(hid_made, 1)

            def second(k, u):
                pe.wait_ge(gelu_ready, k + 1)
                pe.sem_inc(begun, 1)
                products(w2[:, u], p_out[u], hid[:, u, :]).then_inc(out_made, 1)

            def body(k, u):
                pe.wait_ge(pre_ready, k - 1)
                first(k, u, 16 * (k - u) + 32)
                pe.wait_ge(fin_done, 2 * k - 4)
                second(k - 1, 1 - u)

            first(0, 0, 32)
            first(1, 1, 32)
            second(0, 0)
            pe.wait_ge(pre_ready, 1)
            first(2, 0, 64)
            second(1, 1)
            pairs(pe, 3, ROWS, body)
            pe.wait_ge(fin_done, 2 * (ROWS - 2))
            second(ROWS - 1, 1)
            averages(1)

            def split(k, u):
                pe.wait_ge(yn_ready, k + 1)
                pe.matmul(p_main[u][:, :], w_main[:, :], xn[:, u, :], start=True, stop=True)
                pe.matmul(p_gate[u][:, :], w_gate[:, :], xn[:, u, :], start=True, stop=True).then_inc(split_made, 1)

            def con(k, u):
                pe.wait_ge(gated_ready, k + 1)
                pe.matmul(p_con[u][:, :], w_con[:, :], gated[:, u, :], start=True, stop=True).then_inc(con_made, 1)

            def body1(k, u):
                pe.wait_ge(gated_ready, k - 1)
                pe.wait_ge(drive_ready, k - 1)
                split(k, u)
                pe.wait_ge(t_ready, k - 2)
                con(k - 1, 1 - u)

            pe.wait_ge(var_ready, 2)
            split(0, 0)
            split(1, 1)
            con(0, 0)
            pe.wait_ge(gated_ready, 1)
            pe.wait_ge(drive_ready, 1)
            split(2, 0)
            con(1, 1)
            pairs(pe, 3, ROWS, body1)
            pe.wait_ge(t_ready, ROWS - 2)
            con(ROWS - 1, 1)
            def turn(n, u):
                pe.wait_ge(staged_ready, n + 1)
                pe.transpose(p_rows[u][:, 0:P], staged[:, u, :], ident[:, :]).then_inc(turned, 1)

            def turn_next(n, u):
                pe.wait_ge(rows_ready, n - 1)
                turn(n, u)

            turn(0, 0)
            turn(1, 1)
            pairs(pe, 2, 2 * B, turn_next)


H = 4
D = C // H
SLOTS = 8
HALF = S // 2


def wait(eng, semaphore, value):
    if not isinstance(value, int) or value > 0:
        eng.wait_ge(semaphore, value)


def over_images(body, eng):
    body(0, 0, True, False)
    with eng.Fori(0, (B - 2) // 2) as k:
        for u in range(2):
            body(2 * k + 1 + u, (1 + u) % 2, False, False)
    body(B - 1, (B - 1) % 2, False, True)


def mid(ap, n):
    return ap.rearrange("p (j o) -> p j o", o=1).broadcast_to([ap.shape[0], ap.shape[1], n])


def normalise_tokens(dve, pool_pow, x, out, width, eps, s, chained, at):
    steps = [0]

    def step(ins):
        steps[0] += 1
        ins.then_inc(chained, 1)
        dve.wait_ge(chained, at + steps[0])

    step(dve.tensor_reduce(s["sum"][:, :], x, X, ALU.add))
    step(dve.tensor_scalar(s["sum"][:, :], s["sum"][:, :], 1.0 / width, None, ALU.mult))
    step(dve.tensor_tensor(s["centred"], x, mid(s["sum"][:, :], width), ALU.subtract))
    step(dve.tensor_tensor(s["square"], s["centred"], s["centred"], ALU.mult))
    step(dve.tensor_reduce(s["sum"][:, :], s["square"], X, ALU.add))
    pool_pow(dve.tensor_scalar(s["var"][:, :], s["sum"][:, :], 1.0 / width, eps, ALU.mult, ALU.add))
    step(dve.tensor_tensor(out, s["centred"], mid(s["rstd"][:, :], width), ALU.mult))
    return steps[0]


def silu_attention_layer(nc, t):
    with ExitStack() as ctx:
        def sb(name, shape, dt=F32):
            return ctx.enter_context(nc.sbuf_tensor("b_" + name, shape, dt))

        def ps(name, shape, dt=F32):
            return ctx.enter_context(nc.psum_tensor("b_" + name, shape, dt))

        def sem(name):
            return ctx.enter_context(nc.semaphore("b_" + name))

        QKV, U = 3 * C, 2 * C
        SQ_RING, RING = 4, 8
        ident = sb("ident", [P, P])
        ident16 = sb("ident16", [P, P], BF16)
        w_in = sb("w_in", [C + 1, QKV + U])
        w_out = sb("w_out", [U + 1, C])
        gamma = sb("gamma", [P, U])
        beta = sb("beta", [P, U])
        hankel = sb("hankel", [P, S])
        LATER = S - P
        rel = sb("rel", [P, LATER + S])
        last_col = sb("last_col", [P, 1])
        last_row = sb("last_row", [1, P])
        fold = sb("fold", [P, C])
        minus_half = sb("minus_half", [P, J])
        x_in = sb("x_in", [P, J, C])
        ln = {"sum": sb("ln_sum", [P, J]), "var": sb("ln_var", [P, J]), "rstd": sb("ln_rstd", [P, J]),
              "centred": sb("ln_centred", [P, J, C])[:, :, :], "square": sb("ln_square", [P, J, C])[:, :, :]}
        ln2 = {"sum": sb("ln2_sum", [P, J]), "var": sb("ln2_var", [P, J]), "rstd": sb("ln2_rstd", [P, J]),
               "centred": sb("ln2_centred", [P, J, U])[:, :, :], "square": sb("ln2_square", [P, J, U])[:, :, :]}
        xl = sb("xl", [P, J, C])
        base = sb("base", [P, 2, J, C])
        xlT = sb("xlT", [C + 1, S])
        qkv = sb("qkv", [P, J, QKV])
        rest = sb("rest", [P, J, 2 * C])
        parts = sb("parts", [P, J, 2, H, SLOTS, D], BF16)
        qT = sb("qT", [P, 2, 2, S], BF16)
        kT = sb("kT", [P, 2, 2, 2, S], BF16)
        v = sb("v", [P, J, C])
        v_pad = sb("v_pad", [P, 2, J, H, 32])
        posT = sb("posT", [P, S])
        u_gate = sb("u_gate", [P, 2, J, U])
        pos = sb("pos", [P, 2, J, C])
        sq = sb("sq", [P, SQ_RING, 2, HALF])
        wt = sb("wt", [P, RING, 2, HALF])
        o_sb = sb("o_sb", [P, 2, HALF])
        cat = sb("cat", [P, J, U])
        ua = sb("ua", [P, J, U])
        uaT = sb("uaT", [U + 1, S])
        result = sb("result", [P, J, C])

        p_s = [ps(f"p_s{k}", [P, 2, HALF]) for k in range(2)]
        p_o = [ps(f"p_o{k}", [P, HALF]) for k in range(2)]
        p_m = ps("p_m", [P, 2, HALF])
        p_m16 = p_m[:, :, :].rearrange("p a b -> p (a b)").bitcast(BF16).rearrange("p (a b) -> p a b", a=2)

        UNITS = [(qc, kb, g) for qc in range(2) for kb in range(4 * (qc + 1)) for g in range(2)]
        N = len(UNITS)
        assert N % RING == 0

        def span(n):
            qc, kb, _ = UNITS[n]
            q0 = max(qc * HALF, kb * P)
            return q0, (qc + 1) * HALF - q0

        MASKED = [n for n, (qc, kb, _) in enumerate(UNITS) if kb >= 4 * qc]

        const_in = sem("const_in")
        ext_in = sem("ext_in")
        hankel_in = sem("hankel_in")
        cleared = sem("cleared")
        ident_made = sem("ident_made")
        rel_made = sem("rel_made")
        x_loaded = sem("x_loaded")
        chain1, chain2, chain3 = sem("chain1"), sem("chain2"), sem("chain3")
        var_made, rstd_made = sem("var_made"), sem("rstd_made")
        var2_made, rstd2_made = sem("var2_made"), sem("rstd2_made")
        xl_made = sem("xl_made")
        base_made = sem("base_made")
        xl_turned = sem("xl_turned")
        xlT_made = sem("xlT_made")
        qkv_projected = sem("qkv_projected")
        qkv_made = sem("qkv_made")
        parts_made = sem("parts_made")
        v_made = sem("v_made")
        posT_made, posT_copied = sem("posT_made"), sem("posT_copied")
        qk_turned = sem("qk_turned")
        qk_copied = sem("qk_copied")
        upos_made = sem("upos_made")
        upos_copied = sem("upos_copied")
        scored = sem("scored")
        squared = sem("squared")
        masked = sem("masked")
        weighed = sem("weighed")
        summed = sem("summed")
        o_copied = sem("o_copied")
        o_turned = sem("o_turned")
        cat_made = sem("cat_made")
        ua_made = sem("ua_made")
        ua_turned = sem("ua_turned")
        uaT_made = sem("uaT_made")
        projected = sem("projected")
        result_made = sem("result_made")
        stored = sem("stored")
        begun = sem("begun")
        block = ctx.enter_context(nc.Block())

        src = t["t1"].rearrange("(b s) c -> b s c", b=B)
        dst = t["t2"].rearrange("(b s) c -> b s c", b=B)

        def image(ap, i):
            return ap[bass.ds(i, 1), :, :].rearrange("b (j p) c -> p (b j) c", p=P)

        N_CONST = 16 * 13
        K1 = 6 + 1

        @block.sync
        def _(sp):
            ext = t["pos_ext"]
            n_w = t["pos_w"].shape[1]
            sp.dma_start(ext[:, 0:n_w], t["pos_w"]).then_inc(ext_in, 16)
            sp.dma_start(last_col[:, :], t["pos_w"][:, n_w - 1:n_w].broadcast_to([P, 1])).then_inc(const_in, 16)
            for k, name in enumerate(("q", "k", "v")):
                sp.dma_start(w_in[0:C, k * C:(k + 1) * C], t["L2_attn_W" + name]).then_inc(const_in, 16)
                sp.dma_start(w_in[C:C + 1, k * C:(k + 1) * C], t["L2_attn_b" + name]).then_inc(const_in, 16)
            sp.dma_start(w_in[0:C, QKV:QKV + U], t["L2_attn_Wu"]).then_inc(const_in, 16)
            sp.dma_start(w_in[C:C + 1, QKV:QKV + U], t["L2_attn_bu"]).then_inc(const_in, 16)
            sp.dma_start(w_out[0:U, :], t["L2_attn_Wf"]).then_inc(const_in, 16)
            sp.dma_start(w_out[U:U + 1, :], t["L2_attn_bf"]).then_inc(const_in, 16)
            sp.dma_start(gamma[:, :], t["L2_attn_ln_gamma"].broadcast_to([P, U])).then_inc(const_in, 16)
            sp.dma_start(beta[:, :], t["L2_attn_ln_beta"].broadcast_to([P, U])).then_inc(const_in, 16)
            sp.wait_ge(rel_made, 1)
            sp.dma_start(ext[:, n_w:n_w + P], last_row[:, :]).then_inc(ext_in, 16)
            sp.wait_ge(ext_in, 32)
            sp.dma_start(hankel[:, :], bass.AP(tensor=ext.tensor, offset=ext.offset, ap=[[1, P], [1, S]])).then_inc(hankel_in, 16)

            def load(i):
                sp.dma_start(x_in[:, :, :], image(src, i)).then_inc(x_loaded, 16)

            def store(i):
                sp.wait_ge(result_made, i + 1)
                sp.dma_start(image(dst, i), result[:, :, :]).then_inc(stored, 16)

            load(0)

            def body(i, u, first, last):
                if not last:
                    sp.wait_ge(base_made, i + 1)
                    load(i + 1)
                if not first:
                    store(i - 1)

            over_images(body, sp)
            store(B - 1)
            sp.wait_ge(stored, 16 * B)

        @block.gpsimd
        def _(pool):
            pool.memset(ident[:, :], 0.0).then_inc(cleared, 1)
            pool.memset(ident16[:, :], 0.0).then_inc(cleared, 1)
            pool.memset(parts[:, :, :, :, :, :], 0.0).then_inc(cleared, 1)
            pool.memset(v_pad[:, :, :, :, :], 0.0).then_inc(cleared, 1)
            pool.memset(fold[:, :], 0.0).then_inc(cleared, 1)
            pool.memset(minus_half[:, :], -0.5).then_inc(cleared, 1)
            pool.memset(kT[:, :, :, :, :], 0.0).then_inc(cleared, 1)
            pool.wait_ge(cleared, 9)
            for m in (ident, ident16):
                pool.affine_select(out=m[:, :], in_=m[:, :], compare_op=ALU.not_equal, fill=1.0, base=0,
                                   pattern=[[-1, P]], channel_multiplier=1).then_inc(ident_made, 1)
            for k in range(R):
                pool.wait_ge(ident_made, k + 2)
                pool.affine_select(out=fold[:, :], in_=fold[:, :], compare_op=ALU.not_equal, fill=1.0, base=-k * C,
                                   pattern=[[-1, C]], channel_multiplier=1).then_inc(ident_made, 1)

            def mask(i, n):
                if n in MASKED:
                    pool.wait_ge(squared, N * i + n + 1)
                    pool.sem_inc(begun, 1)
                    diag = sq[:, n % SQ_RING, :, 0:P]
                    pool.affine_select(out=diag, in_=diag, compare_op=ALU.is_ge, fill=0.0, base=0,
                                       pattern=[[0, 2], [1, P]], channel_multiplier=-1).then_inc(masked, 1)

            def power(i):
                pool.wait_ge(var_made, i + 1)
                pool.tensor_tensor(ln["rstd"][:, :], ln["var"][:, :], minus_half[:, :], ALU.pow).then_inc(rstd_made, 1)

            def power2(i):
                pool.wait_ge(var2_made, i + 1)
                pool.tensor_tensor(ln2["rstd"][:, :], ln2["var"][:, :], minus_half[:, :], ALU.pow).then_inc(rstd2_made, 1)

            power(0)

            def body(i, u, first, last):
                for n in range(N):
                    mask(i, n)
                    if n == 6 and not first:
                        power2(i - 1)
                    if n == 3 and not last:
                        power(i + 1)

            over_images(body, pool)
            power2(B - 1)

        @block.scalar
        def _(act):
            act.preload_act_table(ACT.Silu)

            def square(i, n):
                act.wait_ge(scored, N * i + n + 1)
                wait(act, weighed, N * i + n + 1 - SQ_RING)
                m = span(n)[1]
                act.activation(sq[:, n % SQ_RING, :, 0:m], p_s[n % 2][:, :, 0:m], ACT.Square).then_inc(squared, 1)

            def weigh(i, n):
                if n in MASKED:
                    act.wait_ge(masked, len(MASKED) * i + MASKED.index(n) + 1)
                else:
                    act.wait_ge(squared, N * i + n + 1)
                wait(act, summed, N * i + n + 1 - RING)
                m = span(n)[1]
                act.activation(wt[:, n % RING, :, 0:m], sq[:, n % SQ_RING, :, 0:m], ACT.Silu,
                               scale=1.0 / D).then_inc(weighed, 1)

            def silu_qkv(i):
                act.wait_ge(qkv_projected, i + 1)
                wait(act, parts_made, i)
                wait(act, v_made, 2 * i)
                act.activation(qkv[:, :, :].rearrange("p (a j) c -> p a (j c)", a=2),
                               p_m[:, :, 0:J // 2 * QKV], ACT.Silu).then_inc(qkv_made, 1)

            silu_qkv(0)
            square(0, 0)
            square(0, 1)

            def body(i, u, first, last):
                for n in range(N):
                    if n + 2 < N:
                        square(i, n + 2)
                    elif not last:
                        square(i + 1, n + 2 - N)
                    weigh(i, n)
                    if n == 8 and not last:
                        silu_qkv(i + 1)

            over_images(body, act)

        @block.tensor
        def _(pe):
            def turn_xl(i):
                pe.wait_ge(xl_made, i + 1)
                for j in range(J):
                    ins = pe.transpose(p_m[0:C, j // 4, (j % 4) * P:(j % 4 + 1) * P], xl[:, j, :], ident[:, :])
                ins.then_inc(xl_turned, 1)

            def project_qkv(i):
                pe.wait_ge(xlT_made, i + 1)
                for j in range(J):
                    o = (j % 4) * QKV
                    ins = pe.matmul(p_m[:, j // 4, o:o + QKV], xlT[:, j * P:(j + 1) * P], w_in[:, 0:QKV],
                                    start=True, stop=True, skip_group_check=True)
                ins.then_inc(qkv_projected, 1)

            def turn_qk(i, which):
                pe.wait_ge(parts_made, i + 1)
                if which:
                    pe.wait_ge(qk_copied, 2 * i + 1)
                for g in range(2):
                    for j in range(J):
                        ins = pe.transpose(p_m16[:, g, j * P:(j + 1) * P],
                                           parts[:, j, which, 2 * g:2 * g + 2, :, :].rearrange("p h s d -> p (h s d)"),
                                           ident16[:, :])
                ins.then_inc(qk_turned, 1)

            def positions(i, half):
                pe.wait_ge(v_made, 2 * i + 1)
                pe.wait_ge(qk_copied, 2 * i + 2)
                for m in range(J):
                    g = m % 4
                    x0 = LATER + half * HALF - m * P
                    ins = pe.matmul(p_m[32 * g:32 * g + 32, half, :], v[:, m, :], rel[:, x0:x0 + HALF],
                                    start=(m < 4), stop=(m >= 4), tile_position=(0, 32 * g),
                                    skip_group_check=True)
                if half:
                    ins.then_inc(posT_made, 1)

            def project_u_and_fold(i):
                pe.wait_ge(posT_copied, i + 1)
                for j in range(J):
                    pe.matmul(p_m[:, 0, j * U:(j + 1) * U], xlT[:, j * P:(j + 1) * P], w_in[:, QKV:QKV + U],
                              start=True, stop=True, skip_group_check=True)
                for j in range(J):
                    ins = pe.matmul(p_m[:, 1, j * C:(j + 1) * C], posT[:, j * P:(j + 1) * P], fold[:, :],
                                    start=True, stop=True, skip_group_check=True)
                ins.then_inc(upos_made, 1)

            def score(i, u, n):
                qc, kb, g = UNITS[n]
                q0, m = span(n)
                if n == 0:
                    pe.wait_ge(qk_copied, 2 * i + 2)
                    pe.wait_ge(v_made, 2 * i + 2)
                wait(pe, squared, N * i + n - 1)
                for r in range(2):
                    ins = pe.matmul(p_s[n % 2][:, r, 0:m], kT[:, u, g, r, kb * P:(kb + 1) * P],
                                    qT[:, u, g, q0:q0 + m], start=True, stop=True)
                ins.then_inc(scored, 1)

            def add_up(i, u, n):
                qc, kb, _ = UNITS[n]
                q0, m = span(n)
                if kb == 0:
                    wait(pe, o_copied, 2 * i + qc - 1)
                pe.wait_ge(weighed, N * i + n + 1)
                for h in range(H):
                    ins = pe.matmul(p_o[qc][32 * h:32 * h + 32, q0 - qc * HALF:q0 - qc * HALF + m],
                                    v_pad[:, u, kb, h, :], wt[:, (n - 1 + h // 2) % RING, h % 2, 0:m],
                                    start=(kb == 0), stop=(kb == 4 * (qc + 1) - 1), tile_position=(0, 32 * h))
                ins.then_inc(summed, 2)

            def turn_o(i):
                pe.wait_ge(o_copied, 2 * i + 2)
                pe.wait_ge(upos_copied, 2 * i + 2)
                for j in range(J):
                    ins = pe.transpose(p_m[:, j // 4, (j % 4) * P:(j % 4 + 1) * P],
                                       o_sb[:, j // 4, (j % 4) * P:(j % 4 + 1) * P], ident[:, :])
                ins.then_inc(o_turned, 1)

            def turn_ua(i):
                pe.wait_ge(ua_made, i + 1)
                pe.sem_inc(begun, 1)
                for j in range(J):
                    ins = pe.transpose(p_m[0:U, j // 4, (j % 4) * P:(j % 4 + 1) * P], ua[:, j, :], ident[:, :])
                ins.then_inc(ua_turned, 1)

            def project_out(i):
                pe.wait_ge(uaT_made, i + 1)
                for j in range(J):
                    ins = pe.matmul(p_m[:, 0, j * C:(j + 1) * C], uaT[:, j * P:(j + 1) * P], w_out[:, :],
                                    start=True, stop=True, skip_group_check=True)
                ins.then_inc(projected, 1)

            pe.wait_ge(ident_made, 2 + R)
            pe.wait_ge(const_in, N_CONST)
            pe.wait_ge(rel_made, 3)
            turn_xl(0)
            project_qkv(0)
            turn_qk(0, 0)
            turn_qk(0, 1)
            positions(0, 0)
            positions(0, 1)
            project_u_and_fold(0)
            score(0, 0, 0)
            score(0, 0, 1)
            score(0, 0, 2)

            def body(i, u, first, last):
                for n in range(N):
                    if n + 3 < N:
                        score(i, u, n + 3)
                    elif not last:
                        score(i + 1, 1 - u, n + 3 - N)
                    if n == 1 and not first:
                        add_up(i - 1, 1 - u, N - 1)
                    elif n % 2 and n > 1:
                        add_up(i, u, n - 2)
                    if n == 2 and not first:
                        turn_o(i - 1)
                    if n == 5 and not last:
                        if not first:
                            pe.wait_ge(cat_made, 2 * i)
                        turn_xl(i + 1)
                    if n == 7 and not last:
                        project_qkv(i + 1)
                    if n == 9 and not first:
                        if not last:
                            pe.wait_ge(qkv_made, i + 2)
                        turn_ua(i - 1)
                    if n == 11 and not first:
                        project_out(i - 1)
                    if not last:
                        if n == 14:
                            if not first:
                                pe.wait_ge(result_made, i)
                            turn_qk(i + 1, 0)
                        if n == 16:
                            turn_qk(i + 1, 1)
                        if n == 18:
                            positions(i + 1, 0)
                        if n == 19:
                            positions(i + 1, 1)
                        if n == 21:
                            project_u_and_fold(i + 1)

            over_images(body, pe)
            add_up(B - 1, (B - 1) % 2, N - 1)
            turn_o(B - 1)
            turn_ua(B - 1)
            project_out(B - 1)

        @block.vector
        def _(dve):
            dve.memset(xlT[C:C + 1, :], 1.0).then_inc(cleared, 1)
            dve.memset(uaT[U:U + 1, :], 1.0).then_inc(cleared, 1)
            dve.wait_ge(const_in, N_CONST)
            dve.tensor_copy(last_row[:, :], last_col[0:1, 0:1].broadcast_to([1, P])).then_inc(rel_made, 1)
            dve.tensor_copy(rel[:, 0:LATER], last_col[:, 0:1].broadcast_to([P, LATER])).then_inc(rel_made, 1)
            dve.wait_ge(hankel_in, 16)
            dve.tensor_copy(rel[:, LATER:], hankel[:, ::-1]).then_inc(rel_made, 1)
            dve.wait_ge(cleared, 9)

            def normalise(i):
                dve.wait_ge(x_loaded, 16 * (i + 1))
                wait(dve, base_made, i)

                def power(ins):
                    ins.then_inc(var_made, 1)
                    dve.wait_ge(rstd_made, i + 1)

                wait(dve, xl_turned, i)
                normalise_tokens(dve, power, x_in[:, :, :], xl[:, :, :], C, 1e-5, ln, chain1, K1 * i)
                dve.sem_inc(xl_made, 1)

            def copy_xlT(i):
                dve.wait_ge(xl_turned, i + 1)
                wait(dve, upos_made, i)
                dve.tensor_copy(xlT[0:C, :], p_m[0:C, :, :].rearrange("p a b -> p (a b)")).then_inc(xlT_made, 1)

            def split(i):
                dve.wait_ge(qkv_made, i + 1)
                wait(dve, qk_turned, 2 * i)
                qk = qkv[:, :, 0:2 * C].rearrange("p j (a d) -> p j a d", d=D)
                left = rest[:, :, :].rearrange("p j (a d) -> p j a d", d=D)

                def slot(s, sides=slice(0, 2)):
                    return parts[:, :, sides, :, s, :].rearrange("p j a h d -> p j (a h) d")

                n = [0]

                def step(ins):
                    n[0] += 1
                    ins.then_inc(chain2, 1)
                    dve.wait_ge(chain2, 11 * i + n[0])

                Q, K = slice(0, 1), slice(1, 2)
                step(dve.tensor_copy(slot(0), qk))
                step(dve.tensor_tensor(left, qk, slot(0), ALU.subtract))
                step(dve.tensor_copy(slot(3), left))
                step(dve.tensor_tensor(left, left, slot(3), ALU.subtract))
                step(dve.tensor_copy(slot(5, Q), left[:, :, 0:H, :]))
                step(dve.tensor_copy(slot(4, K), left[:, :, H:2 * H, :]))
                step(dve.tensor_copy(slot(1, Q), slot(0, Q)))
                step(dve.tensor_copy(slot(4, Q), slot(0, Q)))
                step(dve.tensor_copy(slot(2, Q), slot(3, Q)))
                step(dve.tensor_copy(slot(2, K), slot(0, K)))
                step(dve.tensor_copy(slot(5, K), slot(0, K)))
                dve.tensor_copy(slot(1, K), slot(3, K)).then_inc(parts_made, 1)

            def residual(i, u):
                wait(dve, result_made, i - 1)
                dve.tensor_tensor(base[:, u, :, :], x_in[:, :, :], xl[:, :, :], ALU.add).then_inc(chain1, 1)
                dve.wait_ge(chain1, K1 * i + K1)
                dve.sem_inc(base_made, 1)

            def prepare(i, u):
                wait(dve, posT_made, i)
                dve.tensor_copy(v[:, :, :], qkv[:, :, 2 * C:3 * C]).then_inc(v_made, 1)
                wait(dve, summed, N * (i - 1))
                dve.tensor_copy(v_pad[:, u, :, :, 0:D],
                                qkv[:, :, 2 * C:3 * C].rearrange("p j (h d) -> p j h d", d=D)).then_inc(v_made, 1)
                dve.wait_ge(qk_turned, 2 * i + 1)
                dve.tensor_copy(qT[:, u, :, :], p_m16).then_inc(qk_copied, 1)
                dve.wait_ge(qk_turned, 2 * i + 2)
                dve.tensor_copy(kT[0:64, u, :, 0, :], p_m16[0:64])
                dve.tensor_copy(kT[64:P, u, :, 1, :], p_m16[64:P]).then_inc(qk_copied, 1)
                dve.wait_ge(posT_made, i + 1)
                dve.tensor_copy(posT[:, :], p_m[:, :, :].rearrange("p a b -> p (a b)")).then_inc(posT_copied, 1)
                dve.wait_ge(upos_made, i + 1)
                dve.tensor_copy(u_gate[:, u, :, :].rearrange("p j c -> p (j c)"), p_m[:, 0, :]).then_inc(upos_copied, 1)
                dve.tensor_copy(pos[:, u, :, :].rearrange("p j c -> p (j c)"), p_m[:, 1, 0:J * C]).then_inc(upos_copied, 1)

            def copy_o(i, qc):
                dve.wait_ge(summed, N * i + (8 if qc == 0 else N))
                wait(dve, o_turned, i)
                dve.tensor_copy(o_sb[:, qc, :], p_o[qc][:, :]).then_inc(o_copied, 1)

            def finish(i, u, while_pow, while_projecting):
                dve.wait_ge(o_turned, i + 1)
                wait(dve, ua_made, i)
                turned = p_m[:, :, :].rearrange("p a (j h c) -> p (a j) h c", h=H, c=32)
                dve.tensor_copy(cat[:, :, 0:C].rearrange("p j (h d) -> p j h d", d=D),
                                turned[:, :, :, 0:D]).then_inc(cat_made, 1)
                dve.tensor_copy(cat[:, :, C:U], pos[:, u, :, :]).then_inc(cat_made, 1)
                dve.wait_ge(cat_made, 2 * i + 2)

                def power(ins):
                    ins.then_inc(var2_made, 1)
                    while_pow()
                    dve.wait_ge(rstd2_made, i + 1)

                k = normalise_tokens(dve, power, cat[:, :, :], cat[:, :, :], U, 1e-3, ln2, chain3, (6 + 2) * i)
                gam = gamma[:, :].rearrange("p (o c) -> p o c", o=1).broadcast_to([P, J, U])
                bet = beta[:, :].rearrange("p (o c) -> p o c", o=1).broadcast_to([P, J, U])
                dve.tensor_tensor(cat[:, :, :], cat[:, :, :], gam, ALU.mult).then_inc(chain3, 1)
                dve.wait_ge(chain3, 8 * i + k + 1)
                dve.tensor_tensor(cat[:, :, :], cat[:, :, :], bet, ALU.add).then_inc(chain3, 1)
                dve.wait_ge(chain3, 8 * i + k + 2)
                wait(dve, ua_turned, i)
                dve.tensor_tensor(ua[:, :, :], cat[:, :, :], u_gate[:, u, :, :], ALU.mult).then_inc(ua_made, 1)
                dve.wait_ge(ua_turned, i + 1)
                wait(dve, projected, i)
                dve.tensor_copy(uaT[0:U, :], p_m[0:U, :, :].rearrange("p a b -> p (a b)")).then_inc(uaT_made, 1)
                while_projecting()
                dve.wait_ge(projected, i + 1)
                wait(dve, stored, 16 * i)
                dve.scalar_tensor_tensor(out=result[:, :, :].rearrange("p j c -> p (j c)"), in0=p_m[:, 0, 0:J * C],
                                         scalar=0.0, in1=base[:, u, :, :].rearrange("p j c -> p (j c)"),
                                         op0=ALU.max, op1=ALU.add).then_inc(result_made, 1)

            def nothing():
                pass

            normalise(0)
            copy_xlT(0)
            split(0)
            residual(0, 0)
            prepare(0, 0)

            def body(i, u, first, last):
                if not last:
                    normalise(i + 1)
                if last:
                    finish(i - 1, 1 - u, nothing, nothing)
                elif first:
                    copy_xlT(i + 1)
                    split(i + 1)
                else:
                    finish(i - 1, 1 - u, lambda: copy_xlT(i + 1), lambda: split(i + 1))
                if not last:
                    residual(i + 1, 1 - u)
                copy_o(i, 0)
                if not last:
                    prepare(i + 1, 1 - u)
                copy_o(i, 1)

            over_images(body, dve)
            finish(B - 1, (B - 1) % 2, nothing, nothing)


NE = 16
TOP = 8
GROUP = P // NE
HID = 128


def expert_choice_layer(nc, t):
    with ExitStack() as ctx:
        def sb(name, shape, dt=F32):
            return ctx.enter_context(nc.sbuf_tensor("c_" + name, shape, dt))

        def ps(name, shape, dt=F32):
            return ctx.enter_context(nc.psum_tensor("c_" + name, shape, dt))

        def sem(name):
            return ctx.enter_context(nc.semaphore("c_" + name))

        ROUNDS = B // GROUP
        GJ = GROUP * J
        ident = sb("ident", [P, P])
        gate_w = sb("gate_w", [C + 1, P + P - NE])
        w1 = sb("w1", [C + 1, NE, HID])
        w2 = sb("w2", [HID, NE, C])
        w2_bias = sb("w2_bias", [1, NE, C])
        one = sb("one", [1, GROUP])
        own = sb("own", [P, GROUP])
        minus_half = sb("minus_half", [P, GJ])
        x_in = sb("x_in", [P, 2, GJ, C])
        ln = {"sum": sb("ln_sum", [P, GJ]), "var": sb("ln_var", [P, GJ]), "rstd": sb("ln_rstd", [P, GJ]),
              "centred": sb("ln_centred", [P, GJ, C])[:, :, :], "square": sb("ln_square", [P, GJ, C])[:, :, :]}
        xl = sb("xl", [P, GJ, C])
        xlT = sb("xlT", [C + 1, 2, S])
        peak = sb("peak", [P, 1])
        expo = sb("expo", [P, S])
        total = sb("total", [P, 1])
        share = sb("share", [P, 1])
        probs = sb("probs", [P, S])
        best = sb("best", [P, TOP])
        without = sb("without", [P, S])
        picked = sb("picked", [P, S])
        pickedT = sb("pickedT", [P, J, P])
        pooled = sb("pooled", [C + 1, GROUP, NE])
        hid = sb("hid", [P, NE, GROUP])
        outT = sb("outT", [C, GROUP, NE])
        spread = sb("spread", [P, GROUP, C])
        result = sb("result", [P, GJ, C])

        p_t = ps("p_t", [P, 4, 512])
        p_l = ps("p_l", [P, 2, 512])
        p_x = ps("p_x", [P, 512])
        p_y = ps("p_y", [P, 512])

        const_in, cleared, padded, ident_made = sem("const_in"), sem("cleared"), sem("padded"), sem("ident_made")
        x_loaded = [sem(f"x_loaded{u}") for u in range(2)]
        chain, var_made, rstd_made, xl_made = (
            sem("chain"), sem("var_made"), sem("rstd_made"), sem("xl_made"))
        turned, copied, gated = sem("turned"), sem("copied"), sem("gated")
        peak_made, expo_made, picked_made = sem("peak_made"), sem("expo_made"), sem("picked_made")
        picked_turned, pickedT_made = sem("picked_turned"), sem("pickedT_made")
        pooling_done, pooled_made = sem("pooling_done"), sem("pooled_made")
        hid_summed, hid_made = sem("hid_summed"), sem("hid_made")
        out_summed, outT_made, out_turned, spread_made = (
            sem("out_summed"), sem("outT_made"), sem("out_turned"), sem("spread_made"))
        scattered, result_made, stored, begun = (
            sem("scattered"), sem("result_made"), sem("stored"), sem("begun"))
        block = ctx.enter_context(nc.Block())

        def image(ap, i):
            return ap.rearrange("(b s) c -> b s c", b=B)[bass.ds(i, 1), :, :].rearrange("b (j p) c -> p (b j) c", p=P)

        @block.sync
        def _(sp):
            sp.wait_ge(padded, 1)
            sp.dma_start(gate_w[0:C, P - NE:P], t["L2_ffn_gate_w"]).then_inc(const_in, 16)
            sp.dma_start(gate_w[C:C + 1, P - NE:P], t["L2_ffn_gate_b"]).then_inc(const_in, 16)
            sp.dma_start(w1[:, :, :], t["L2_ffn_weight1"].rearrange("e d h -> d e h")).then_inc(const_in, 16)
            w2_in = t["L2_ffn_weight2"].rearrange("e h o -> h e o")
            sp.dma_start(w2[:, :, :], w2_in[0:HID]).then_inc(const_in, 16)
            sp.dma_start(w2_bias[:, :, :], w2_in[HID:HID + 1]).then_inc(const_in, 16)

            def load(k, u):
                for b in range(GROUP):
                    sp.dma_start(x_in[:, u, b * J:(b + 1) * J, :], image(t["t2"], k * GROUP + b)).then_inc(x_loaded[u], 16)

            def store(k):
                sp.wait_ge(result_made, k + 1)
                for b in range(GROUP):
                    sp.dma_start(image(t["t3"], k * GROUP + b), result[:, b * J:(b + 1) * J, :]).then_inc(stored, 16)

            def store_and_load(k, u):
                store(k)
                load(k + 2, u)

            load(0, 0)
            load(1, 1)
            pairs(sp, 0, ROUNDS - 2, store_and_load)
            store(ROUNDS - 2)
            store(ROUNDS - 1)
            sp.wait_ge(stored, 16 * B)

        @block.gpsimd
        def _(pool):
            pool.memset(ident[:, :], 0.0).then_inc(cleared, 1)
            pool.memset(minus_half[:, :], -0.5).then_inc(cleared, 1)
            pool.memset(own[:, :], 1.0).then_inc(cleared, 1)
            pool.wait_ge(cleared, 3)
            pool.affine_select(out=ident[:, :], in_=ident[:, :], compare_op=ALU.not_equal, fill=1.0, base=0,
                               pattern=[[-1, P]], channel_multiplier=1).then_inc(ident_made, 1)
            pool.affine_select(out=own[:, :], in_=own[:, :], compare_op=ALU.is_ge, fill=0.0, base=0,
                               pattern=[[-NE, GROUP]], channel_multiplier=1).then_inc(ident_made, 1)
            pool.wait_ge(ident_made, 2)
            pool.affine_select(out=own[:, :], in_=own[:, :], compare_op=ALU.is_ge, fill=0.0, base=NE - 1,
                               pattern=[[NE, GROUP]], channel_multiplier=-1).then_inc(ident_made, 1)
            with pool.Fori(0, ROUNDS) as k:
                pool.wait_ge(var_made, k + 1)
                pool.tensor_tensor(ln["rstd"][:, :], ln["var"][:, :], minus_half[:, :], ALU.pow).then_inc(rstd_made, 1)

        @block.scalar
        def _(act):
            with act.Fori(0, ROUNDS) as k:
                act.wait_ge(peak_made, k + 1)
                act.activation(expo[:, :], p_l[:, :, :].rearrange("p a b -> p (a b)"), ACT.Exp, bias=peak[:, 0:1],
                               accum_out=total[:, 0:1]).then_inc(expo_made, 1)
                act.wait_ge(hid_summed, k + 1)
                act.activation(hid[:, :, :].rearrange("p e b -> p (e b)"), p_x[:, 0:P], ACT.Gelu).then_inc(hid_made, 1)

        @block.tensor
        def _(pe):
            def arrived(semaphore, value):
                pe.wait_ge(semaphore, value)
                pe.sem_inc(begun, 1)

            pe.wait_ge(ident_made, 3)
            pe.wait_ge(const_in, 16 * 5)
            with pe.Fori(0, ROUNDS) as k:
                arrived(xl_made, k + 1)
                for b in range(GROUP + 1):
                    if b < GROUP:
                        if b >= 2:
                            arrived(copied, GROUP * k + b - 1)
                        for j in range(J):
                            at = 2 * (b % 2) + j // 4
                            ins = pe.transpose(p_t[0:C, at, (j % 4) * P:(j % 4 + 1) * P], xl[:, b * J + j, :], ident[:, :])
                        ins.then_inc(turned, 1)
                    if b > 0:
                        c = b - 1
                        arrived(copied, GROUP * k + c + 1)
                        w = gate_w[:, P - NE - NE * c:2 * P - NE - NE * c]
                        for half in range(2):
                            ins = pe.matmul(p_l[:, half, :], w, xlT[:, c % 2, half * 512:(half + 1) * 512],
                                            start=(c == 0), stop=(c == GROUP - 1), skip_group_check=True)
                        ins.then_inc(gated, 1)
                arrived(picked_made, k + 1)
                for j in range(J):
                    ins = pe.transpose(p_t[:, j // 4, (j % 4) * P:(j % 4 + 1) * P], picked[:, j * P:(j + 1) * P], ident[:, :])
                ins.then_inc(picked_turned, 1)
                arrived(pickedT_made, k + 1)
                for b in range(GROUP):
                    for j in range(J):
                        ins = pe.matmul(p_x[0:C, b * NE:(b + 1) * NE], xl[:, b * J + j, :],
                                        pickedT[:, j, b * NE:(b + 1) * NE], start=(j == 0), stop=(j == J - 1),
                                        skip_group_check=True)
                ins.then_inc(pooling_done, 1)
                arrived(pooled_made, k + 1)
                for e in range(NE):
                    ins = pe.matmul(p_x[:, e * GROUP:(e + 1) * GROUP], w1[:, e, :], pooled[:, :, e],
                                    start=True, stop=True, skip_group_check=True)
                ins.then_inc(hid_summed, 1)
                arrived(hid_made, k + 1)
                for e in range(NE):
                    at = p_y[0:C, e * GROUP:(e + 1) * GROUP]
                    pe.matmul(at, w2[:, e, :], hid[:, e, :], start=True, stop=False, skip_group_check=True)
                    ins = pe.matmul(at, w2_bias[:, e, :], one[:, :], start=False, stop=True, skip_group_check=True)
                ins.then_inc(out_summed, 1)
                arrived(outT_made, k + 1)
                pe.transpose(p_x[:, 0:C], outT[:, :, :].rearrange("o b e -> o (b e)"), ident[0:C, 0:C]).then_inc(out_turned, 1)
                arrived(spread_made, k + 1)
                for j in range(J):
                    ins = pe.matmul(p_t[:, j // 2, (j % 2) * 256:(j % 2 + 1) * 256], picked[:, j * P:(j + 1) * P],
                                    spread[:, :, :].rearrange("p b c -> p (b c)"), start=True, stop=True,
                                    skip_group_check=True)
                ins.then_inc(scattered, 1)

        @block.vector
        def _(dve):
            dve.memset(gate_w[:, :], 0.0).then_inc(chain, 1)
            dve.memset(xlT[C:C + 1, :, :], 1.0).then_inc(chain, 1)
            dve.memset(pooled[C:C + 1, :, :], 1.0).then_inc(chain, 1)
            dve.memset(one[:, :], 1.0).then_inc(chain, 1)
            dve.wait_ge(chain, 4)
            dve.sem_inc(padded, 1)
            dve.wait_ge(ident_made, 3)
            M = 6 + 4 + GROUP

            def body(k, u):
                dve.wait_ge(x_loaded[u], 8 * GROUP * (k - u) + 16 * GROUP)

                def power(ins):
                    ins.then_inc(var_made, 1)
                    dve.wait_ge(rstd_made, k + 1)

                n = [normalise_tokens(dve, power, x_in[:, u, :, :], xl[:, :, :], C, 1e-5, ln, chain, M * k + 4)]
                dve.sem_inc(xl_made, 1)

                def step(ins):
                    n[0] += 1
                    ins.then_inc(chain, 1)
                    dve.wait_ge(chain, M * k + 4 + n[0])

                for b in range(GROUP):
                    dve.wait_ge(turned, GROUP * k + b + 1)
                    if b >= 2:
                        dve.wait_ge(gated, GROUP * k + b - 1)
                    dve.tensor_copy(xlT[0:C, b % 2, :], p_t[0:C, 2 * (b % 2):2 * (b % 2) + 2, :]
                                    .rearrange("p a b -> p (a b)")).then_inc(copied, 1)
                dve.wait_ge(gated, GROUP * (k + 1))
                logits = p_l[:, :, :].rearrange("p a b -> p (a b)")
                dve.tensor_reduce(peak[:, :], logits, X, ALU.max, negate=True).then_inc(peak_made, 1)
                dve.wait_ge(expo_made, k + 1)
                step(dve.reciprocal(share[:, :], total[:, :]))
                step(dve.tensor_scalar(probs[:, :], expo[:, :], share[:, 0:1], None, ALU.mult))
                dve.sem_inc(begun, 1)
                step(dve.max(best[:, :], probs[:, :]))
                dve.sem_inc(begun, 1)
                step(dve.match_replace(out=without[:, :], in_to_replace=best[:, :], in_values=probs[:, :], imm_value=-1.0))
                dve.scalar_tensor_tensor(out=picked[:, :], in0=without[:, :], scalar=0.0, in1=probs[:, :],
                                         op0=ALU.is_lt, op1=ALU.mult).then_inc(picked_made, 1)
                dve.wait_ge(picked_turned, k + 1)
                dve.tensor_copy(pickedT[:, :, :].rearrange("p j q -> p (j q)"),
                                p_t[:, 0:2, :].rearrange("p a b -> p (a b)")).then_inc(pickedT_made, 1)
                dve.wait_ge(pooling_done, k + 1)
                dve.tensor_copy(pooled[0:C, :, :].rearrange("p b e -> p (b e)"), p_x[0:C, 0:P]).then_inc(pooled_made, 1)
                dve.wait_ge(out_summed, k + 1)
                dve.tensor_copy(outT[:, :, :], p_y[0:C, 0:P].rearrange("o (e b) -> o b e", b=GROUP)).then_inc(outT_made, 1)
                dve.wait_ge(out_turned, k + 1)
                dve.tensor_tensor(spread[:, :, :], p_x[:, 0:C].rearrange("p (o c) -> p o c", o=1).broadcast_to([P, GROUP, C]),
                                  mid(own[:, :], C), ALU.mult).then_inc(spread_made, 1)
                dve.wait_ge(scattered, k + 1)
                wait(dve, stored, 16 * GROUP * k)
                for b in range(GROUP):
                    at = p_t[:, :, :].rearrange("p a (j b c) -> p (a j) b c", j=2, b=GROUP)[:, :, b, :]
                    dve.tensor_tensor(result[:, b * J:(b + 1) * J, :], at, x_in[:, u, b * J:(b + 1) * J, :],
                                      ALU.add).then_inc(chain, 1)
                n[0] += GROUP
                assert n[0] == M
                dve.wait_ge(chain, M * (k + 1) + 4)
                dve.sem_inc(result_made, 1)

            pairs(dve, 0, ROUNDS, body)


ER = 8


def softmax_attention_and_router_layer(nc, t):
    with ExitStack() as ctx:
        def sb(name, shape, dt=F32):
            return ctx.enter_context(nc.sbuf_tensor("d_" + name, shape, dt))

        def ps(name, shape, dt=F32):
            return ctx.enter_context(nc.psum_tensor("d_" + name, shape, dt))

        def sem(name):
            return ctx.enter_context(nc.semaphore("d_" + name))

        QKV = 3 * C
        SCALE = float(C) ** -0.5
        RING = 8
        SHIFT = 6
        ident = sb("ident", [P, P])
        ident16 = sb("ident16", [P, P], BF16)
        w_in = sb("w_in", [C + 1, QKV])
        w_out = sb("w_out", [C + 1, C])
        w_router = sb("w_router", [C + 1, ER])
        w_expert = sb("w_expert", [C + 1, ER * C])
        earlier = sb("earlier", [P, ER, ER])
        minus_half = sb("minus_half", [P, J])
        x_in = sb("x_in", [P, J, C])
        ln = {"sum": sb("ln_sum", [P, J]), "var": sb("ln_var", [P, J]), "rstd": sb("ln_rstd", [P, J]),
              "centred": sb("ln_centred", [P, J, C])[:, :, :], "square": sb("ln_square", [P, J, C])[:, :, :]}
        ln2 = {"sum": sb("ln2_sum", [P, J]), "var": sb("ln2_var", [P, J]), "rstd": sb("ln2_rstd", [P, J]),
               "centred": sb("ln2_centred", [P, J, C])[:, :, :], "square": sb("ln2_square", [P, J, C])[:, :, :]}
        xl = sb("xl", [P, J, C])
        x_keep = sb("x_keep", [P, 2, J, C])
        xlT = sb("xlT", [C + 1, S])
        qkv = sb("qkv", [P, J, QKV])
        rest = sb("rest", [P, J, 2 * C])
        parts = sb("parts", [P, 2, J, 2, H, SLOTS, D], BF16)
        qT = sb("qT", [P, 2, 2, S], BF16)
        kT = sb("kT", [P, 2, 2, 2, S], BF16)
        v_pad = sb("v_pad", [P, 2, J, H, 32])
        peaks = sb("peaks", [P, J * H, 2])
        shift = sb("shift", [P, J * H])
        wt = sb("wt", [P, RING, HALF])
        o_sb = sb("o_sb", [P, 2, HALF])
        share = sb("share", [P, J * H])
        att = sb("att", [P, J, C])
        attT = sb("attT", [C + 1, S])
        x4 = sb("x4", [P, J, C])
        xl4 = sb("xl4", [P, J, C])
        xl4T = sb("xl4T", [C + 1, S])
        col = sb("col", [P, J])
        expo = sb("expo", [P, J, ER])
        prob = sb("prob", [P, J, ER])
        above = sb("above", [P, J, ER, ER])
        equal = sb("equal", [P, J, ER, ER])
        rank = sb("rank", [P, J, ER])
        mix = sb("mix", [P, J, ER])
        scaled = sb("scaled", [P, 4, ER, C])
        mixed = sb("mixed", [P, 4, C])
        result = sb("result", [P, J, C])

        BANKS = 3
        p_s = [ps(f"p_s{k}", [P, HALF]) for k in range(BANKS)]
        p_k = [ps(f"p_k{k}", [P, HALF]) for k in range(2)]
        p_o = ps("p_o", [P, HALF])
        p_m = ps("p_m", [P, 2, HALF])
        p_m16 = p_m[:, :, :].rearrange("p a b -> p (a b)").bitcast(BF16).rearrange("p (a b) -> p a b", a=2)

        UNITS = [(qc, kb, h) for qc in range(2) for kb in range(J) for h in range(H)]
        N = len(UNITS)
        assert N % RING == 0 and N % BANKS == 1
        BANK = [n % BANKS for n in range(N - 1)] + [1]
        BEFORE = [max(k for k in range(-N, n) if BANK[k % N] == BANK[n]) for n in range(N)]
        PEAKS = [(j, h, half) for j in range(J) for h in range(H) for half in range(2)]
        NP = len(PEAKS)
        AHEAD = 44
        OWN_AT = {3: 2, 4: 1, 5: 2, 6: 1, 7: 2, 13: 2, 14: 2, 15: 2, 16: 2, 17: 2, 18: 2}
        NEXT_AT = {23: 2, 24: 1, 25: 2, 26: 1, 30: 2, 31: 1, 32: 2, 33: 1, 34: 2, 35: 1, 44: 1, 48: 2, 49: 2, 50: 2,
                   51: 2, 52: 2, 53: 2, 54: 2, 55: 2, 58: 2, 59: 2, 60: 2, 61: 2, 62: 2, 63: 2}
        assert sum(OWN_AT.values()) == NP - AHEAD and sum(NEXT_AT.values()) == AHEAD

        const_in, cleared, ident_made = sem("const_in"), sem("cleared"), sem("ident_made")
        x_loaded = sem("x_loaded")
        chain1, chain2, chain3, chain4 = sem("chain1"), sem("chain2"), sem("chain3"), sem("chain4")
        var_made, rstd_made = sem("var_made"), sem("rstd_made")
        var2_made, rstd2_made = sem("var2_made"), sem("rstd2_made")
        xl_made = sem("xl_made")
        x_kept = [sem(f"x_kept{u}") for u in range(2)]
        xl_turned = sem("xl_turned")
        xlT_made = sem("xlT_made")
        qkv_projected = sem("qkv_projected")
        qkv_made = sem("qkv_made")
        parts_made = sem("parts_made")
        PARTS = 6 + 1
        v_pad_made = sem("v_pad_made")
        split_made = sem("split_made")
        K_, Q_, LOW, HIGH = range(4)
        kq_turned, kq_copied = sem("kq_turned"), sem("kq_copied")
        shifted_turned, shifted_copied = sem("shifted_turned"), sem("shifted_copied")
        peak_scored = sem("peak_scored")
        peak_read = sem("peak_read")
        shift_made = sem("shift_made")
        chain5 = sem("chain5")
        scored = sem("scored")
        weighed = sem("weighed")
        summed = sem("summed")
        o_copied = sem("o_copied")
        o_turned = sem("o_turned")
        att_made = sem("att_made")
        att_turned = sem("att_turned")
        attT_made = sem("attT_made")
        projected = sem("projected")
        xl4_made = sem("xl4_made")
        xl4_turned = sem("xl4_turned")
        xl4T_made = sem("xl4T_made")
        routed = sem("routed")
        logits_read = sem("logits_read")
        expo_made = sem("expo_made")
        experts_made = sem("experts_made")
        experts_read = sem("experts_read")
        result_made = sem("result_made")
        stored = sem("stored")
        begun = sem("begun")
        block = ctx.enter_context(nc.Block())

        src = t["t3"].rearrange("(b s) c -> b s c", b=B)
        dst = t["t4"].rearrange("(b s) c -> b s c", b=B)

        def image(ap, i):
            return ap[bass.ds(i, 1), :, :].rearrange("b (j p) c -> p (b j) c", p=P)

        @block.sync
        def _(sp):
            sp.dma_start(w_in[0:C, :], t["L3_attn_W_qkv"]).then_inc(const_in, 16)
            sp.dma_start(w_in[C:C + 1, :], t["L3_attn_b_qkv"]).then_inc(const_in, 16)
            sp.dma_start(w_out[0:C, :], t["L3_attn_W_proj"]).then_inc(const_in, 16)
            sp.dma_start(w_out[C:C + 1, :], t["L3_attn_b_proj"]).then_inc(const_in, 16)
            sp.dma_start(w_router[0:C, :], t["L3_ffn_router_w"]).then_inc(const_in, 16)
            sp.dma_start(w_router[C:C + 1, :], t["L3_ffn_router_b"]).then_inc(const_in, 16)
            sp.dma_start(w_expert[0:C, :].rearrange("d (e c) -> d e c", e=ER),
                         t["L3_ffn_expert_w"].rearrange("e d c -> d e c")).then_inc(const_in, 16)
            sp.dma_start(w_expert[C:C + 1, :], t["L3_ffn_expert_b"]).then_inc(const_in, 16)

            def load(i):
                sp.dma_start(x_in[:, :, :], image(src, i)).then_inc(x_loaded, 16)

            def keep(i, u):
                sp.dma_start(x_keep[:, u, :, :], image(src, i)).then_inc(x_kept[u], 16)

            def store(i):
                sp.wait_ge(result_made, 2 * i + 2)
                sp.dma_start(image(dst, i), result[:, :, :]).then_inc(stored, 16)

            load(0)

            def body(i, u, first, last):
                if not last:
                    sp.wait_ge(xl_made, i + 1)
                    load(i + 1)
                if not first:
                    wait(sp, xl4_made, i - 1)
                keep(i, u)
                if not first:
                    store(i - 1)

            over_images(body, sp)
            store(B - 1)
            sp.wait_ge(stored, 16 * B)

        @block.gpsimd
        def _(pool):
            pool.memset(ident[:, :], 0.0).then_inc(cleared, 1)
            pool.memset(ident16[:, :], 0.0).then_inc(cleared, 1)
            pool.memset(earlier[:, :, :], 1.0).then_inc(cleared, 1)
            pool.memset(parts[:, :, :, :, :, :, :], 0.0).then_inc(cleared, 1)
            pool.memset(v_pad[:, :, :, :, :], 0.0).then_inc(cleared, 1)
            pool.memset(minus_half[:, :], -0.5).then_inc(cleared, 1)
            pool.memset(kT[:, :, :, :, :], 0.0).then_inc(cleared, 1)
            pool.wait_ge(cleared, 7)
            for m in (ident, ident16):
                pool.affine_select(out=m[:, :], in_=m[:, :], compare_op=ALU.not_equal, fill=1.0, base=0,
                                   pattern=[[-1, P]], channel_multiplier=1).then_inc(ident_made, 1)
            pool.affine_select(out=earlier[:, :, :], in_=earlier[:, :, :], compare_op=ALU.is_gt, fill=0.0, base=0,
                               pattern=[[1, ER], [-1, ER]], channel_multiplier=0).then_inc(ident_made, 1)
            for u in range(2):
                pool.memset(parts[:, u, :, 1, :, SHIFT, 0:3], 1.0).then_inc(ident_made, 1)
            pool.memset(v_pad[:, :, :, :, D:D + 1], 1.0).then_inc(ident_made, 1)

            def power(i):
                pool.wait_ge(var_made, i + 1)
                pool.tensor_tensor(ln["rstd"][:, :], ln["var"][:, :], minus_half[:, :], ALU.pow).then_inc(rstd_made, 1)

            def power2(i):
                pool.wait_ge(var2_made, i + 1)
                pool.tensor_tensor(ln2["rstd"][:, :], ln2["var"][:, :], minus_half[:, :], ALU.pow).then_inc(rstd2_made, 1)

            def spread_parts(i, u):
                def slot(s, side):
                    return parts[:, u, :, side, :, s, :]

                Q, K = 0, 1
                pool.wait_ge(qkv_made, i + 1)
                wait(pool, summed, N * (i - 1))
                pool.sem_inc(begun, 1)
                pool.tensor_copy(v_pad[:, u, :, :, 0:D],
                                 qkv[:, :, 2 * C:3 * C].rearrange("p j (h d) -> p j h d", d=D)).then_inc(v_pad_made, 1)
                pool.wait_ge(split_made, 2 * i + 1)
                pool.sem_inc(begun, 1)
                pool.tensor_copy(slot(1, Q), slot(0, Q)).then_inc(parts_made, 1)
                pool.tensor_copy(slot(4, Q), slot(0, Q)).then_inc(parts_made, 1)
                pool.tensor_copy(slot(2, K), slot(0, K)).then_inc(parts_made, 1)
                pool.tensor_copy(slot(5, K), slot(0, K)).then_inc(parts_made, 1)
                pool.wait_ge(split_made, 2 * i + 2)
                pool.sem_inc(begun, 1)
                pool.tensor_copy(slot(2, Q), slot(3, Q)).then_inc(parts_made, 1)
                pool.tensor_copy(slot(1, K), slot(3, K)).then_inc(parts_made, 1)

            power(0)
            spread_parts(0, 0)

            def body(i, u, first, last):
                if not last:
                    power(i + 1)
                    spread_parts(i + 1, 1 - u)
                if not first:
                    power2(i - 1)

            over_images(body, pool)
            power2(B - 1)

        @block.scalar
        def _(act):
            act.preload_act_table(ACT.Exp)

            def weigh(i, n):
                act.wait_ge(scored, N * i + n + 1)
                wait(act, summed, N * i + n + 1 - RING)
                act.activation(wt[:, n % RING, :], p_s[BANK[n]][:, :], ACT.Exp, scale=SCALE).then_inc(weighed, 1)

            def copy_o(i, qc):
                act.wait_ge(summed, N * i + (N // 2) * (qc + 1))
                wait(act, o_turned, i)
                act.activation(o_sb[:, qc, :], p_o[:, :], ACT.Copy).then_inc(o_copied, 1)

            def copy_xlT(i):
                act.wait_ge(xl_turned, i + 1)
                wait(act, qkv_projected, i)
                act.activation(xlT[0:C, :], p_m[0:C, :, :].rearrange("p a b -> p (a b)"), ACT.Copy).then_inc(xlT_made, 1)

            def copy_qkv(i):
                act.wait_ge(qkv_projected, i + 1)
                wait(act, parts_made, PARTS * i)
                wait(act, v_pad_made, i)
                act.activation(qkv[:, :, :].rearrange("p (a j) c -> p a (j c)", a=2),
                               p_m[:, :, 0:J // 2 * QKV], ACT.Copy).then_inc(qkv_made, 1)

            def copy_k(i, u, g, r):
                if (g, r) == (0, 0):
                    act.wait_ge(kq_turned, 2 * i + 1)
                    wait(act, scored, N * (i - 1))
                rows = slice(64 * r, 64 * r + 64)
                ins = act.activation(kT[rows, u, g, r, :], p_m16[rows, g, :], ACT.Copy)
                if (g, r) == (1, 1):
                    ins.then_inc(kq_copied, 1)

            def copy_q(i, u, g):
                if g == 0:
                    act.wait_ge(kq_turned, 2 * i + 2)
                ins = act.activation(qT[:, u, g, :], p_m16[:, g, :], ACT.Copy)
                if g == 1:
                    ins.then_inc(kq_copied, 1)

            def copy_shifted(i, u, k):
                act.wait_ge(shifted_turned, 2 * i + 1 + k - LOW)
                qs = slice((k - LOW) * HALF, (k - LOW + 1) * HALF)
                act.activation(qT[:, u, :, qs], p_m16[:, :, qs], ACT.Copy).then_inc(shifted_copied, 1)

            def exp_router(i):
                act.wait_ge(logits_read, i + 1)
                act.activation(expo[:, :, :], expo[:, :, :], ACT.Exp).then_inc(expo_made, 1)

            def turned_copy(i, made, out, out_semaphore):
                act.wait_ge(made, i + 1)
                act.activation(out[0:C, :], p_m[0:C, :, :].rearrange("p a b -> p (a b)"), ACT.Copy).then_inc(out_semaphore, 1)

            copy_xlT(0)
            copy_qkv(0)
            for g in range(2):
                for r in range(2):
                    copy_k(0, 0, g, r)
            for g in range(2):
                copy_q(0, 0, g)
            copy_shifted(0, 0, LOW)

            def body(i, u, first, last):
                for n in range(N):
                    weigh(i, n)
                    if n == 33:
                        copy_o(i, 0)
                    if n == 24:
                        copy_shifted(i, u, HIGH)
                    if not first:
                        if n == 1:
                            copy_o(i - 1, 1)
                        if n == 13:
                            turned_copy(i - 1, att_turned, attT, attT_made)
                        if n == 33:
                            turned_copy(i - 1, xl4_turned, xl4T, xl4T_made)
                        if n == 35:
                            exp_router(i - 1)
                    if not last:
                        if n == 6:
                            copy_xlT(i + 1)
                        if n == 8:
                            copy_qkv(i + 1)
                        if n in (16, 17, 18, 19):
                            copy_k(i + 1, 1 - u, (n - 16) // 2, n % 2)
                        if n in (21, 22):
                            copy_q(i + 1, 1 - u, n - 21)
                        if n == 59:
                            copy_shifted(i + 1, 1 - u, LOW)

            over_images(body, act)
            copy_o(B - 1, 1)
            turned_copy(B - 1, att_turned, attT, attT_made)
            turned_copy(B - 1, xl4_turned, xl4T, xl4T_made)
            exp_router(B - 1)

        @block.tensor
        def _(pe):
            def arrived(semaphore, value):
                wait(pe, semaphore, value)
                pe.sem_inc(begun, 1)

            def turn(i, made, x, done):
                arrived(made, i + 1)
                for j in range(J):
                    ins = pe.transpose(p_m[0:C, j // 4, (j % 4) * P:(j % 4 + 1) * P], x[:, j, :], ident[:, :])
                ins.then_inc(done, 1)

            def project(i, made, xT, w, width, done, half=False):
                arrived(made, i + 1)
                for j in range(J):
                    at = p_m[:, 0, j * width:(j + 1) * width] if half else \
                        p_m[:, j // 4, (j % 4) * width:(j % 4 + 1) * width]
                    ins = pe.matmul(at, xT[:, j * P:(j + 1) * P], w[:, :], start=True, stop=True,
                                    skip_group_check=True)
                ins.then_inc(done, 1)

            def turn_xl(i):
                wait(pe, shifted_copied, 2 * i - 1)
                turn(i, xl_made, xl, xl_turned)

            def turn_parts(i, u, k, next_q=None):
                if k == K_:
                    arrived(parts_made, PARTS * (i + 1))
                    wait(pe, attT_made, i - 1)
                elif k == Q_:
                    arrived(kq_copied, 2 * i + 1)
                elif k == LOW:
                    arrived(shift_made, 2 * i + 1)
                    wait(pe, experts_read, 2 * (i - 1))
                else:
                    arrived(shift_made, 2 * i + 2)
                    if next_q is not None:
                        pe.wait_ge(kq_copied, 2 * next_q)
                js = range(J // 2) if k == LOW else range(J // 2, J) if k == HIGH else range(J)
                for g in range(2):
                    for j in js:
                        ins = pe.transpose(p_m16[:, g, j * P:(j + 1) * P],
                                           parts[:, u, j, int(k == K_), 2 * g:2 * g + 2, :, :].rearrange("p h s d -> p (h s d)"),
                                           ident16[:, :])
                ins.then_inc(kq_turned if k in (K_, Q_) else shifted_turned, 1)

            def peak(i, u, m):
                j, h, half = PEAKS[m]
                g, r = h // 2, h % 2
                if m == 0:
                    arrived(kq_copied, 2 * i + 2)
                wait(pe, peak_read, NP * i + m - 1)
                pe.matmul(p_k[m % 2][:, :], qT[:, u, g, j * P:(j + 1) * P],
                          kT[:, u, g, r, half * HALF:(half + 1) * HALF], start=True, stop=True).then_inc(peak_scored, 1)

            def score(i, u, n):
                qc, kb, h = UNITS[n]
                if n == 0:
                    pe.wait_ge(shifted_copied, 2 * i + 1)
                if n == N // 2:
                    pe.wait_ge(shifted_copied, 2 * i + 2)
                wait(pe, weighed, N * i + BEFORE[n] + 1)
                pe.matmul(p_s[BANK[n]][:, :], kT[:, u, h // 2, h % 2, kb * P:(kb + 1) * P],
                          qT[:, u, h // 2, qc * HALF:(qc + 1) * HALF], start=True, stop=True).then_inc(scored, 1)

            def add_up(i, u, n):
                qc, kb, _ = UNITS[n]
                if kb == 0:
                    wait(pe, o_copied, 2 * i + qc)
                    if qc == 0:
                        pe.wait_ge(v_pad_made, i + 1)
                pe.wait_ge(weighed, N * i + n + 1)
                for h in range(H):
                    ins = pe.matmul(p_o[32 * h:32 * h + 32, :], v_pad[:, u, kb, h, :],
                                    wt[:, (n + 1 - H + h) % RING, :],
                                    start=(kb == 0), stop=(kb == J - 1), tile_position=(0, 32 * h))
                ins.then_inc(summed, H)

            def turn_o(i, next_qkv):
                pe.wait_ge(o_copied, 2 * i + 2)
                pe.wait_ge(qkv_made, next_qkv)
                for j in range(J):
                    ins = pe.transpose(p_m[:, j // 4, (j % 4) * P:(j % 4 + 1) * P],
                                       o_sb[:, j // 4, (j % 4) * P:(j % 4 + 1) * P], ident[:, :])
                ins.then_inc(o_turned, 1)

            def experts(i, half):
                if half:
                    arrived(experts_read, 2 * i + 1)
                else:
                    arrived(logits_read, i + 1)
                for j in range(J // 2):
                    tok = (half * J // 2 + j) * P
                    ins = pe.matmul(p_m[:, j // 2, (j % 2) * 256:(j % 2 + 1) * 256], xl4T[:, tok:tok + P],
                                    w_expert[:, :], start=True, stop=True, skip_group_check=True)
                ins.then_inc(experts_made, 1)

            def finish_turn_att(i):
                turn(i, att_made, att, att_turned)

            def finish_project(i):
                project(i, attT_made, attT, w_out, C, projected, half=True)

            def finish_turn_x(i):
                turn(i, xl4_made, xl4, xl4_turned)

            def finish_route(i):
                project(i, xl4T_made, xl4T, w_router, ER, routed, half=True)

            pe.wait_ge(ident_made, 6)
            pe.wait_ge(const_in, 16 * 8)
            turn_xl(0)
            project(0, xlT_made, xlT, w_in, QKV, qkv_projected)
            pe.wait_ge(qkv_made, 1)
            turn_parts(0, 0, K_)
            turn_parts(0, 0, Q_)
            for m in range(NP // 2):
                peak(0, 0, m)
            turn_parts(0, 0, LOW)
            for m in range(NP // 2, AHEAD):
                peak(0, 0, m)
            for n in range(BANKS):
                score(0, 0, n)

            def body(i, u, first, last):
                done = {"own": AHEAD, "next": 0}

                def peaks_of(n, lo, hi):
                    for _ in range(lo, min(hi, OWN_AT.get(n, 0))):
                        peak(i, u, done["own"])
                        done["own"] += 1
                    for _ in range(lo, 0 if last else min(hi, NEXT_AT.get(n, 0))):
                        peak(i + 1, 1 - u, done["next"])
                        done["next"] += 1

                for n in range(N):
                    peaks_of(n, 0, 1)
                    if n + BANKS < N:
                        score(i, u, n + BANKS)
                    elif not last:
                        score(i + 1, 1 - u, n + BANKS - N)
                    if n % H == H - 1:
                        add_up(i, u, n)
                    peaks_of(n, 1, 2)
                    if n == 23:
                        turn_parts(i, u, HIGH, None if last else i + 2)
                    if not last:
                        if n == 5:
                            turn_xl(i + 1)
                        if n == 7:
                            project(i + 1, xlT_made, xlT, w_in, QKV, qkv_projected)
                        if n == 15:
                            turn_parts(i + 1, 1 - u, K_)
                        if n == 20:
                            turn_parts(i + 1, 1 - u, Q_)
                        if n == 58:
                            turn_parts(i + 1, 1 - u, LOW)
                    if not first:
                        if n == 9:
                            turn_o(i - 1, i + 1 if last else i + 2)
                        if n == 12:
                            finish_turn_att(i - 1)
                        if n == 26:
                            pe.wait_ge(shifted_copied, 2 * i + 2)
                            finish_project(i - 1)
                        if n == 32:
                            finish_turn_x(i - 1)
                        if n == 34:
                            finish_route(i - 1)
                        if n == 37:
                            experts(i - 1, 0)
                        if n == 44:
                            experts(i - 1, 1)

            over_images(body, pe)
            i = B - 1
            pe.wait_ge(experts_read, 2 * i)
            turn_o(i, B)
            finish_turn_att(i)
            finish_project(i)
            finish_turn_x(i)
            finish_route(i)
            experts(i, 0)
            experts(i, 1)

        @block.vector
        def _(dve):
            dve.memset(xlT[C:C + 1, :], 1.0).then_inc(chain4, 1)
            dve.memset(attT[C:C + 1, :], 1.0).then_inc(chain4, 1)
            dve.memset(xl4T[C:C + 1, :], 1.0).then_inc(chain4, 1)
            dve.wait_ge(chain4, 3)
            dve.wait_ge(ident_made, 6)

            def normalise(i, meanwhile):
                dve.wait_ge(x_loaded, 16 * (i + 1))
                wait(dve, xl_turned, i)

                def power(ins):
                    ins.then_inc(var_made, 1)
                    meanwhile()
                    dve.wait_ge(rstd_made, i + 1)

                normalise_tokens(dve, power, x_in[:, :, :], xl[:, :, :], C, 1e-5, ln, chain1, 6 * i)
                dve.sem_inc(xl_made, 1)

            def split(i, u):
                dve.wait_ge(qkv_made, i + 1)
                wait(dve, shifted_turned, 2 * i - 2)
                qk = qkv[:, :, 0:2 * C].rearrange("p j (a d) -> p j a d", d=D)
                left = rest[:, :, :].rearrange("p j (a d) -> p j a d", d=D)

                def slot(s):
                    return parts[:, u, :, :, :, s, :].rearrange("p j a h d -> p j (a h) d")

                dve.memset(parts[:, u, :, 0, :, SHIFT, 0:3], 0.0).then_inc(chain2, 1)
                dve.tensor_copy(slot(0), qk).then_inc(split_made, 1)
                dve.wait_ge(split_made, 2 * i + 1)
                dve.tensor_tensor(left, qk, slot(0), ALU.subtract).then_inc(chain2, 1)
                dve.wait_ge(chain2, 5 * i + 2)
                dve.tensor_copy(slot(3), left).then_inc(split_made, 1)
                dve.wait_ge(split_made, 2 * i + 2)
                dve.tensor_tensor(left, left, slot(3), ALU.subtract).then_inc(chain2, 1)
                dve.wait_ge(chain2, 5 * i + 3)
                dve.tensor_copy(parts[:, u, :, 0, :, 5, :], left[:, :, 0:H, :]).then_inc(chain2, 1)
                dve.tensor_copy(parts[:, u, :, 1, :, 4, :], left[:, :, H:2 * H, :]).then_inc(chain2, 1)
                dve.wait_ge(chain2, 5 * i + 5)
                dve.sem_inc(parts_made, 1)

            def maxima(i, lo, hi):
                for m in range(lo, hi):
                    j, h, half = PEAKS[m]
                    dve.wait_ge(peak_scored, NP * i + m + 1)
                    dve.tensor_reduce(peaks[:, j * H + h, half:half + 1], p_k[m % 2][:, :], X, ALU.max).then_inc(peak_read, 1)

            def shifts(i, u, high):
                n = [0]

                def step(ins):
                    n[0] += 1
                    ins.then_inc(chain5, 1)
                    dve.wait_ge(chain5, 8 * i + 4 * high + n[0])

                js = slice(high * J // 2, (high + 1) * J // 2)
                at = slice(high * J * H // 2, (high + 1) * J * H // 2)
                dve.wait_ge(peak_read, NP * i + NP // 2 * (high + 1))

                def part(k):
                    return parts[:, u, js, 0, :, SHIFT, k]

                sh = shift[:, at].rearrange("p (j h) -> p j h", h=H)
                step(dve.tensor_reduce(shift[:, at], peaks[:, at, :], X, ALU.max, negate=True))
                step(dve.tensor_copy(part(0), sh))
                step(dve.tensor_tensor(sh, sh, part(0), ALU.subtract))
                step(dve.tensor_copy(part(1), sh))
                dve.tensor_tensor(part(2), sh, part(1), ALU.subtract).then_inc(shift_made, 1)

            K = 2 + 6 + 10
            n = [0]

            def finish_step(i, ins):
                n[0] += 1
                ins.then_inc(chain3, 1)
                dve.wait_ge(chain3, K * i + n[0])

            def attended(i):
                n[0] = 0
                dve.wait_ge(o_turned, i + 1)
                turned = p_m[:, :, :].rearrange("p a (j h c) -> p (a j h) c", h=H, c=32)
                finish_step(i, dve.reciprocal(share[:, :], turned[:, :, D]))
                dve.tensor_tensor(att[:, :, :].rearrange("p j (h d) -> p (j h) d", d=D), turned[:, :, 0:D],
                                  mid(share[:, :], D), ALU.mult).then_inc(att_made, 1)

            def residual(i, u, meanwhile):
                dve.wait_ge(x_kept[u], 8 * (i - u) + 16)
                dve.wait_ge(projected, i + 1)
                finish_step(i, dve.tensor_tensor(x4[:, :, :].rearrange("p j c -> p (j c)"), p_m[:, 0, 0:J * C],
                                                 x_keep[:, u, :, :].rearrange("p j c -> p (j c)"), ALU.add))

                def power(ins):
                    ins.then_inc(var2_made, 1)
                    meanwhile()
                    dve.wait_ge(rstd2_made, i + 1)

                n[0] += normalise_tokens(dve, power, x4[:, :, :], xl4[:, :, :], C, 1e-5, ln2, chain3, K * i + n[0])
                dve.sem_inc(xl4_made, 1)

            def route(i, meanwhile):
                def step(ins):
                    finish_step(i, ins)

                dve.wait_ge(routed, i + 1)
                logits = p_m[:, 0, 0:J * ER].rearrange("p (j e) -> p j e", e=ER)
                step(dve.tensor_reduce(col[:, :], logits, X, ALU.max))
                dve.tensor_tensor(expo[:, :, :], logits, mid(col[:, :], ER), ALU.subtract).then_inc(logits_read, 1)
                meanwhile()
                dve.wait_ge(expo_made, i + 1)
                step(dve.tensor_reduce(col[:, :], expo[:, :, :], X, ALU.add))
                step(dve.reciprocal(col[:, :], col[:, :]))
                step(dve.tensor_tensor(prob[:, :, :], expo[:, :, :], mid(col[:, :], ER), ALU.mult))
                mine = prob[:, :, :].rearrange("p j (e o) -> p j e o", o=1).broadcast_to([P, J, ER, ER])
                other = prob[:, :, :].rearrange("p j (o e) -> p j o e", o=1).broadcast_to([P, J, ER, ER])
                before = earlier[:, :, :].rearrange("p (o e) f -> p o e f", o=1).broadcast_to([P, J, ER, ER])
                step(dve.tensor_tensor(equal[:, :, :, :], other, mine, ALU.is_equal))
                step(dve.tensor_tensor(equal[:, :, :, :], equal[:, :, :, :], before, ALU.mult))
                step(dve.tensor_tensor(above[:, :, :, :], other, mine, ALU.is_gt))
                step(dve.tensor_tensor(above[:, :, :, :], above[:, :, :, :], equal[:, :, :, :], ALU.add))
                step(dve.tensor_reduce(rank[:, :, :], above[:, :, :, :], X, ALU.add))
                step(dve.scalar_tensor_tensor(out=mix[:, :, :], in0=rank[:, :, :], scalar=2.0, in1=prob[:, :, :],
                                              op0=ALU.is_lt, op1=ALU.mult))
                dve.tensor_reduce(col[:, :], mix[:, :, :], X, ALU.add).then_inc(chain4, 1)
                dve.wait_ge(chain4, 6 * i + 4)
                dve.reciprocal(col[:, :], col[:, :]).then_inc(chain4, 1)
                dve.wait_ge(chain4, 6 * i + 5)
                dve.tensor_tensor(mix[:, :, :], mix[:, :, :], mid(col[:, :], ER), ALU.mult).then_inc(chain4, 1)
                dve.wait_ge(chain4, 6 * i + 6)
                wait(dve, stored, 16 * i)
                assert n[0] == K, n[0]

            def combine(i, halves):
                for half in halves:
                    js = slice(half * J // 2, (half + 1) * J // 2)
                    dve.wait_ge(experts_made, 2 * i + half + 1)
                    dve.tensor_tensor(scaled[:, :, :, :].rearrange("p j e c -> p (j e) c"),
                                      p_m[:, :, :].rearrange("p a (x c) -> p (a x) c", c=C),
                                      mid(mix[:, js, :].rearrange("p j e -> p (j e)"), C), ALU.mult).then_inc(experts_read, 1)
                    dve.wait_ge(experts_read, 2 * i + half + 1)
                    dve.tensor_reduce(mixed[:, :, :], scaled[:, :, :, :].rearrange("p j e c -> p j c e"), X,
                                      ALU.add).then_inc(chain4, 1)
                    dve.wait_ge(chain4, 6 * i + 7 + 2 * half)
                    dve.tensor_tensor(result[:, js, :], mixed[:, :, :], x4[:, js, :], ALU.add).then_inc(result_made, 1)
                    if half == 0:
                        dve.wait_ge(result_made, 2 * i + 1)
                        dve.sem_inc(chain4, 1)

            def nothing():
                pass

            normalise(0, nothing)
            split(0, 0)
            maxima(0, 0, NP // 2)
            shifts(0, 0, 0)
            maxima(0, NP // 2, AHEAD)

            def body(i, u, first, last):
                if last:
                    maxima(i, AHEAD, AHEAD + 8)
                else:
                    normalise(i + 1, lambda: maxima(i, AHEAD, AHEAD + 3))
                    maxima(i, AHEAD + 3, AHEAD + 8)
                    split(i + 1, 1 - u)
                if not first:
                    attended(i - 1)
                maxima(i, AHEAD + 8, NP)
                shifts(i, u, 1)

                def ahead(lo, hi):
                    if not last:
                        maxima(i + 1, lo, hi)

                ahead(0, 6)
                if not first:
                    residual(i - 1, 1 - u, lambda: ahead(6, 9))
                    ahead(9, 14)
                    route(i - 1, lambda: ahead(14, 15))
                    combine(i - 1, (0,))
                    ahead(15, 16)
                    combine(i - 1, (1,))
                    ahead(16, NP // 2)
                else:
                    ahead(6, NP // 2)
                if not last:
                    shifts(i + 1, 1 - u, 0)
                ahead(NP // 2, AHEAD)

            over_images(body, dve)
            attended(B - 1)
            residual(B - 1, (B - 1) % 2, nothing)
            route(B - 1, nothing)
            combine(B - 1, (0, 1))


def kernel(**inputs):
    import numpy as np
    import concourse.bacc as bacc
    from concourse.bass_utils import run_bass_kernel_spmd as run

    def lay(a):
        return np.ascontiguousarray(a)

    i = {k: np.asarray(v) for k, v in inputs.items()}
    arrays = {
        "x": lay(i["x"].reshape(B, NI, R * C).transpose(2, 1, 0)),
        "L0_conv_W1": lay(i["L0_conv_W1"].reshape(NI, R * C, C).transpose(1, 0, 2)),
        "L0_conv_W2": lay(i["L0_conv_W2"].reshape(NI, R * C, C).transpose(1, 0, 2)),
        "L0_conv_b1": lay(i["L0_conv_b1"].reshape(NI, R * C).T),
        "L0_conv_b2": lay(i["L0_conv_b2"].reshape(NI, R * C).T),
        "L1_conv_W_exp": lay(i["L1_conv_W_exp"].T),
        "L1_conv_W_con": lay(i["L1_conv_W_con"].T),
        "L1_conv_b_exp": lay(i["L1_conv_b_exp"].reshape(2 * C, 1)),
        "L1_conv_b_con": lay(i["L1_conv_b_con"].reshape(C, 1)),
    }
    arrays.update({
        "L2_attn_Wq": i["L2_attn_Wq"], "L2_attn_Wk": i["L2_attn_Wk"], "L2_attn_Wv": i["L2_attn_Wv"],
        "L2_attn_Wu": i["L2_attn_Wu"], "L2_attn_Wf": i["L2_attn_Wf"],
        "pos_w": i["L2_attn_pos_w"].reshape(1, -1),
    })
    for name in ("L2_attn_bq", "L2_attn_bk", "L2_attn_bv", "L2_attn_bu", "L2_attn_bf", "L2_attn_ln_gamma",
                 "L2_attn_ln_beta"):
        arrays[name] = i[name].reshape(1, -1)
    arrays.update({
        "L2_ffn_gate_w": lay(i["L2_ffn_gate_w"].T), "L2_ffn_gate_b": i["L2_ffn_gate_b"].reshape(1, -1),
        "L2_ffn_weight1": i["L2_ffn_weight1"], "L2_ffn_weight2": i["L2_ffn_weight2"],
    })
    arrays.update({
        "L3_attn_W_qkv": lay(i["L3_attn_W_qkv"].reshape(C, H, D, 3).transpose(0, 3, 1, 2).reshape(C, 3 * C)),
        "L3_attn_b_qkv": lay(i["L3_attn_b_qkv"].reshape(H, D, 3).transpose(2, 0, 1).reshape(1, 3 * C)),
        "L3_attn_W_proj": i["L3_attn_W_proj"], "L3_attn_b_proj": i["L3_attn_b_proj"].reshape(1, -1),
        "L3_ffn_router_w": i["L3_ffn_router_w"], "L3_ffn_router_b": i["L3_ffn_router_b"].reshape(1, -1),
        "L3_ffn_expert_w": i["L3_ffn_expert_w"], "L3_ffn_expert_b": i["L3_ffn_expert_b"].reshape(1, -1),
    })
    nc = bacc.Bacc("TRN2", target_bir_lowering=False, num_devices=1)
    t = {k: nc.dram_tensor("in_" + k, a.shape, F32, kind="ExternalInput").ap() for k, a in arrays.items()}
    t["rows1"] = nc.dram_tensor("t1", (B * NI, R * C), F32, kind="Internal").ap()
    t["t1"] = t["rows1"].rearrange("n (r c) -> (n r) c", c=C)
    t["pos_ext"] = nc.dram_tensor("pos_ext", (1, t["pos_w"].shape[1] + P), F32, kind="Internal").ap()
    t["t2"] = nc.dram_tensor("t2", (B * S, C), F32, kind="Internal").ap()
    t["t3"] = nc.dram_tensor("t3", (B * S, C), F32, kind="Internal").ap()
    t["t4"] = nc.dram_tensor("out", (B * S, C), F32, kind="ExternalOutput").ap()
    positionwise_layers(nc, t)
    silu_attention_layer(nc, t)
    expert_choice_layer(nc, t)
    softmax_attention_and_router_layer(nc, t)
    r = run(nc, [{"in_" + k: a for k, a in arrays.items()}], core_ids=[0])
    return r.results[0]["out"].reshape(B, ROWS, ROWS, C)
```
